# Optimizing a Trainium2 kernel written in Bass

```python
import numpy as np
import jax
import jax.numpy as jnp

def _softmax(x, axis=-1):
    return jax.nn.softmax(x, axis=axis)

def _gelu(x):
    return jax.nn.gelu(x, approximate=True)

def _silu(x):
    return jax.nn.silu(x)

def _sigmoid(x):
    return jax.nn.sigmoid(x)

def _layernorm(x, axis=-1, eps=1e-05):
    m = jnp.mean(x, axis=axis, keepdims=True)
    v = jnp.var(x, axis=axis, keepdims=True)
    return (x - m) / jnp.sqrt(v + eps)

def _scatter_add(tgt, idx, src, axis=0):
    return tgt.at[idx].add(src)

def _segment_sum(src, seg, n):
    return jax.ops.segment_sum(src, seg, n)
kernel_name = 'mk_vit_tower_cls_d1_tok_img768_r4_99fd60'

def setup_inputs(seed: int=0):
    np.random.seed(seed)
    _w = jnp.asarray

    def _rec_inputs():
        import jax
        import jax.numpy as jnp
        _rk = jax.random.key(seed)
        x = -0.000222058 + 0.999998 * jax.random.normal(jax.random.fold_in(_rk, 1), (16, 3, 128, 128), jnp.float32)
        cls_tok = 0.02 * jax.random.normal(jax.random.fold_in(_rk, 5), (1, 1, 192), jnp.float32)
        return (x, cls_tok)
    x, cls_tok = _rec_inputs()

    def _L0_tok_setup():
        import jax, jax.numpy as jnp
        import numpy as np
        DIM = 192
        HEADS = 12
        HEAD_DIM = DIM // HEADS
        MLP_HIDDEN = DIM * 4
        PATCH = 16
        IMG = 128
        CH = 3
        BATCH = 32
        WINDOW = 128
        MAX_FREQ = 10.0
        LN_EPS = 1e-05
        TOKEN_SELF_ATTN_VALUE = -50000.0

        def layernorm(x, g, b):
            mu = jnp.mean(x, -1, keepdims=True)
            var = jnp.var(x, -1, keepdims=True)
            return (x - mu) * jax.lax.rsqrt(var + LN_EPS) * g + b

        def swiglu(x, w1, w2, w3):
            return jax.nn.silu(x @ w1) * (x @ w3) @ w2

        def axial_rotary_sin(n, dim):
            scales = jnp.linspace(1.0, MAX_FREQ / 2, dim // 4)
            seq = jnp.linspace(-1.0, 1.0, n)[:, None] * scales[None, :] * jnp.pi
            x_sinu = jnp.broadcast_to(seq[:, None, :], (n, n, dim // 4))
            y_sinu = jnp.broadcast_to(seq[None, :, :], (n, n, dim // 4))
            sin = jnp.concatenate([jnp.sin(x_sinu), jnp.sin(y_sinu)], -1).reshape(n * n, dim // 2)
            return jnp.repeat(sin, 2, axis=-1)[None]

        def rotate_half(t):
            t1, t2 = jnp.split(t, 2, axis=-1)
            return jnp.concatenate([-t2, t1], axis=-1)

        def local_attention(q, k, v):
            b, n0, d = q.shape
            inv_freq = 1.0 / 10000.0 ** (jnp.arange(0, d, 2, dtype=jnp.float32) / d)
            freqs = jnp.arange(n0, dtype=jnp.float32)[:, None] * inv_freq[None, :]
            freqs = jnp.concatenate([freqs, freqs], -1)
            cos_f, sin_f = (jnp.cos(freqs), jnp.sin(freqs))
            q = q * cos_f + rotate_half(q) * sin_f
            k = k * cos_f + rotate_half(k) * sin_f
            pad = -n0 % WINDOW
            if pad:
                q, k, v = (jnp.pad(t, ((0, 0), (0, pad), (0, 0))) for t in (q, k, v))
            n = n0 + pad
            w = n // WINDOW
            k = k / jnp.maximum(jnp.linalg.norm(k, axis=-1, keepdims=True), 1e-12)
            bq = q.reshape(b, w, WINDOW, d)
            bk = k.reshape(b, w, WINDOW, d)
            bv = v.reshape(b, w, WINDOW, d)

            def look_around(t, pad_value):
                pad_cfg = [(0, 0), (1, 0)] + [(0, 0)] * (t.ndim - 2)
                padded = jnp.pad(t, pad_cfg, constant_values=pad_value)
                return jnp.concatenate([padded[:, :w], padded[:, 1:w + 1]], axis=2)
            bk = look_around(bk, -1.0)
            bv = look_around(bv, -1.0)
            seq = jnp.arange(n).reshape(1, w, WINDOW)
            i_idx = seq[..., :, None]
            j_idx = look_around(seq, -1)[..., None, :]
            sim = jnp.einsum('bwie,bwje->bwij', bq, bk) * d ** (-0.5)
            neg = -jnp.finfo(sim.dtype).max
            sim = jnp.where(i_idx == j_idx, TOKEN_SELF_ATTN_VALUE, sim)
            sim = jnp.where(i_idx < j_idx, neg, sim)
            sim = jnp.where(j_idx == -1, neg, sim)
            attn = jax.nn.softmax(sim, -1)
            out = jnp.einsum('bwij,bwje->bwie', attn, bv).reshape(b, n, d)
            return out[:, :n0]

        def mqa(x, wqkv, bqkv, wo, bo):
            b, n, d = x.shape
            qkv = x @ wqkv + bqkv
            q = qkv[..., :DIM].reshape(b, n, HEADS, HEAD_DIM)
            kk = qkv[..., DIM:DIM + HEAD_DIM]
            vv = qkv[..., DIM + HEAD_DIM:]
            scores = jnp.einsum('bihd,bjd->bhij', q, kk) * (1.0 / np.sqrt(HEAD_DIM))
            causal = jnp.arange(n)[:, None] >= jnp.arange(n)[None, :]
            scores = jnp.where(causal, scores, jnp.finfo(scores.dtype).min)
            attn = jax.nn.softmax(scores, -1)
            out = jnp.einsum('bhij,bjd->bihd', attn, vv).reshape(b, n, d)
            return out @ wo + bo

        def _forward(x, patch_w, patch_b, ln_g, ln_b, w1, w2, w3, wqkv, bqkv, wo, bo):
            b, c, h, wd = x.shape
            hh, ww = (h // PATCH, wd // PATCH)
            patches = x.reshape(b, c, hh, PATCH, ww, PATCH).transpose(0, 2, 4, 3, 5, 1)
            patches = patches.reshape(b, hh * ww, PATCH * PATCH * c)
            tok = patches @ patch_w + patch_b
            skip1 = tok
            n_side = int(np.sqrt(hh * ww))
            sin = axial_rotary_sin(n_side, DIM)
            _ = layernorm(tok, ln_g, ln_b)
            y = local_attention(sin, sin, sin) + skip1
            skip2 = y
            y = layernorm(y, ln_g, ln_b)
            y = swiglu(y, w1, w2, w3) + skip2
            _ = layernorm(y, ln_g, ln_b)
            z = mqa(sin, wqkv, bqkv, wo, bo) + skip1
            skip3 = z
            z = layernorm(z, ln_g, ln_b)
            return swiglu(z, w1, w2, w3) + skip3
        key = jax.random.key(seed)
        ks = jax.random.split(key, 8)
        patch_dim = CH * PATCH * PATCH
        s = lambda fan_in: 1.0 / np.sqrt(fan_in)
        return {'x': jax.random.normal(ks[0], (BATCH, CH, IMG, IMG), jnp.float32), 'patch_w': jax.random.normal(ks[1], (patch_dim, DIM), jnp.float32) * s(patch_dim), 'patch_b': jnp.zeros((DIM,), jnp.float32), 'ln_g': jnp.ones((DIM,), jnp.float32), 'ln_b': jnp.zeros((DIM,), jnp.float32), 'w1': jax.random.normal(ks[2], (DIM, MLP_HIDDEN), jnp.float32) * s(DIM), 'w2': jax.random.normal(ks[3], (MLP_HIDDEN, DIM), jnp.float32) * s(MLP_HIDDEN), 'w3': jax.random.normal(ks[4], (DIM, MLP_HIDDEN), jnp.float32) * s(DIM), 'wqkv': jax.random.normal(ks[5], (DIM, DIM + 2 * HEAD_DIM), jnp.float32) * s(DIM), 'bqkv': jnp.zeros((DIM + 2 * HEAD_DIM,), jnp.float32), 'wo': jax.random.normal(ks[6], (DIM, DIM), jnp.float32) * s(DIM), 'bo': jnp.zeros((DIM,), jnp.float32)}
    _L0_tok_all = _L0_tok_setup()
    _L0_tok_in = {k: v for k, v in _L0_tok_all.items() if k in ('patch_w', 'patch_b', 'ln_g', 'ln_b', 'w1', 'w2', 'w3', 'wqkv', 'bqkv', 'wo', 'bo')}
    del _L0_tok_all

    def _L0_attn_setup():
        import jax, jax.numpy as jnp
        import numpy as np
        B, T, C, NH = (8, 256, 192, 12)
        HD = C // NH
        key = jax.random.key(seed)
        k1, k2, k3, k4, k5 = jax.random.split(key, 5)
        s = 0.02
        return {'x': jax.random.normal(k1, (B, T, C), dtype=jnp.float32), 'w_attn': jax.random.normal(k2, (C, 3 * C), dtype=jnp.float32) * s, 'b_attn': jax.random.normal(k3, (3 * C,), dtype=jnp.float32) * s, 'w_proj': jax.random.normal(k4, (C, C), dtype=jnp.float32) * s, 'b_proj': jax.random.normal(k5, (C,), dtype=jnp.float32) * s}
    _L0_attn_all = _L0_attn_setup()
    _L0_attn_in = {k: v for k, v in _L0_attn_all.items() if k in ('w_attn', 'b_attn', 'w_proj', 'b_proj')}
    del _L0_attn_all

    def _L0_ffn_setup():
        import jax, jax.numpy as jnp
        import numpy as np
        DIM = 192
        HEADS = 12
        EXPERTS = 8
        HID = 768
        TOP_K = 2
        LN_EPS = 1e-05

        def _layer_norm(x, g, b):
            mu = x.mean(-1, keepdims=True)
            var = ((x - mu) ** 2).mean(-1, keepdims=True)
            return (x - mu) * jax.lax.rsqrt(var + LN_EPS) * g + b

        def _attention(x, qkv_w, qkv_b, proj_w, proj_b):
            B, N, C = x.shape
            hd = C // HEADS
            qkv = (x @ qkv_w + qkv_b).reshape(B, N, 3, HEADS, hd).transpose(2, 0, 3, 1, 4)
            q, k, v = (qkv[0], qkv[1], qkv[2])
            attn = jax.nn.softmax(jnp.einsum('bhnd,bhmd->bhnm', q, k) * hd ** (-0.5), axis=-1)
            o = jnp.einsum('bhnm,bhmd->bhnd', attn, v).transpose(0, 2, 1, 3).reshape(B, N, C)
            return o @ proj_w + proj_b

        def _moe_mlp(xn, gate_w, w1, b1, w2, b2):
            T = xn.shape[0]
            logits = xn @ gate_w
            top_logits, top_idx = jax.lax.top_k(logits, TOP_K)
            top_gates = jax.nn.softmax(top_logits, axis=-1)
            gates = jnp.zeros((T, EXPERTS), xn.dtype).at[jnp.arange(T)[:, None], top_idx].set(top_gates)
            h = jax.nn.gelu(jnp.einsum('td,edh->teh', xn, w1) + b1, approximate=False)
            y = jnp.einsum('teh,ehd->ted', h, w2) + b2
            return jnp.einsum('ted,te->td', y, gates)
        key = jax.random.key(seed)
        ks = jax.random.split(key, 16)
        s = 0.02
        return {'x': jax.random.normal(ks[0], (8, 196, DIM), jnp.float32), 'ln1_g': jnp.ones((DIM,), jnp.float32), 'ln1_b': jnp.zeros((DIM,), jnp.float32), 'qkv_w': jax.random.normal(ks[1], (DIM, 3 * DIM), jnp.float32) * s, 'qkv_b': jnp.zeros((3 * DIM,), jnp.float32), 'proj_w': jax.random.normal(ks[2], (DIM, DIM), jnp.float32) * s, 'proj_b': jnp.zeros((DIM,), jnp.float32), 'ln2_g': jnp.ones((DIM,), jnp.float32), 'ln2_b': jnp.zeros((DIM,), jnp.float32), 'gate_w': jax.random.normal(ks[3], (DIM, EXPERTS), jnp.float32) * s, 'w1': jax.random.normal(ks[4], (EXPERTS, DIM, HID), jnp.float32) * s, 'b1': jnp.zeros((EXPERTS, HID), jnp.float32), 'w2': jax.random.normal(ks[5], (EXPERTS, HID, DIM), jnp.float32) * s, 'b2': jnp.zeros((EXPERTS, DIM), jnp.float32)}
    _L0_ffn_all = _L0_ffn_setup()
    _L0_ffn_in = {k: v for k, v in _L0_ffn_all.items() if k in ('ln1_g', 'ln1_b', 'qkv_w', 'qkv_b', 'proj_w', 'proj_b', 'ln2_g', 'ln2_b', 'gate_w', 'w1', 'b1', 'w2', 'b2')}
    del _L0_ffn_all
    return {'x': x, 'cls_tok': cls_tok, 'L0_tok_patch_w': _L0_tok_in['patch_w'], 'L0_tok_patch_b': _L0_tok_in['patch_b'], 'L0_tok_ln_g': _L0_tok_in['ln_g'], 'L0_tok_ln_b': _L0_tok_in['ln_b'], 'L0_tok_w1': _L0_tok_in['w1'], 'L0_tok_w2': _L0_tok_in['w2'], 'L0_tok_w3': _L0_tok_in['w3'], 'L0_tok_wqkv': _L0_tok_in['wqkv'], 'L0_tok_bqkv': _L0_tok_in['bqkv'], 'L0_tok_wo': _L0_tok_in['wo'], 'L0_tok_bo': _L0_tok_in['bo'], 'L0_attn_w_attn': _L0_attn_in['w_attn'], 'L0_attn_b_attn': _L0_attn_in['b_attn'], 'L0_attn_w_proj': _L0_attn_in['w_proj'], 'L0_attn_b_proj': _L0_attn_in['b_proj'], 'L0_ffn_ln1_g': _L0_ffn_in['ln1_g'], 'L0_ffn_ln1_b': _L0_ffn_in['ln1_b'], 'L0_ffn_qkv_w': _L0_ffn_in['qkv_w'], 'L0_ffn_qkv_b': _L0_ffn_in['qkv_b'], 'L0_ffn_proj_w': _L0_ffn_in['proj_w'], 'L0_ffn_proj_b': _L0_ffn_in['proj_b'], 'L0_ffn_ln2_g': _L0_ffn_in['ln2_g'], 'L0_ffn_ln2_b': _L0_ffn_in['ln2_b'], 'L0_ffn_gate_w': _L0_ffn_in['gate_w'], 'L0_ffn_w1': _L0_ffn_in['w1'], 'L0_ffn_b1': _L0_ffn_in['b1'], 'L0_ffn_w2': _L0_ffn_in['w2'], 'L0_ffn_b2': _L0_ffn_in['b2']}

def reference(x, cls_tok, L0_tok_patch_w, L0_tok_patch_b, L0_tok_ln_g, L0_tok_ln_b, L0_tok_w1, L0_tok_w2, L0_tok_w3, L0_tok_wqkv, L0_tok_bqkv, L0_tok_wo, L0_tok_bo, L0_attn_w_attn, L0_attn_b_attn, L0_attn_w_proj, L0_attn_b_proj, L0_ffn_ln1_g, L0_ffn_ln1_b, L0_ffn_qkv_w, L0_ffn_qkv_b, L0_ffn_proj_w, L0_ffn_proj_b, L0_ffn_ln2_g, L0_ffn_ln2_b, L0_ffn_gate_w, L0_ffn_w1, L0_ffn_b1, L0_ffn_w2, L0_ffn_b2):
    import jax
    import jax.numpy as jnp

    def _L0_tok_ref(x, patch_w, patch_b, ln_g, ln_b, w1, w2, w3, wqkv, bqkv, wo, bo):
        import jax, jax.numpy as jnp
        import numpy as np
        DIM = 192
        HEADS = 12
        HEAD_DIM = DIM // HEADS
        MLP_HIDDEN = DIM * 4
        PATCH = 16
        IMG = 128
        CH = 3
        BATCH = 32
        WINDOW = 128
        MAX_FREQ = 10.0
        LN_EPS = 1e-05
        TOKEN_SELF_ATTN_VALUE = -50000.0

        def layernorm(x, g, b):
            mu = jnp.mean(x, -1, keepdims=True)
            var = jnp.var(x, -1, keepdims=True)
            return (x - mu) * jax.lax.rsqrt(var + LN_EPS) * g + b

        def swiglu(x, w1, w2, w3):
            return jax.nn.silu(x @ w1) * (x @ w3) @ w2

        def axial_rotary_sin(n, dim):
            scales = jnp.linspace(1.0, MAX_FREQ / 2, dim // 4)
            seq = jnp.linspace(-1.0, 1.0, n)[:, None] * scales[None, :] * jnp.pi
            x_sinu = jnp.broadcast_to(seq[:, None, :], (n, n, dim // 4))
            y_sinu = jnp.broadcast_to(seq[None, :, :], (n, n, dim // 4))
            sin = jnp.concatenate([jnp.sin(x_sinu), jnp.sin(y_sinu)], -1).reshape(n * n, dim // 2)
            return jnp.repeat(sin, 2, axis=-1)[None]

        def rotate_half(t):
            t1, t2 = jnp.split(t, 2, axis=-1)
            return jnp.concatenate([-t2, t1], axis=-1)

        def local_attention(q, k, v):
            b, n0, d = q.shape
            inv_freq = 1.0 / 10000.0 ** (jnp.arange(0, d, 2, dtype=jnp.float32) / d)
            freqs = jnp.arange(n0, dtype=jnp.float32)[:, None] * inv_freq[None, :]
            freqs = jnp.concatenate([freqs, freqs], -1)
            cos_f, sin_f = (jnp.cos(freqs), jnp.sin(freqs))
            q = q * cos_f + rotate_half(q) * sin_f
            k = k * cos_f + rotate_half(k) * sin_f
            pad = -n0 % WINDOW
            if pad:
                q, k, v = (jnp.pad(t, ((0, 0), (0, pad), (0, 0))) for t in (q, k, v))
            n = n0 + pad
            w = n // WINDOW
            k = k / jnp.maximum(jnp.linalg.norm(k, axis=-1, keepdims=True), 1e-12)
            bq = q.reshape(b, w, WINDOW, d)
            bk = k.reshape(b, w, WINDOW, d)
            bv = v.reshape(b, w, WINDOW, d)

            def look_around(t, pad_value):
                pad_cfg = [(0, 0), (1, 0)] + [(0, 0)] * (t.ndim - 2)
                padded = jnp.pad(t, pad_cfg, constant_values=pad_value)
                return jnp.concatenate([padded[:, :w], padded[:, 1:w + 1]], axis=2)
            bk = look_around(bk, -1.0)
            bv = look_around(bv, -1.0)
            seq = jnp.arange(n).reshape(1, w, WINDOW)
            i_idx = seq[..., :, None]
            j_idx = look_around(seq, -1)[..., None, :]
            sim = jnp.einsum('bwie,bwje->bwij', bq, bk) * d ** (-0.5)
            neg = -jnp.finfo(sim.dtype).max
            sim = jnp.where(i_idx == j_idx, TOKEN_SELF_ATTN_VALUE, sim)
            sim = jnp.where(i_idx < j_idx, neg, sim)
            sim = jnp.where(j_idx == -1, neg, sim)
            attn = jax.nn.softmax(sim, -1)
            out = jnp.einsum('bwij,bwje->bwie', attn, bv).reshape(b, n, d)
            return out[:, :n0]

        def mqa(x, wqkv, bqkv, wo, bo):
            b, n, d = x.shape
            qkv = x @ wqkv + bqkv
            q = qkv[..., :DIM].reshape(b, n, HEADS, HEAD_DIM)
            kk = qkv[..., DIM:DIM + HEAD_DIM]
            vv = qkv[..., DIM + HEAD_DIM:]
            scores = jnp.einsum('bihd,bjd->bhij', q, kk) * (1.0 / np.sqrt(HEAD_DIM))
            causal = jnp.arange(n)[:, None] >= jnp.arange(n)[None, :]
            scores = jnp.where(causal, scores, jnp.finfo(scores.dtype).min)
            attn = jax.nn.softmax(scores, -1)
            out = jnp.einsum('bhij,bjd->bihd', attn, vv).reshape(b, n, d)
            return out @ wo + bo

        def _forward(x, patch_w, patch_b, ln_g, ln_b, w1, w2, w3, wqkv, bqkv, wo, bo):
            b, c, h, wd = x.shape
            hh, ww = (h // PATCH, wd // PATCH)
            patches = x.reshape(b, c, hh, PATCH, ww, PATCH).transpose(0, 2, 4, 3, 5, 1)
            patches = patches.reshape(b, hh * ww, PATCH * PATCH * c)
            tok = patches @ patch_w + patch_b
            skip1 = tok
            n_side = int(np.sqrt(hh * ww))
            sin = axial_rotary_sin(n_side, DIM)
            _ = layernorm(tok, ln_g, ln_b)
            y = local_attention(sin, sin, sin) + skip1
            skip2 = y
            y = layernorm(y, ln_g, ln_b)
            y = swiglu(y, w1, w2, w3) + skip2
            _ = layernorm(y, ln_g, ln_b)
            z = mqa(sin, wqkv, bqkv, wo, bo) + skip1
            skip3 = z
            z = layernorm(z, ln_g, ln_b)
            return swiglu(z, w1, w2, w3) + skip3
        return _forward(x, patch_w, patch_b, ln_g, ln_b, w1, w2, w3, wqkv, bqkv, wo, bo)

    def _L0_attn_ref(x, w_attn, b_attn, w_proj, b_proj):
        import jax, jax.numpy as jnp
        import numpy as np
        B, T, C, NH = (8, 256, 192, 12)
        HD = C // NH
        Bv, Tv, Cv = x.shape
        qkv = jnp.einsum('btc,cd->btd', x, w_attn) + b_attn
        q, k, v = jnp.split(qkv, 3, axis=-1)
        q = q.reshape(Bv, Tv, NH, HD).transpose(0, 2, 1, 3)
        k = k.reshape(Bv, Tv, NH, HD).transpose(0, 2, 1, 3)
        v = v.reshape(Bv, Tv, NH, HD).transpose(0, 2, 1, 3)
        scale = 1.0 / np.sqrt(HD).astype(np.float32)
        att = jnp.einsum('bhqd,bhkd->bhqk', q, k) * scale
        causal = jnp.tril(jnp.ones((Tv, Tv), dtype=bool))
        att = jnp.where(causal, att, -jnp.inf)
        att = jax.nn.softmax(att, axis=-1)
        y = jnp.einsum('bhqk,bhkd->bhqd', att, v)
        y = y.transpose(0, 2, 1, 3).reshape(Bv, Tv, Cv)
        return jnp.einsum('btc,cd->btd', y, w_proj) + b_proj

    def _L0_ffn_ref(x, ln1_g, ln1_b, qkv_w, qkv_b, proj_w, proj_b, ln2_g, ln2_b, gate_w, w1, b1, w2, b2):
        import jax, jax.numpy as jnp
        import numpy as np
        DIM = 192
        HEADS = 12
        EXPERTS = 8
        HID = 768
        TOP_K = 2
        LN_EPS = 1e-05

        def _layer_norm(x, g, b):
            mu = x.mean(-1, keepdims=True)
            var = ((x - mu) ** 2).mean(-1, keepdims=True)
            return (x - mu) * jax.lax.rsqrt(var + LN_EPS) * g + b

        def _attention(x, qkv_w, qkv_b, proj_w, proj_b):
            B, N, C = x.shape
            hd = C // HEADS
            qkv = (x @ qkv_w + qkv_b).reshape(B, N, 3, HEADS, hd).transpose(2, 0, 3, 1, 4)
            q, k, v = (qkv[0], qkv[1], qkv[2])
            attn = jax.nn.softmax(jnp.einsum('bhnd,bhmd->bhnm', q, k) * hd ** (-0.5), axis=-1)
            o = jnp.einsum('bhnm,bhmd->bhnd', attn, v).transpose(0, 2, 1, 3).reshape(B, N, C)
            return o @ proj_w + proj_b

        def _moe_mlp(xn, gate_w, w1, b1, w2, b2):
            T = xn.shape[0]
            logits = xn @ gate_w
            top_logits, top_idx = jax.lax.top_k(logits, TOP_K)
            top_gates = jax.nn.softmax(top_logits, axis=-1)
            gates = jnp.zeros((T, EXPERTS), xn.dtype).at[jnp.arange(T)[:, None], top_idx].set(top_gates)
            h = jax.nn.gelu(jnp.einsum('td,edh->teh', xn, w1) + b1, approximate=False)
            y = jnp.einsum('teh,ehd->ted', h, w2) + b2
            return jnp.einsum('ted,te->td', y, gates)
        B, N, C = x.shape
        x = x + _attention(_layer_norm(x, ln1_g, ln1_b), qkv_w, qkv_b, proj_w, proj_b)
        xn = _layer_norm(x, ln2_g, ln2_b).reshape(B * N, C)
        moe_out = _moe_mlp(xn, gate_w, w1, b1, w2, b2).reshape(B, N, C)
        return x + moe_out
    h = _L0_tok_ref(x, L0_tok_patch_w, L0_tok_patch_b, L0_tok_ln_g, L0_tok_ln_b, L0_tok_w1, L0_tok_w2, L0_tok_w3, L0_tok_wqkv, L0_tok_bqkv, L0_tok_wo, L0_tok_bo)
    h = jnp.concatenate([jnp.broadcast_to(cls_tok, (h.shape[0], 1, h.shape[2])), h], axis=1)
    h = h + _L0_attn_ref(_layernorm(h, axis=-1), L0_attn_w_attn, L0_attn_b_attn, L0_attn_w_proj, L0_attn_b_proj)
    h = h + _L0_ffn_ref(_layernorm(h, axis=-1), L0_ffn_ln1_g, L0_ffn_ln1_b, L0_ffn_qkv_w, L0_ffn_qkv_b, L0_ffn_proj_w, L0_ffn_proj_b, L0_ffn_ln2_g, L0_ffn_ln2_b, L0_ffn_gate_w, L0_ffn_w1, L0_ffn_b1, L0_ffn_w2, L0_ffn_b2)
    return h

_drawn_inputs = setup_inputs


def setup_inputs(seed=0):
    import zlib

    import numpy as np

    out = dict(_drawn_inputs(seed))
    spreads = {'L0_tok_patch_b': (0.0, 0.1),
     'L0_tok_ln_g': (1.0, 0.2),
     'L0_tok_ln_b': (0.0, 0.1),
     'L0_tok_bqkv': (0.0, 0.1),
     'L0_tok_bo': (0.0, 0.1),
     'L0_ffn_ln1_g': (1.0, 0.6),
     'L0_ffn_ln1_b': (0.0, 0.8),
     'L0_ffn_qkv_b': (0.0, 0.494),
     'L0_ffn_proj_b': (0.0, 0.1),
     'L0_ffn_ln2_g': (1.0, 0.6),
     'L0_ffn_ln2_b': (0.0, 0.699),
     'L0_ffn_b1': (0.0, 0.8),
     'L0_ffn_b2': (0.0, 0.344)}
    factors = {'L0_attn_b_attn': 7.89, 'L0_ffn_qkv_w': 5.623, 'L0_ffn_proj_w': 3.143}
    for name, (base, spread) in spreads.items():
        noise = np.random.default_rng([zlib.crc32(name.encode()), seed]).standard_normal(out[name].shape)
        drawn = base * np.exp(spread * noise) if base else spread * noise
        out[name] = jnp.asarray(drawn.astype(out[name].dtype))
    for name, factor in factors.items():
        out[name] = (out[name] * factor).astype(out[name].dtype)
    return out
```

```python
from contextlib import ExitStack

import numpy as np
import concourse.bass as bass
from concourse import mybir

F32 = mybir.dt.float32
BF16 = mybir.dt.bfloat16
U32 = mybir.dt.uint32
ALU = mybir.AluOpType
ACT = mybir.ActivationFunctionType
AX_X = mybir.AxisListType.X

B = 16
NP = 64
S = NP + 1
C = 192
HC = C // 2
HEADS = 12
HD = C // HEADS
HH = HEADS // 2
PAIRS = HEADS // 2
VW = HD + 1
T = B * NP // 128
CLS = T
HID = 4 * C
KP = HID // 128
E = 8
LN_EPS = 1e-5
SCALE = 0.25
BANK = 512
LN_TOK, LN_ATT, LN_OUTER, LN_ONE, LN_TWO = range(5)


def rows_of(t):
    return B if isinstance(t, int) and t == CLS else 128


def bcast(ap, at, n):
    a = ap.unsqueeze(at)
    shape = list(a.shape)
    shape[at] = n
    return a.to_broadcast(shape)


def in_pairs(eng, step, n=T):
    step(0, 0)
    with eng.Fori(0, (n - 2) // 2) as i:
        step(2 * i + 1, 1)
        step(2 * i + 2, 0)
    step(n - 1, (n - 1) % 2)


def build(nc, d, dbg=None):
    with ExitStack() as ctx:
        def sb(name, shape, dt=F32):
            return ctx.enter_context(nc.sbuf_tensor(name, shape, dt))

        def sem(name):
            return ctx.enter_context(nc.semaphore(name))

        bank = [ctx.enter_context(nc.psum_tensor(f"bank{i}", [128, BANK], F32)) for i in range(8)]

        ident = sb("ident", [128, 128])
        identb = sb("identb", [128, 128], BF16)
        maskb = sb("maskb", [128, HH, S], BF16)
        ones = sb("ones", [1, 128])
        head_mask = sb("head_mask", [HC, 2, HEADS])
        ln_cols = sb("ln_cols", [HC, 3, 2, 2])
        sinT = sb("sinT", [HC + 1, 2, 2, NP])
        patch_b = sb("patch_b", [1, C])
        wqkv_m = sb("wqkv_m", [HC + 1, 2, C + 2 * HD])
        wo_m = sb("wo_m", [HC + 1, 2, C])
        w_patch = sb("w_patch", [128, KP, C])
        w2t = sb("w2t", [128, KP, C])
        wqkv = [sb(f"wqkv{L}", [HC + 1, 2, 3 * C]) for L in range(2)]
        wproj = [sb(f"wproj{L}", [HC + 1, 2, C]) for L in range(2)]
        w_gate = sb("w_gate", [HC, 2, E])
        b2 = sb("b2", [E, C])
        iota8 = sb("iota8", [128, E])

        H = sb("H", [128, T + 1, C])
        U = sb("U", [128, T + 1, C])
        stat = sb("stat", [128, 2, 6])
        mean = sb("mean", [128, 5, T + 1, 1])
        mvs = sb("mvs", [128, 2, 2])
        veps = sb("veps", [128, 2, 1])
        rstd = sb("rstd", [128, 5, T + 1, 1])
        mhalf = sb("mhalf", [128, 1])
        MD = sb("MD", [128, C])
        XN = sb("XN", [128, 2, C])
        XT = sb("XT", [HC + 1, 2, 2, 128])
        qT = sb("qT", [HC, 2, T * 128 + B])
        kT = sb("kT", [HC, 2, B, S])
        KB = sb("KB", [HC, 2, 2, HH, 2 * S])
        arena = sb("arena", [128, 2 * (T * 128 + B) + 4 * HID + 2 * KP * C + 2 * KP * 128])

        def carve(specs):
            at, views = 0, []
            for rows, names, sizes in specs:
                n = int(np.prod(sizes))
                views.append(arena[0:rows, at:at + n].rearrange(
                    f"p ({' '.join(names)}) -> p {' '.join(names)}", **dict(zip(names, sizes))))
                at += n
            return views

        w13, px, silu, gT = carve((
            (HC, "ab", (2, 2 * HID)), (128, "abc", (2, KP, 128)), (128, "abc", (2, KP, 128)), (128, "abc", (2, KP, 128))))
        XTA, w1s, w2s, hT = carve((
            (HC + 1, "ab", (2, T * 128 + B)), (HC + 1, "abc", (2, 2, HID)), (128, "abc", (2, KP, C)), (128, "abc", (2, KP, 128))))
        VB = sb("VB", [128, B, PAIRS, 2, VW])
        VC = sb("VC", [B, C])
        VCB = sb("VCB", [HEADS, B, HEADS * VW])
        vcs = sb("vcs", [HEADS, 2, 2, HEADS * VW])
        VN = sb("VN", [S, B, C])
        qs = sb("qs", [HC, 2, 2, 128])
        P = sb("P", [128, 2, HEADS * S])
        PT = sb("PT", [128, 2, PAIRS + 1, 128])
        mx = sb("mx", [128, 2, HEADS])
        rec = sb("rec", [NP, 2, 2 * HEADS])
        ON = sb("ON", [NP, 2, 2, C])
        OT = sb("OT", [HC + 1, 2, 2, 128])
        OTc = sb("OTc", [HC + 1, 2, B])
        QCB = sb("QCB", [HC, 2, B, HEADS])
        Pc = sb("Pc", [HEADS, B, S])
        mxc = sb("mxc", [HEADS, B])
        smc = sb("smc", [HEADS, B])
        PcT = sb("PcT", [S, B, HEADS])
        OCm = sb("OCm", [HC, 2, B, HEADS])
        qm = sb("qm", [HD, HEADS, NP])
        km = sb("km", [HD, NP])
        VM = sb("VM", [128, 2, VW])
        lg = sb("lg", [128, 2, E])
        mx8 = sb("mx8", [128, T + 1, 8])
        ix8 = sb("ix8", [128, T + 1, 8], U32)
        ixf = sb("ixf", [128, T + 1, 2])
        e2 = sb("e2", [128, T + 1, 1])
        g12 = sb("g12", [128, T + 1, 2])
        hot = sb("hot", [128, T + 1, E])
        gate = sb("gate", [128, T + 1, E])
        gateT = sb("gateT", [E, 2, 128])

        s_ld_const = sem("s_ld_const")
        s_ld_mixer = sem("s_ld_mixer")
        s_ld_up = sem("s_ld_up")
        s_ld_down = sem("s_ld_down")
        s_ld_attn = sem("s_ld_attn")
        s_ld_ffn = sem("s_ld_ffn")
        s_ld_px0 = sem("s_ld_px0")
        s_ld_px1 = sem("s_ld_px1")
        s_ld_cls = sem("s_ld_cls")
        s_out_done = sem("s_out_done")
        s_m_q = sem("s_m_q")
        s_m_k = sem("s_m_k")
        s_m_qc = sem("s_m_qc")
        s_m_s = sem("s_m_s")
        s_m_max = sem("s_m_max")
        s_m_sub = sem("s_m_sub")
        s_m_exp = sem("s_m_exp")
        s_m_t = sem("s_m_t")
        s_m_tc = sem("s_m_tc")
        s_m_o = sem("s_m_o")
        s_m_rec = sem("s_m_rec")
        s_m_norm = sem("s_m_norm")
        s_m_ot = sem("s_m_ot")
        s_m_otc = sem("s_m_otc")
        s_m_md = sem("s_m_md")
        s_m_mdc = sem("s_m_mdc")
        s_tok_ready = sem("s_tok_ready")
        s_z_ready = sem("s_z_ready")
        s_stat_ready = sem("s_stat_ready")
        s_mv_ready = sem("s_mv_ready")
        s_mean_ready = sem("s_mean_ready")
        s_veps_ready = sem("s_veps_ready")
        s_rstd_ready = sem("s_rstd_ready")
        s_xn_ready = sem("s_xn_ready")
        s_xt_psum = sem("s_xt_psum")
        s_xt_ready = sem("s_xt_ready")
        s_up1 = sem("s_up1")
        s_up3 = sem("s_up3")
        s_silu_ready = sem("s_silu_ready")
        s_g_ready = sem("s_g_ready")
        s_down_ready = sem("s_down_ready")
        s_res_ready = sem("s_res_ready")
        s_qk_psum = sem("s_qk_psum")
        s_v_psum = sem("s_v_psum")
        s_k_copied = sem("s_k_copied")
        s_q_copied = sem("s_q_copied")
        s_v_copied = sem("s_v_copied")
        s_vn_copied = sem("s_vn_copied")
        s_kb_loaded0 = sem("s_kb_loaded0")
        s_kb_loaded1 = sem("s_kb_loaded1")
        s_vcb_loaded = sem("s_vcb_loaded")
        s_vn_loaded = sem("s_vn_loaded")
        s_q_slot = sem("s_q_slot")
        s_vc_slot = sem("s_vc_slot")
        s_own_waits = sem("s_own_waits")
        s_s_psum = sem("s_s_psum")
        s_max_ready = sem("s_max_ready")
        s_sub_ready = sem("s_sub_ready")
        s_exp_ready = sem("s_exp_ready")
        s_pt_psum = sem("s_pt_psum")
        s_pta_copied = sem("s_pta_copied")
        s_ptb_copied = sem("s_ptb_copied")
        s_o_psum = sem("s_o_psum")
        s_rec_ready = sem("s_rec_ready")
        s_on_ready = sem("s_on_ready")
        s_ot_psum = sem("s_ot_psum")
        s_ot_copied = sem("s_ot_copied")
        s_proj_psum = sem("s_proj_psum")
        s_presets = sem("s_presets")
        s_kb_zero = sem("s_kb_zero")
        s_cls_otc = sem("s_cls_otc")
        s_c_qcb = sem("s_c_qcb")
        s_c_s = sem("s_c_s")
        s_c_max = sem("s_c_max")
        s_c_sub = sem("s_c_sub")
        s_c_exp = sem("s_c_exp")
        s_c_sum = sem("s_c_sum")
        s_c_rec = sem("s_c_rec")
        s_c_p = sem("s_c_p")
        s_c_pt = sem("s_c_pt")
        s_c_ptc = sem("s_c_ptc")
        s_c_o = sem("s_c_o")
        s_c_om = sem("s_c_om")
        s_lg_psum = sem("s_lg_psum")
        s_lg_copied = sem("s_lg_copied")
        s_mx8_ready = sem("s_mx8_ready")
        s_ix8_ready = sem("s_ix8_ready")
        s_r1 = sem("s_r1")
        s_r2 = sem("s_r2")
        s_r3 = sem("s_r3")
        s_r4 = sem("s_r4")
        s_r5 = sem("s_r5")
        s_r6 = sem("s_r6")
        s_r7 = sem("s_r7")
        s_r8 = sem("s_r8")
        s_gate_ready = sem("s_gate_ready")
        s_gt_psum = sem("s_gt_psum")
        s_gt_copied = sem("s_gt_copied")
        s_b2_psum = sem("s_b2_psum")
        s_b2_added = sem("s_b2_added")
        s_xta_ready = sem("s_xta_ready")
        s_w_loaded0 = sem("s_w_loaded0")
        s_w_loaded1 = sem("s_w_loaded1")
        s_w_used = sem("s_w_used")
        s_h_psum = sem("s_h_psum")
        s_h_ready = sem("s_h_ready")
        s_y_psum = sem("s_y_psum")
        s_y_added = sem("s_y_added")
        s_fin_ready = sem("s_fin_ready")

        ld_px = (s_ld_px0, s_ld_px1)
        kb_loaded = (s_kb_loaded0, s_kb_loaded1)
        w_loaded = (s_w_loaded0, s_w_loaded1)

        def ln_at(n, t):
            return (0 if n == LN_TOK else T + (n - 1) * (T + 1)) + t + 1

        def xt_at(n, t):
            base = {LN_TOK: 0, LN_ATT: T, LN_ONE: 2 * T + 1, LN_TWO: 3 * T + 2}[n]
            return base + t + 1

        def slot_of(t):
            return t % 2

        def tile_cols(t):
            return bass.ts(t, 128) if not (isinstance(t, int) and t == CLS) else slice(T * 128, T * 128 + B)

        def own_wait(eng):
            eng.sem_inc(s_own_waits, 1)

        def weights(u, r0, r1):
            return P[r0:r1, u, 0:HEADS * NP].rearrange("p (h j) -> p h j", h=HEADS)

        block = ctx.enter_context(nc.Block())

        N_CONST = 9
        N_MIX = 4

        @block.sync
        def _(sp):
            for dst, src in (
                (sinT, "sinT"), (patch_b, "patch_b"), (ident, "ident"), (identb, "identb"),
                (maskb, "maskb"), (head_mask, "head_mask"), (ln_cols, "ln_cols"), (ones, "ones"),
                (iota8, "iota8"),
            ):
                sp.dma_start(dst[:], d[src]).then_inc(s_ld_const, 16)
            for dst, src in ((wqkv_m, "wqkv_m"), (wo_m, "wo_m"), (VM, "vm0"), (w_patch, "w_patch")):
                sp.dma_start(dst[:], d[src]).then_inc(s_ld_mixer, 16)
            for t in range(2):
                sp.dma_start(px[:, t], d["patches"][t]).then_inc(ld_px[t], 16)
            sp.dma_start(w13[:], d["w13"]).then_inc(s_ld_up, 16)
            sp.dma_start(w2t[:], d["w2t"]).then_inc(s_ld_down, 16)
            sp.dma_start(H[0:B, CLS, :], d["cls"]).then_inc(s_ld_cls, 16)
            for L in range(2):
                sp.dma_start(wqkv[L][:], d[f"wqkv{L}"]).then_inc(s_ld_attn, 16)
                sp.dma_start(wproj[L][:], d[f"wproj{L}"]).then_inc(s_ld_attn, 16)
            sp.dma_start(VB[:], d["vb0"]).then_inc(s_ld_attn, 16)
            sp.dma_start(VCB[:], d["vcb0"]).then_inc(s_ld_attn, 16)
            sp.dma_start(w_gate[:], d["w_gate"]).then_inc(s_ld_ffn, 16)
            sp.dma_start(b2[:], d["b2"]).then_inc(s_ld_ffn, 16)
            with sp.Fori(0, (T - 2) // 2) as i:
                for u in range(2):
                    sp.wait_ge(s_tok_ready, 2 * i + u + 1)
                    sp.dma_start(px[:, u], d["patches"][2 * i + u + 2]).then_inc(ld_px[u], 16)
            for L in range(2):
                sp.wait_ge(s_v_copied, (L + 1) * (T + 1))
                for h in range(HEADS):
                    sp.dma_start(VCB[h:h + 1, :, VW * h:VW * h + HD],
                                 VC[:, HD * h:HD * h + HD]).then_inc(s_vcb_loaded, 16)
                if L == 1:
                    sp.dma_start(VN[NP:S, :, :], VC[:, :]).then_inc(s_vn_loaded, 16)
                sp.wait_ge(s_kb_zero, 1)
                sp.wait_ge(s_k_copied, (L + 1) * (T + 1))

                def spread_keys(t, u):
                    if not (isinstance(t, int) and L * T + t < 2):
                        sp.wait_ge(s_s_psum, L * T + t - 1)
                    for h in range(HH):
                        p0 = HD * h
                        sp.dma_start(KB[p0:p0 + HD, u, :, h, :],
                                     kT[p0:p0 + HD, :, bass.ts(t, 2), :].rearrange("p g j s -> p g (j s)")).then_inc(kb_loaded[u], 16)
                spread_keys(0, 0)
                spread_keys(1, 1)
                with sp.Fori(1, T // 2) as i:
                    for u in range(2):
                        spread_keys(2 * i + u, u)
            sp.wait_ge(s_down_ready, T)
            with sp.Fori(0, E // 2) as i:
                for u in range(2):
                    sp.wait_ge(s_w_used, 2 * i + u + 1)
                    sp.dma_start(w1s[:, u], d["w1"][2 * i + u]).then_inc(w_loaded[u], 16)
                    sp.dma_start(w2s[:, u], d["w2"][2 * i + u]).then_inc(w_loaded[u], 16)
            n_out = 0
            for t in range(T):
                sp.wait_ge(s_fin_ready, t + 1)
                for j in range(2):
                    sp.dma_start(d["out"][2 * t + j, 1:S, :], H[NP * j:NP * j + NP, t, :]).then_inc(s_out_done, 16)
                    n_out += 1
            sp.wait_ge(s_fin_ready, T + 1)
            sp.dma_start(d["out"][:, 0, :], H[0:B, CLS, :]).then_inc(s_out_done, 16)
            n_out += 1
            if dbg:
                for name, ap in (("H", H), ("U", U), ("MD", MD), ("gate", gate), ("rstd", rstd), ("kT", kT),("qT",qT)):
                    if name in dbg:
                        sp.dma_start(d["dbg_" + name], ap[:]).then_inc(s_out_done, 16)
                        n_out += 1
            sp.wait_ge(s_out_done, 16 * n_out)

        @block.tensor
        def _(pe):
            def both_halves(out, lhs, rhs, bias=True, start=True, stop=True):
                k = HC + 1 if bias else HC
                pe.matmul(out, lhs(0)[0:HC], rhs(0)[0:HC], start=start, stop=False)
                return pe.matmul(out, lhs(1)[0:k], rhs(1)[0:k], start=False, stop=stop)

            pe.wait_ge(s_ld_const, 16 * N_CONST)
            pe.wait_ge(s_ld_mixer, 16 * N_MIX)
            for h in range(HEADS):
                mm = both_halves(bank[h // HH][0:HD, NP * (h % HH):NP * (h % HH) + NP],
                                 lambda g: wqkv_m[:, g, HD * h:HD * h + HD], lambda g: sinT[:, g, 0, :])
            mm.then_inc(s_m_q, 1)
            both_halves(bank[2][0:HD, 0:NP], lambda g: wqkv_m[:, g, C:C + HD], lambda g: sinT[:, g, 0, :])
            both_halves(bank[2][:, NP:NP + HD], lambda g: sinT[:, g].rearrange("p a b -> p (a b)"),
                        lambda g: wqkv_m[:, g, C + HD:C + 2 * HD]).then_inc(s_m_k, 1)
            pe.wait_ge(s_m_qc, 4)
            for g in range(2):
                pe.matmul(bank[3 + g][0:NP, 0:HH * NP], identb[0:NP, 0:NP], maskb[0:NP, :, 0:NP],
                          start=True, stop=False)
                for j in range(HH):
                    mm = pe.matmul(bank[3 + g][0:NP, NP * j:NP * j + NP], qm[:, HH * g + j, :], km[:, :],
                                   start=False, stop=(j == HH - 1))
            mm.then_inc(s_m_s, 1)

            def tok(t, u):
                pe.wait_ge(ld_px[u], 8 * (t - u) + 16)
                if not (isinstance(t, int) and t == 0):
                    pe.wait_ge(s_z_ready, t)
                for k in range(KP):
                    mm = pe.matmul(bank[7][:, 0:C], px[:, u, k, :], w_patch[:, k, :],
                                   start=(k == 0), stop=(k == KP - 1))
                mm.then_inc(s_tok_ready, 1)
            tok(0, 0)

            pe.wait_ge(s_m_exp, 1)
            for p in range(PAIRS):
                mm = pe.transpose(bank[5][:, NP * p:NP * p + NP], P[0:NP, 0, 2 * NP * p:2 * NP * (p + 1)], ident[0:NP, 0:NP])
            mm.then_inc(s_m_t, 1)
            pe.wait_ge(s_m_tc, 1)
            for p in range(PAIRS):
                mm = pe.matmul(bank[6][0:NP, 2 * VW * p:2 * VW * p + 2 * VW], PT[:, 0, p, 0:NP], VM[:, :, :],
                               start=True, stop=True)
            mm.then_inc(s_m_o, 1)
            pe.wait_ge(s_m_norm, 1)
            for g in range(2):
                mm = pe.transpose(bank[5][0:HC, NP * g:NP * g + NP], ON[:, 0, 0, HC * g:HC * g + HC], ident[0:NP, 0:NP])
            mm.then_inc(s_m_ot, 1)
            pe.wait_ge(s_m_otc, 1)
            pe.wait_ge(s_presets, 4)
            both_halves(bank[6][:, 0:C], lambda g: OT[:, 0, g, :], lambda g: wo_m[:, g, :], stop=False)
            pe.matmul(bank[6][:, 0:C], ones[:, :], patch_b[:, :], start=False, stop=True).then_inc(s_m_md, 1)

            def turn(n, t, u, b):
                r = rows_of(t)
                pe.wait_ge(s_xn_ready, xt_at(n, t))
                if not (n == LN_TOK and isinstance(t, int) and t == 0):
                    pe.wait_ge(s_xt_ready, xt_at(n, t) - 1)
                for g in range(2):
                    mm = pe.transpose(bank[b][0:HC, 128 * g:128 * g + r], XN[0:r, u, HC * g:HC * g + HC], ident[0:r, 0:r])
                mm.then_inc(s_xt_psum, 1)

            def mixer(t, u):
                last = isinstance(t, int) and t == T - 1
                if not last:
                    tok(t + 1, 1 - u)
                pe.wait_ge(s_xt_ready, xt_at(LN_TOK, t))
                if not (isinstance(t, int) and t == 0):
                    pe.wait_ge(s_silu_ready, t)
                else:
                    pe.wait_ge(s_m_norm, 1)
                    pe.wait_ge(s_ld_up, 16)
                for w, done in ((0, s_up1), (1, s_up3)):
                    if w == 1 and not (isinstance(t, int) and t == 0):
                        pe.wait_ge(s_g_ready, t)
                    for m in range(KP):
                        mm = both_halves(bank[2 * w + m // 4][:, 128 * (m % 4):128 * (m % 4) + 128],
                                         lambda g: w13[:, g, HID * w + 128 * m:HID * w + 128 * m + 128],
                                         lambda g: XT[:, u, g, :], bias=False)
                    mm.then_inc(done, 1)
                if not last:
                    turn(LN_TOK, t + 1, 1 - u, 5)
                pe.wait_ge(s_g_ready, t + 1)
                if not (isinstance(t, int) and t == 0):
                    pe.wait_ge(s_res_ready, t)
                else:
                    pe.wait_ge(s_ld_down, 16)
                for k in range(KP):
                    mm = pe.matmul(bank[6][:, 0:C], gT[:, u, k, :], w2t[:, k, :], start=(k == 0), stop=(k == KP - 1))
                mm.then_inc(s_down_ready, 1)

            turn(LN_TOK, 0, 0, 5)
            in_pairs(pe, mixer)

            for L, n in ((0, LN_ATT), (1, LN_ONE)):
                base = L * (T + 1)

                def qkv(t, u):
                    last = isinstance(t, int) and t == T
                    if not last:
                        turn(n, t + 1, 1 - u, 5)
                    r = rows_of(t)
                    pe.wait_ge(s_xt_ready, xt_at(n, t))
                    if not (base == 0 and isinstance(t, int) and t == 0):
                        pe.wait_ge(s_q_copied, base + t)
                        pe.wait_ge(s_k_copied, base + t)
                    for m in range(4):
                        mm = both_halves(bank[m - m % 2][0:HC, 128 * (m % 2):128 * (m % 2) + r], lambda g: wqkv[L][:, g, HC * m:HC * m + HC],
                                         lambda g: XT[:, u, g, 0:r])
                    mm.then_inc(s_qk_psum, 1)
                    if not (base == 0 and isinstance(t, int) and t == 0):
                        pe.wait_ge(s_v_copied, base + t)
                    if last:
                        if L == 0:
                            for m in range(2):
                                both_halves(bank[1][0:HC, 256 + B * m:256 + B * m + B],
                                            lambda g: wqkv[L][:, g, 2 * C + HC * m:2 * C + HC * m + HC],
                                            lambda g: XT[:, u, g, 0:B])
                        mm = both_halves(bank[1][0:B, 0:C], lambda g: XT[:, u, g, 0:B], lambda g: wqkv[L][:, g, 2 * C:3 * C])
                    else:
                        both_halves(bank[1][:, 0:C], lambda g: XT[:, u, g, :], lambda g: wqkv[L][:, g, 2 * C:3 * C])

                        def by_head(ap, a):
                            return ap.rearrange("p (m a d) -> p m a d", m=PAIRS, a=2)[:, :, a, :]
                        both_halves(by_head(bank[1][NP:128, C:2 * C], 1), lambda g: XT[:, u, g, 0:NP],
                                    lambda g: by_head(wqkv[L][:, g, 2 * C:3 * C], 1))
                        if L == 0:
                            mm = both_halves(by_head(bank[1][0:NP, C:2 * C], 0), lambda g: XT[:, u, g, NP:128],
                                             lambda g: by_head(wqkv[L][:, g, 2 * C:3 * C], 0))
                        else:
                            mm = both_halves(bank[1][0:NP, C:2 * C], lambda g: XT[:, u, g, NP:128],
                                             lambda g: wqkv[L][:, g, 2 * C:3 * C])
                    mm.then_inc(s_v_psum, 1)

                if L == 0:
                    pe.wait_ge(s_ld_attn, 16 * 6)
                    pe.wait_ge(s_res_ready, T)
                else:
                    pe.wait_ge(s_res_ready, 2 * T + 1)
                turn(n, 0, 0, 5)
                in_pairs(pe, qkv)
                qkv(T, 0)

                def scores(t, u):
                    pe.wait_ge(s_q_slot, L * T + t + 1)
                    pe.wait_ge(kb_loaded[u], 16 * HH * (L * T // 2 + 1) + 8 * HH * (t - u))
                    if not (L == 0 and isinstance(t, int) and t == 0):
                        pe.wait_ge(s_sub_ready, L * T + t)
                    for g in range(2):
                        for j in range(2):
                            if L == 0:
                                pe.matmul(bank[2 + g][NP * j:NP * j + NP, 0:HH * S], identb[:, NP * j:NP * j + NP],
                                          maskb[:, :, :], start=True, stop=False)
                            mm = pe.matmul(bank[2 + g][NP * j:NP * j + NP, 0:HH * S], qs[:, u, g, NP * j:NP * j + NP],
                                           KB[:, u, g, :, S * j:S * j + S], start=(L == 1), stop=True)
                    mm.then_inc(s_s_psum, 1)

                def attend(t, u):
                    last = isinstance(t, int) and t == T - 1
                    first = isinstance(t, int) and t == 0
                    if not last:
                        scores(t + 1, 1 - u)
                    pe.wait_ge(s_exp_ready, L * T + t + 1)
                    if not (L == 0 and first):
                        pe.wait_ge(s_pta_copied, L * T + t)
                        pe.wait_ge(s_ptb_copied, L * T + t)
                    for p in range(PAIRS):
                        pe.transpose(bank[4 + p // 4][:, 128 * (p % 4):128 * (p % 4) + 128],
                                     P[:, u, 2 * NP * p:2 * NP * (p + 1)], ident[:, :])
                    pe.transpose(bank[5][0:HEADS, 256:384], P[:, u, HEADS * NP:], ident[:, :]).then_inc(s_pt_psum, 1)
                    if not first:
                        out_turn(t - 1, 1 - u)
                    pe.wait_ge(s_pta_copied, L * T + t + 1)
                    pe.wait_ge(s_ptb_copied, L * T + t + 1)
                    pe.wait_ge(s_vc_slot, L * T + t + 1)
                    for j in range(2):
                        o = bank[6][0:NP, HEADS * VW * j:HEADS * VW * (j + 1)]
                        pe.matmul(o, PT[0:HEADS, u, PAIRS, NP * j:NP * j + NP],
                                  vcs[:, u, j, :], start=True, stop=False)
                        for p in range(PAIRS):
                            mm = pe.matmul(o[:, 2 * VW * p:2 * VW * p + 2 * VW], PT[:, u, p, NP * j:NP * j + NP],
                                           VB[:, 2 * t + j, p].rearrange("p a b -> p (a b)"), start=False, stop=(p == PAIRS - 1))
                    mm.then_inc(s_o_psum, 1)
                    if not first:
                        project(t - 1, 1 - u)

                def out_turn(t, u):
                    pe.wait_ge(s_on_ready, L * T + t + 1)
                    if not (L == 0 and isinstance(t, int) and t == 0):
                        pe.wait_ge(s_ot_copied, L * T + t)
                    own_wait(pe)
                    for g in range(2):
                        for j in range(2):
                            mm = pe.transpose(bank[7][0:HC, 128 * g + NP * j:128 * g + NP * j + NP],
                                              ON[:, u, j, HC * g:HC * g + HC], ident[0:NP, 0:NP])
                    mm.then_inc(s_ot_psum, 1)

                def project(t, u):
                    pe.wait_ge(s_ot_copied, L * T + t + 1)
                    if isinstance(t, int) and t == 0:
                        pe.wait_ge(s_v_copied, (L + 1) * (T + 1))
                    else:
                        pe.wait_ge(s_res_ready, T + L * (T + 1) + t)
                    both_halves(bank[1][:, 0:C], lambda g: OT[:, u, g, :], lambda g: wproj[L][:, g, :]).then_inc(s_proj_psum, 1)

                scores(0, 0)
                pe.wait_ge(s_xt_ready, xt_at(n, T))
                in_pairs(pe, attend)
                out_turn(T - 1, 1)
                project(T - 1, 1)

                if L == 1:
                    pe.wait_ge(s_c_qcb, 2)
                    pe.wait_ge(s_sub_ready, 2 * T)
                    pe.wait_ge(s_ptb_copied, 2 * T)
                    pe.wait_ge(s_pta_copied, 2 * T)
                    for b in range(B):
                        mm = both_halves(bank[2 + b // 7][0:HEADS, S * (b % 7):S * (b % 7) + S],
                                         lambda g: QCB[:, g, b, :], lambda g: kT[:, g, b, :], bias=False)
                    mm.then_inc(s_c_s, 1)
                    pe.wait_ge(s_c_p, 1)
                    for b in range(B):
                        mm = pe.transpose(bank[5][0:S, HEADS * b:HEADS * b + HEADS], Pc[:, b, :], ident[0:HEADS, 0:HEADS])
                    mm.then_inc(s_c_pt, 1)
                    pe.wait_ge(s_c_ptc, 1)
                    pe.wait_ge(s_vn_loaded, 16)
                    pe.wait_ge(s_vn_copied, T)
                    pe.wait_ge(s_on_ready, 2 * T)
                    for g in range(2):
                        for b in range(B):
                            c0 = (g * B + b) * HEADS
                            mm = pe.matmul(bank[6][0:HC, c0:c0 + HEADS], VN[:, b, HC * g:HC * g + HC], PcT[:, b, :],
                                           start=True, stop=True)
                    mm.then_inc(s_c_o, 1)
                pe.wait_ge(s_cls_otc, L + 1)
                pe.wait_ge(s_res_ready, T + L * (T + 1) + T)
                both_halves(bank[1][0:B, 0:C], lambda g: OTc[:, g, :], lambda g: wproj[L][:, g, :]).then_inc(s_proj_psum, 1)

            pe.wait_ge(s_ld_ffn, 32)

            def route(t, u):
                if not (isinstance(t, int) and t == T):
                    turn(LN_TWO, t + 1, 1 - u, 5)
                r = rows_of(t)
                pe.wait_ge(s_xt_ready, xt_at(LN_TWO, t))
                if not (isinstance(t, int) and t == 0):
                    pe.wait_ge(s_lg_copied, t)
                both_halves(bank[0][0:r, 0:E], lambda g: XT[:, u, g, 0:r], lambda g: w_gate[:, g, :], bias=False)\
                    .then_inc(s_lg_psum, 1)

            turn(LN_TWO, 0, 0, 5)
            for t in range(T + 1):
                route(t, t % 2)

            def bias_out(t, u):
                r = rows_of(t)
                if isinstance(t, int) and t == 0:
                    pe.wait_ge(s_gate_ready, 2)
                else:
                    pe.wait_ge(s_b2_added, t)
                pe.transpose(bank[6][0:E, 0:r], gate[0:r, t, :], ident[0:r, 0:r]).then_inc(s_gt_psum, 1)
                pe.wait_ge(s_gt_copied, t + 1)
                pe.matmul(bank[7][0:r, 0:C], gateT[:, u, 0:r], b2[:, :], start=True, stop=True).then_inc(s_b2_psum, 1)

            for t in range(T + 1):
                bias_out(t, t % 2)

            pe.wait_ge(s_xta_ready, T + 1)
            pe.wait_ge(s_b2_added, T + 1)
            pe.sem_inc(s_w_used, 2)

            def expert(e, ue):
                pe.wait_ge(w_loaded[ue], 16 * (e - ue) + 32)

                def one(t, u):
                    r = rows_of(t)
                    k = e * (T + 1) + t
                    first = isinstance(k, int) and k == 0
                    pe.wait_ge(s_h_ready, k + 1)
                    for m in range(KP):
                        mm = both_halves(bank[2 * u + m // 4][:, 128 * (m % 4):128 * (m % 4) + r],
                                         lambda g: w1s[:, ue, g, 128 * m:128 * m + 128],
                                         lambda g: XTA[:, g, tile_cols(t)])
                    mm.then_inc(s_h_psum, 1)
                    if not (isinstance(t, int) and t == 0):
                        down(t - 1, 1 - u)

                def down(t, u):
                    r = rows_of(t)
                    k = e * (T + 1) + t
                    pe.wait_ge(s_h_ready, k + 3)
                    pe.wait_ge(s_y_added, k + 1)
                    for m in range(KP):
                        mm = pe.matmul(bank[6 + u][0:r, 0:C], hT[:, u, m, 0:r], w2s[:, ue, m, :],
                                       start=(m == 0), stop=(m == KP - 1))
                    mm.then_inc(s_y_psum, 1)
                in_pairs(pe, lambda t, u: one(t, (u + ue) % 2))
                one(T, ue)
                down(T, ue)
                pe.wait_ge(s_y_psum, (e + 1) * (T + 1))
                pe.sem_inc(s_w_used, 1)

            with pe.Fori(0, E // 2) as i:
                for ue in range(2):
                    expert(2 * i + ue, ue)

        @block.vector
        def _(dve):
            def stats(n, t, u, src):
                r = rows_of(t)
                at = ln_at(n, t)
                own_wait(dve)
                dve.bn_stats(stat[0:r, 0, :], src).then_inc(s_stat_ready, 1)
                if not (isinstance(t, int) and n == LN_TOK and t < 2):
                    dve.wait_ge(s_veps_ready, at - 1 if isinstance(t, int) and t == 0 and n != LN_ATT else at - 2)
                dve.wait_ge(s_stat_ready, at)
                own_wait(dve)
                dve.bn_aggr(mvs[0:r, u, :], stat[0:r, 0, :]).then_inc(s_mv_ready, 1)
                dve.wait_ge(s_mv_ready, at)
                dve.tensor_copy(mean[0:r, n, t], mvs[0:r, u, 0:1]).then_inc(s_mean_ready, 1)
                dve.wait_ge(s_mean_ready, at)

            def normed(n, t, out, src):
                r = rows_of(t)
                dve.wait_ge(s_rstd_ready, ln_at(n, t))
                return dve.tensor_scalar(out, src, mean[0:r, n, t], rstd[0:r, n, t], ALU.subtract, ALU.mult)

            def to_slot(n, t, u, src):
                at = xt_at(n, t)
                if not (isinstance(t, int) and n == LN_TOK and t < 2):
                    dve.wait_ge(s_xt_psum, at - 2)
                normed(n, t, XN[0:rows_of(t), u, :], src).then_inc(s_xn_ready, 1)

            dve.wait_ge(s_m_q, 1)
            dve.tensor_copy(qm[:, 0:HH, :], bank[0][0:HD, 0:HH * NP]).then_inc(s_m_qc, 1)
            dve.tensor_copy(qm[:, HH:HEADS, :], bank[1][0:HD, 0:HH * NP]).then_inc(s_m_qc, 1)
            dve.wait_ge(s_m_k, 1)
            dve.tensor_copy(km[:, :], bank[2][0:HD, 0:NP]).then_inc(s_m_qc, 1)
            dve.tensor_copy(VM[0:NP, 0, 0:HD], bank[2][0:NP, NP:NP + HD])
            dve.tensor_copy(VM[NP:128, 1, 0:HD], bank[2][NP:128, NP:NP + HD]).then_inc(s_m_qc, 1)
            dve.wait_ge(s_m_s, 1)
            for g in range(2):
                dve.reduce_max(mx[0:NP, 0, HH * g:HH * g + HH], bank[3 + g][0:NP, 0:HH * NP].rearrange("p (h j) -> p h j", h=HH),
                               AX_X).then_inc(s_m_max, 1)
            dve.wait_ge(s_m_max, 2)
            for g in range(2):
                dve.tensor_tensor(weights(0, 0, NP)[:, HH * g:HH * g + HH, :], bank[3 + g][0:NP, 0:HH * NP].rearrange("p (h j) -> p h j", h=HH),
                                  bcast(mx[0:NP, 0, HH * g:HH * g + HH], 2, NP), ALU.subtract).then_inc(s_m_sub, 1)
            dve.wait_ge(s_m_t, 1)
            dve.tensor_copy(PT[:, 0, 0:PAIRS, 0:NP], bank[5][:, 0:PAIRS * NP].rearrange("p (a b) -> p a b", a=PAIRS)).then_inc(s_m_tc, 1)
            dve.wait_ge(s_m_o, 1)
            o = bank[6][0:NP, 0:HEADS * VW].rearrange("p (h v) -> p h v", h=HEADS)
            dve.reciprocal(rec[:, 0, 0:HEADS], o[:, :, HD]).then_inc(s_m_rec, 1)
            dve.wait_ge(s_m_rec, 1)
            dve.tensor_tensor(ON[:, 0, 0].rearrange("p (h v) -> p h v", h=HEADS), o[:, :, 0:HD],
                              bcast(rec[:, 0, 0:HEADS], 2, HD), ALU.mult).then_inc(s_m_norm, 1)
            dve.wait_ge(s_m_ot, 1)
            dve.tensor_copy(OT[0:HC, 0].rearrange("p g (a b) -> p g a b", a=2),
                            bcast(bank[5][0:HC, 0:2 * NP].rearrange("p (g b) -> p g b", g=2), 2, 2)).then_inc(s_m_otc, 1)
            dve.wait_ge(s_m_md, 1)
            dve.tensor_copy(MD[:, :], bank[6][:, 0:C]).then_inc(s_m_mdc, 1)
            dve.wait_ge(s_m_mdc, 1)

            def z_of(t, u):
                dve.wait_ge(s_tok_ready, t + 1)
                dve.tensor_tensor(H[:, t, :], bank[7][:, 0:C], MD[:, :], ALU.add).then_inc(s_z_ready, 1)
                dve.wait_ge(s_z_ready, t + 1)
                stats(LN_TOK, t, u, H[:, t, :])
                to_slot(LN_TOK, t, u, H[:, t, :])

            def mixer(t, u):
                if not (isinstance(t, int) and t == T - 1):
                    z_of(t + 1, 1 - u)
                dve.wait_ge(s_silu_ready, t + 1)
                dve.wait_ge(s_up3, t + 1)
                if not (isinstance(t, int) and t < 2):
                    dve.wait_ge(s_down_ready, t - 1)
                dve.tensor_tensor(gT[:, u, 0:4, :], bank[2][:, :], silu[:, u, 0:4, :], ALU.mult)
                dve.tensor_tensor(gT[:, u, 4:6, :], bank[3][:, 0:256], silu[:, u, 4:6, :], ALU.mult).then_inc(s_g_ready, 1)
                dve.wait_ge(s_down_ready, t + 1)
                dve.tensor_tensor(H[:, t, :], bank[6][:, 0:C], H[:, t, :], ALU.add).then_inc(s_res_ready, 1)

            z_of(0, 0)
            in_pairs(dve, mixer)
            dve.wait_ge(s_res_ready, T)
            dve.wait_ge(s_ld_cls, 16)

            def att_stats(t, u):
                stats(LN_ATT, t, u, H[0:rows_of(t), t, :])
            in_pairs(dve, att_stats)
            att_stats(T, 0)

            for L, n in ((0, LN_ATT), (1, LN_ONE)):
                base = L * (T + 1)
                X = H if L == 0 else U
                if L == 1:
                    def outer(t, u):
                        r = rows_of(t)
                        normed(LN_OUTER, t, U[0:r, t, :], H[0:r, t, :]).then_inc(s_z_ready, 1)
                        dve.wait_ge(s_z_ready, T + t + 1)
                        stats(LN_ONE, t, u, U[0:r, t, :])
                    in_pairs(dve, outer)
                    outer(T, 0)

                def qkv(t, u):
                    last = isinstance(t, int) and t == T
                    if not last:
                        to_slot(n, t + 1, 1 - u, X[0:rows_of(t + 1), t + 1, :])
                    r = rows_of(t)
                    dve.wait_ge(s_qk_psum, base + t + 1)
                    if not (base == 0 and isinstance(t, int) and t == 0) and isinstance(t, int) and t == 0:
                        dve.wait_ge(s_q_slot, T)
                    dve.tensor_copy(qT[:, :, tile_cols(t)], bank[0][0:HC, 0:256].rearrange("p (a b) -> p a b", a=2)[:, :, 0:r])\
                        .then_inc(s_q_copied, 1)
                    dve.wait_ge(s_v_psum, base + t + 1)
                    if isinstance(t, int) and t == 0:
                        if L == 0:
                            dve.wait_ge(s_ld_attn, 16 * 6)
                        else:
                            dve.wait_ge(s_o_psum, T)
                    if last:
                        if L == 0:
                            dve.tensor_copy(OTc[0:HC, :, :], bank[1][0:HC, 256:256 + 2 * B].rearrange("p (a b) -> p a b", a=2))\
                                .then_inc(s_cls_otc, 1)
                        else:
                            dve.wait_ge(s_vcb_loaded, 16 * HEADS)
                        dve.tensor_copy(VC[:, :], bank[1][0:B, 0:C]).then_inc(s_v_copied, 1)
                    else:
                        v = bank[1][:, 0:2 * C].rearrange("p (j m a d) -> p j m a d", j=2, m=PAIRS, a=2)
                        dve.tensor_copy(VB[0:NP, bass.ts(t, 2), :, 0, 0:HD], v[0:NP, :, :, 0, :])
                        for j in range(2):
                            mm = dve.tensor_copy(VB[NP:128, 2 * t + j, :, 1, 0:HD], v[NP:128, 1 - j, :, 1, :])
                        if L == 1:
                            dve.tensor_copy(VN[0:NP, bass.ts(t, 2), :], bank[1][0:NP, 0:2 * C]).then_inc(s_vn_copied, 1)
                            dve.wait_ge(s_vn_copied, t + 1)
                            dve.sem_inc(s_v_copied, 1)
                        else:
                            mm.then_inc(s_v_copied, 1)

                to_slot(n, 0, 0, X[:, 0, :])
                in_pairs(dve, qkv)
                qkv(T, 0)

                def maxes(t, u):
                    dve.wait_ge(s_s_psum, L * T + t + 1)
                    for g in range(2):
                        mm = dve.reduce_max(mx[:, u, HH * g:HH * g + HH], bank[2 + g][:, 0:HH * S].rearrange("p (h j) -> p h j", h=HH), AX_X)
                    mm.then_inc(s_max_ready, 1)

                def residual(t, u):
                    r = rows_of(t)
                    n_res = T + L * (T + 1) + t + 1
                    dve.wait_ge(s_proj_psum, L * (T + 1) + t + 1)
                    dve.tensor_tensor(X[0:r, t, :], bank[1][0:r, 0:C], X[0:r, t, :], ALU.add).then_inc(s_res_ready, 1)
                    dve.wait_ge(s_res_ready, n_res)
                    stats(LN_OUTER if L == 0 else LN_TWO, t, u, X[0:r, t, :])

                def attend(t, u):
                    first = isinstance(t, int) and t == 0
                    dve.wait_ge(s_max_ready, L * T + t + 1)
                    if not (isinstance(t, int) and L * T + t < 2):
                        dve.wait_ge(s_pt_psum, L * T + t - 1)
                    for g in range(2):
                        sc = bank[2 + g][:, 0:HH * S].rearrange("p (h j) -> p h j", h=HH)
                        m = mx[:, u, HH * g:HH * g + HH]
                        dve.tensor_tensor(weights(u, 0, 128)[:, HH * g:HH * g + HH, :], sc[:, :, 0:NP], bcast(m, 2, NP), ALU.subtract)
                        c0 = HEADS * NP + HH * g
                        mm = dve.tensor_tensor(P[:, u, c0:c0 + HH], sc[:, :, NP], m, ALU.subtract)
                    mm.then_inc(s_sub_ready, 1)
                    if not (isinstance(t, int) and t == T - 1):
                        maxes(t + 1, 1 - u)
                    dve.wait_ge(s_pt_psum, L * T + t + 1)
                    if not (isinstance(t, int) and L * T + t < 2):
                        dve.wait_ge(s_o_psum, L * T + t - 1)
                    dve.tensor_copy(PT[:, u, 4:6, :], bank[5][:, 0:256])
                    dve.tensor_copy(PT[0:HEADS, u, 6, :], bank[5][0:HEADS, 256:384]).then_inc(s_ptb_copied, 1)
                    dve.wait_ge(s_o_psum, L * T + t + 1)
                    o = bank[6][0:NP, 0:2 * HEADS * VW].rearrange("p (h v) -> p h v", v=VW)
                    dve.reciprocal(rec[:, u, :], o[:, :, HD]).then_inc(s_rec_ready, 1)
                    dve.wait_ge(s_rec_ready, L * T + t + 1)
                    dve.tensor_tensor(ON[:, u].rearrange("p j (h v) -> p (j h) v", v=HD), o[:, :, 0:HD],
                                      bcast(rec[:, u, :], 2, HD), ALU.mult).then_inc(s_on_ready, 1)
                    if not first:
                        residual(t - 1, 1 - u)

                maxes(0, 0)
                in_pairs(dve, attend)
                residual(T - 1, 1)
                if L == 1:
                    dve.wait_ge(s_c_s, 1)
                    spans = ((0, 7), (7, 14), (14, 16))
                    sc = [bank[2 + i][0:HEADS, 0:S * (b1 - b0)].rearrange("p (b j) -> p b j", j=S) for i, (b0, b1) in enumerate(spans)]
                    for i, (b0, b1) in enumerate(spans):
                        dve.reduce_max(mxc[:, b0:b1], sc[i], AX_X).then_inc(s_c_max, 1)
                    dve.wait_ge(s_c_max, 3)
                    for i, (b0, b1) in enumerate(spans):
                        dve.tensor_tensor(Pc[:, b0:b1, :], sc[i], bcast(mxc[:, b0:b1], 2, S), ALU.subtract).then_inc(s_c_sub, 1)
                    dve.wait_ge(s_c_exp, 1)
                    dve.reduce_sum(smc[:, :], Pc[:, :, :], AX_X).then_inc(s_c_sum, 1)
                    dve.wait_ge(s_c_sum, 1)
                    dve.reciprocal(mxc[:, :], smc[:, :]).then_inc(s_c_rec, 1)
                    dve.wait_ge(s_c_rec, 1)
                    dve.tensor_tensor(Pc[:, :, :], Pc[:, :, :], bcast(mxc[:, :], 2, S), ALU.mult).then_inc(s_c_p, 1)
                    dve.wait_ge(s_c_pt, 1)
                    dve.tensor_copy(PcT[:, :, :], bank[5][0:S, 0:B * HEADS]).then_inc(s_c_ptc, 1)
                    dve.wait_ge(s_c_o, 1)
                    for g in range(2):
                        dve.tensor_tensor(OCm[:, g], bank[6][0:HC, g * B * HEADS:(g + 1) * B * HEADS].rearrange("p (b h) -> p b h", b=B),
                                          bcast(head_mask[:, g, :], 1, B), ALU.mult).then_inc(s_c_om, 1)
                    dve.wait_ge(s_c_om, 2)
                    dve.reduce_sum(OTc[0:HC, :, :], OCm[:, :, :, :], AX_X).then_inc(s_cls_otc, 1)
                residual(T, 0)

            def route(t, u):
                if not (isinstance(t, int) and t == T):
                    to_slot(LN_TWO, t + 1, 1 - u, U[0:rows_of(t + 1), t + 1, :])
                r = rows_of(t)
                dve.wait_ge(s_lg_psum, t + 1)
                dve.tensor_copy(lg[0:r, u, :], bank[0][0:r, 0:E]).then_inc(s_lg_copied, 1)
                dve.wait_ge(s_lg_copied, t + 1)
                dve.max(mx8[0:r, t, :], lg[0:r, u, :]).then_inc(s_mx8_ready, 1)
                dve.wait_ge(s_mx8_ready, t + 1)
                dve.max_index(ix8[0:r, t, :], mx8[0:r, t, :], lg[0:r, u, :]).then_inc(s_ix8_ready, 1)
            to_slot(LN_TWO, 0, 0, U[:, 0, :])
            for t in range(T + 1):
                route(t, t % 2)
            dve.wait_ge(s_ix8_ready, T + 1)
            for k, (r, ts) in enumerate(((128, slice(0, T)), (B, slice(T, T + 1)))):
                nt = T if k == 0 else 1
                dve.tensor_copy(ixf[0:r, ts, :], ix8[0:r, ts, 0:2]).then_inc(s_r1, 1)
                dve.tensor_tensor(e2[0:r, ts, :], mx8[0:r, ts, 1:2], mx8[0:r, ts, 0:1], ALU.subtract).then_inc(s_r2, 1)
                dve.wait_ge(s_r3, k + 1)
                dve.tensor_scalar(g12[0:r, ts, 0:1], e2[0:r, ts, :], 1.0, None, ALU.add).then_inc(s_r4, 1)
                dve.wait_ge(s_r4, k + 1)
                dve.reciprocal(g12[0:r, ts, 0:1], g12[0:r, ts, 0:1]).then_inc(s_r5, 1)
                dve.wait_ge(s_r5, k + 1)
                dve.tensor_tensor(g12[0:r, ts, 1:2], e2[0:r, ts, :], g12[0:r, ts, 0:1], ALU.mult).then_inc(s_r6, 1)
                dve.wait_ge(s_r1, k + 1)
                for j in range(2):
                    c = 2 * k + j
                    out = gate if j == 0 else hot
                    dve.tensor_tensor(out[0:r, ts, :], bcast(iota8[0:r, :], 1, nt), ixf[0:r, ts, j:j + 1].to_broadcast([r, nt, E]),
                                      ALU.is_equal).then_inc(s_r7, 1)
                    dve.wait_ge(s_r7, c + 1)
                    dve.wait_ge(s_r6, k + 1)
                    dve.tensor_tensor(out[0:r, ts, :], out[0:r, ts, :], g12[0:r, ts, j:j + 1].to_broadcast([r, nt, E]),
                                      ALU.mult).then_inc(s_r8, 1)
                dve.wait_ge(s_r8, 2 * k + 2)
                dve.tensor_tensor(gate[0:r, ts, :], gate[0:r, ts, :], hot[0:r, ts, :], ALU.add).then_inc(s_gate_ready, 1)
            for t in range(T + 1):
                r = rows_of(t)
                dve.wait_ge(s_gt_psum, t + 1)
                dve.tensor_copy(gateT[:, t % 2, 0:r], bank[6][0:E, 0:r]).then_inc(s_gt_copied, 1)
                dve.tensor_tensor(H[0:r, t, :], H[0:r, t, :], U[0:r, t, :], ALU.add).then_inc(s_c_om, 1)
                dve.wait_ge(s_c_om, 3 + t)
                dve.wait_ge(s_b2_psum, t + 1)
                dve.tensor_tensor(H[0:r, t, :], bank[7][0:r, 0:C], H[0:r, t, :], ALU.add).then_inc(s_b2_added, 1)
            dve.wait_ge(s_b2_added, T + 1)
            dve.sem_inc(s_y_added, 2)
            with dve.Fori(0, E // 2) as i:
                for ue in range(2):
                    e = 2 * i + ue

                    def add(t, u):
                        r = rows_of(t)
                        k = e * (T + 1) + t
                        dve.wait_ge(s_y_psum, k + 1)
                        dve.wait_ge(s_y_added, k + 1)
                        dve.scalar_tensor_tensor(out=H[0:r, t, :], in0=bank[6 + u][0:r, 0:C], scalar=gate[0:r, t, bass.ds(e, 1)],
                                                 in1=H[0:r, t, :], op0=ALU.mult, op1=ALU.add).then_inc(s_y_added, 1)
                    in_pairs(dve, lambda t, u: add(t, (u + ue) % 2))
                    add(T, ue)
            dve.wait_ge(s_y_added, 2 + E * (T + 1))
            dve.sem_inc(s_fin_ready, T + 1)

        @block.scalar
        def _(act):
            act.wait_ge(s_m_sub, 2)
            act.activation(P[0:NP, 0, 0:HEADS * NP], P[0:NP, 0, 0:HEADS * NP], ACT.Exp, scale=SCALE).then_inc(s_m_exp, 1)

            def turned(n, t, u, cols):
                r = rows_of(t)
                act.wait_ge(s_xt_psum, xt_at(n, t))
                for g in range(2):
                    src = bank[5][0:HC, 128 * g:128 * g + r]
                    dst = XT[0:HC, u, g, 0:r]
                    if cols is None:
                        a = act.activation(dst, src, ACT.Copy)
                    else:
                        a = act.activation(dst, src, ACT.Identity, bias=ln_cols[:, cols, 1, g:g + 1], scale=ln_cols[:, cols, 0, g:g + 1])
                a.then_inc(s_xt_ready, 1)

            act.wait_ge(s_ld_const, 16 * N_CONST)
            turned(LN_TOK, 0, 0, 0)

            def mixer(t, u):
                act.wait_ge(s_up1, t + 1)
                if not (isinstance(t, int) and t < 2):
                    act.wait_ge(s_g_ready, t - 1)
                act.activation(silu[:, u, 0:4, :], bank[0][:, :], ACT.Silu)
                act.activation(silu[:, u, 4:6, :], bank[1][:, 0:256], ACT.Silu).then_inc(s_silu_ready, 1)
                if not (isinstance(t, int) and t == T - 1):
                    turned(LN_TOK, t + 1, 1 - u, 0)
            in_pairs(act, mixer)

            for L, n in ((0, LN_ATT), (1, LN_ONE)):
                base = L * (T + 1)
                cols = None if L == 0 else 1

                def qkv(t, u):
                    last = isinstance(t, int) and t == T
                    first = isinstance(t, int) and t == 0
                    if not last:
                        if not (base == 0 and first):
                            act.wait_ge(s_v_psum, base + t)
                        turned(n, t + 1, 1 - u, cols)
                    act.wait_ge(s_qk_psum, base + t + 1)
                    if L == 1 and first:
                        for u2 in range(2):
                            act.wait_ge(kb_loaded[u2], 16 * HH * (T // 2))
                    src = bank[2][0:HC, 0:256].rearrange("p (a c) -> p a c", a=2)
                    if last:
                        act.activation(kT[:, :, :, NP], src[:, :, 0:B], ACT.Copy).then_inc(s_k_copied, 1)
                    else:
                        for g in range(2):
                            a = act.activation(kT[:, g, bass.ts(t, 2), 0:NP], src[:, g, :].rearrange("p (j c) -> p j c", j=2), ACT.Copy)
                        a.then_inc(s_k_copied, 1)
                if L == 0:
                    act.wait_ge(s_up3, T)
                else:
                    act.wait_ge(s_v_psum, base)
                turned(n, 0, 0, cols)
                in_pairs(act, qkv)
                qkv(T, 0)

                def attend(t, u):
                    act.wait_ge(s_sub_ready, L * T + t + 1)
                    act.activation(P[:, u], P[:, u], ACT.Exp, scale=SCALE).then_inc(s_exp_ready, 1)
                    act.wait_ge(s_pt_psum, L * T + t + 1)
                    if not (isinstance(t, int) and L * T + t < 2):
                        act.wait_ge(s_o_psum, L * T + t - 1)
                    act.activation(PT[:, u, 0:4, :], bank[4][:, :], ACT.Copy).then_inc(s_pta_copied, 1)
                    if not (isinstance(t, int) and t == 0):
                        turned_out(t - 1, 1 - u)

                def turned_out(t, u):
                    act.wait_ge(s_ot_psum, L * T + t + 1)
                    if not (isinstance(t, int) and t < 2):
                        act.wait_ge(s_proj_psum, L * (T + 1) + t)
                    act.activation(OT[0:HC, u], bank[7][0:HC, 0:256].rearrange("p (a c) -> p a c", a=2), ACT.Copy).then_inc(s_ot_copied, 1)

                in_pairs(act, attend)
                turned_out(T - 1, 1)
                if L == 1:
                    act.wait_ge(s_c_sub, 3)
                    act.activation(Pc[:, :, :], Pc[:, :, :], ACT.Exp, scale=SCALE).then_inc(s_c_exp, 1)

            def route(t, u):
                if not (isinstance(t, int) and t == T):
                    if not (isinstance(t, int) and t == 0):
                        act.wait_ge(s_lg_psum, t)
                        act.wait_ge(s_xta_ready, t)
                    turned(LN_TWO, t + 1, 1 - u, 2)
            turned(LN_TWO, 0, 0, 2)
            for t in range(T):
                route(t, t % 2)
            for k, (r, ts) in enumerate(((128, slice(0, T)), (B, slice(T, T + 1)))):
                act.wait_ge(s_r2, k + 1)
                act.activation(e2[0:r, ts, :], e2[0:r, ts, :], ACT.Exp).then_inc(s_r3, 1)

            act.sem_inc(s_h_ready, 2)
            with act.Fori(0, E // 2) as i:
                for ue in range(2):
                    e = 2 * i + ue

                    def gelu(t, u):
                        r = rows_of(t)
                        k = e * (T + 1) + t
                        act.wait_ge(s_h_psum, k + 1)
                        act.wait_ge(s_y_added, k + 1)
                        act.activation(hT[:, u, 0:4, 0:r], bank[2 * u][:, :].rearrange("p (m c) -> p m c", m=4)[:, :, 0:r], ACT.Gelu)
                        act.activation(hT[:, u, 4:6, 0:r], bank[2 * u + 1][:, 0:256].rearrange("p (m c) -> p m c", m=2)[:, :, 0:r],
                                       ACT.Gelu).then_inc(s_h_ready, 1)
                    in_pairs(act, lambda t, u: gelu(t, (u + ue) % 2))
                    gelu(T, ue)

        @block.gpsimd
        def _(pool):
            for n, (buf, value) in enumerate(((mhalf[:, :], -0.5), (OT[HC:HC + 1], 1.0), (OTc[HC:HC + 1], 1.0), (XT[HC:HC + 1], 1.0))):
                pool.memset(buf, value).then_inc(s_presets, 1)
                pool.wait_ge(s_presets, n + 1)
            pool.memset(KB[:], 0.0).then_inc(s_kb_zero, 1)
            pool.wait_ge(s_kb_zero, 1)

            def inv_std(n, t, u):
                r = rows_of(t)
                at = ln_at(n, t)
                pool.wait_ge(s_mv_ready, at)
                own_wait(pool)
                pool.tensor_scalar(veps[0:r, u], mvs[0:r, u, 1:2], LN_EPS, None, ALU.add).then_inc(s_veps_ready, 1)
                pool.wait_ge(s_veps_ready, at)
                pool.tensor_tensor(rstd[0:r, n, t], veps[0:r, u], mhalf[0:r, :], ALU.pow).then_inc(s_rstd_ready, 1)
                pool.wait_ge(s_rstd_ready, at)

            def all_stats(n):
                in_pairs(pool, lambda t, u: inv_std(n, t, u))
                if n != LN_TOK:
                    inv_std(n, T, 0)

            all_stats(LN_TOK)
            pool.wait_ge(s_down_ready, T)
            pool.memset(XTA[HC:HC + 1], 1.0).then_inc(s_kb_zero, 1)
            pool.wait_ge(s_kb_zero, 2)
            all_stats(LN_ATT)
            for L in range(2):
                if L == 1:
                    all_stats(LN_ONE)
                    pool.wait_ge(s_q_copied, 2 * (T + 1))
                    for g in range(2):
                        pool.tensor_tensor(QCB[:, g], qT[:, g, T * 128:T * 128 + B].unsqueeze(2).to_broadcast([HC, B, HEADS]),
                                           bcast(head_mask[:, g, :], 1, B), ALU.mult).then_inc(s_c_qcb, 1)

                def queries(t, u):
                    pool.wait_ge(s_q_copied, L * (T + 1) + t + 1)
                    if not (isinstance(t, int) and L * T + t < 2):
                        pool.wait_ge(s_s_psum, L * T + t - 1)
                    pool.tensor_copy(qs[:, u], qT[:, :, bass.ts(t, 128)]).then_inc(s_q_slot, 1)
                    if isinstance(t, int) and t == 0:
                        pool.wait_ge(s_vcb_loaded, 16 * HEADS * (L + 1))
                    if not (isinstance(t, int) and L * T + t < 2):
                        pool.wait_ge(s_o_psum, L * T + t - 1)
                    pool.wait_ge(s_q_slot, L * T + t + 1)
                    pool.tensor_copy(vcs[:, u], VCB[:, bass.ts(t, 2), :]).then_inc(s_vc_slot, 1)
                    pool.wait_ge(s_vc_slot, L * T + t + 1)
                queries(0, 0)
                queries(1, 1)

                def ahead(t, u):
                    queries(t, u)
                with pool.Fori(1, T // 2) as i:
                    for u in range(2):
                        queries(2 * i + u, u)
                        inv_std(LN_OUTER if L == 0 else LN_TWO, 2 * i + u - 2, u)
                for t in range(T - 2, T + 1):
                    inv_std(LN_OUTER if L == 0 else LN_TWO, t, t % 2)

            def keep(t, u):
                r = rows_of(t)
                pool.wait_ge(s_xt_ready, xt_at(LN_TWO, t))
                pool.tensor_copy(XTA[0:HC, :, tile_cols(t)], XT[0:HC, u, :, 0:r]).then_inc(s_xta_ready, 1)
            in_pairs(pool, keep)
            keep(T, 0)


def kernel(x, cls_tok, **w):
    import concourse.bacc as bacc
    from concourse.bass_utils import run_bass_kernel_spmd

    arrays = {f"in_{n}": a for n, a in layout(x, cls_tok, w).items()}
    nc = bacc.Bacc("TRN2", target_bir_lowering=False, num_devices=1)
    d = {n[3:]: nc.dram_tensor(n, a.shape, mybir.dt.from_np(a.dtype), kind="ExternalInput").ap() for n, a in arrays.items()}
    d["out"] = nc.dram_tensor("out", (B, S, C), F32, kind="ExternalOutput").ap()
    build(nc, d)
    return run_bass_kernel_spmd(nc, [arrays], core_ids=[0]).results[0]["out"]


def layout(x, cls_tok, w):
    def halves(a, bias=None, row=False):
        a = np.asarray(a)
        out = np.zeros((HC + int(row or bias is not None), 2, a.shape[1]), np.float32)
        out[0:HC] = a.reshape(2, HC, a.shape[1]).transpose(1, 0, 2)
        if bias is not None:
            out[HC, 1] = np.asarray(bias)
        return out

    def chunks(a):
        a = np.asarray(a)
        return np.ascontiguousarray(a.reshape(KP, 128, a.shape[1]).transpose(1, 0, 2))

    side, patch = 8, 16
    p = np.asarray(x).reshape(B, 3, side, patch, side, patch).transpose(0, 2, 4, 3, 5, 1)
    p = p.reshape(T, 128, KP, 128).transpose(0, 3, 2, 1)

    scales = np.linspace(1.0, 5.0, C // 4)
    seq = np.linspace(-1.0, 1.0, side)[:, None] * scales[None, :] * np.pi
    xs = np.broadcast_to(seq[:, None, :], (side, side, C // 4))
    ys = np.broadcast_to(seq[None, :, :], (side, side, C // 4))
    sin = np.repeat(np.concatenate([np.sin(xs), np.sin(ys)], -1).reshape(NP, C // 2), 2, axis=-1)
    sinT = halves(np.tile(sin.T.astype(np.float32), (1, 2)), row=True)
    sinT[HC] = 1.0

    i, j = np.arange(128)[:, None] % NP, np.arange(S)[None, :]
    mask = np.where((j <= i) | (j == NP), 0.0, -1e30)
    mask = np.broadcast_to(mask[:, None, :], (128, HH, S)).astype(np.dtype("bfloat16"))
    head_mask = np.zeros((HC, 2, HEADS), np.float32)
    for h in range(HEADS):
        head_mask[HD * (h % HH):HD * (h % HH) + HD, h // HH, h] = 1.0
    vb0 = np.zeros((128, B, PAIRS, 2, VW), np.float32)
    vb0[0:NP, :, :, 0, HD] = 1.0
    vb0[NP:128, :, :, 1, HD] = 1.0
    vcb0 = np.zeros((HEADS, B, HEADS * VW), np.float32)
    for h in range(HEADS):
        vcb0[h, :, VW * h + HD] = 1.0
    cols = np.stack([np.stack([np.asarray(w[n]).reshape(2, HC).T for n in pair], 1) for pair in (
        ("L0_tok_ln_g", "L0_tok_ln_b"), ("L0_ffn_ln1_g", "L0_ffn_ln1_b"), ("L0_ffn_ln2_g", "L0_ffn_ln2_b"))], 1)
    return {
        "patches": np.ascontiguousarray(p),
        "cls": np.ascontiguousarray(np.broadcast_to(np.asarray(cls_tok).reshape(1, C), (B, C))),
        "sinT": sinT.reshape(HC + 1, 2, 2, NP),
        "ident": np.eye(128, dtype=np.float32),
        "identb": np.eye(128).astype(np.dtype("bfloat16")),
        "maskb": np.ascontiguousarray(mask),
        "ones": np.ones((1, 128), np.float32),
        "head_mask": head_mask,
        "iota8": np.broadcast_to(np.arange(E, dtype=np.float32), (128, E)).copy(),
        "vm0": vb0[:, 0, 0].copy(),
        "vb0": vb0,
        "vcb0": vcb0,
        "ln_cols": np.ascontiguousarray(cols),
        "patch_b": np.asarray(w["L0_tok_patch_b"]).reshape(1, C),
        "w_patch": chunks(w["L0_tok_patch_w"]),
        "wqkv_m": halves(w["L0_tok_wqkv"], w["L0_tok_bqkv"]),
        "wo_m": halves(w["L0_tok_wo"], w["L0_tok_bo"]),
        "w13": halves(np.concatenate([np.asarray(w["L0_tok_w1"]), np.asarray(w["L0_tok_w3"])], 1)),
        "w2t": chunks(w["L0_tok_w2"]),
        "wqkv0": halves(w["L0_attn_w_attn"], w["L0_attn_b_attn"]),
        "wproj0": halves(w["L0_attn_w_proj"], w["L0_attn_b_proj"]),
        "wqkv1": halves(w["L0_ffn_qkv_w"], w["L0_ffn_qkv_b"]),
        "wproj1": halves(w["L0_ffn_proj_w"], w["L0_ffn_proj_b"]),
        "w_gate": halves(w["L0_ffn_gate_w"]),
        "w1": np.stack([halves(np.asarray(w["L0_ffn_w1"])[e], np.asarray(w["L0_ffn_b1"])[e]) for e in range(E)]),
        "w2": np.stack([chunks(np.asarray(w["L0_ffn_w2"])[e]) for e in range(E)]),
        "b2": np.asarray(w["L0_ffn_b2"]),
    }
```

```python
from contextlib import ExitStack

import numpy as np
import concourse.bass as bass
from concourse import mybir

F32 = mybir.dt.float32
BF16 = mybir.dt.bfloat16
U32 = mybir.dt.uint32
ALU = mybir.AluOpType
ACT = mybir.ActivationFunctionType
AX_X = mybir.AxisListType.X

B = 16
NP = 64
S = NP + 1
C = 192
HC = C // 2
HEADS = 12
HD = C // HEADS
HH = HEADS // 2
PAIRS = HEADS // 2
VW = HD + 1
T = B * NP // 128
CLS = T
HID = 4 * C
KP = HID // 128
E = 8
TOP = 2
MT = (TOP * B * S + E * 127) // 128
SLOTS = MT * 128
LN_EPS = 1e-5
SCALE = 0.25
BANK = 512
LN_TOK, LN_ATT, LN_OUTER, LN_ONE, LN_TWO = range(5)


def rows_of(t):
    return B if isinstance(t, int) and t == CLS else 128


def bcast(ap, at, n):
    a = ap.unsqueeze(at)
    shape = list(a.shape)
    shape[at] = n
    return a.to_broadcast(shape)


def in_pairs(eng, step, n=T, tail=1):
    assert (n - 1 - tail) % 2 == 0
    step(0, 0)
    with eng.Fori(0, (n - 1 - tail) // 2) as i:
        step(2 * i + 1, 1)
        step(2 * i + 2, 0)
    for t in range(n - tail, n):
        step(t, t % 2)


def is_tile(t, *which):
    return isinstance(t, int) and t in which


def build(nc, d, dbg=None):
    with ExitStack() as ctx:
        def sb(name, shape, dt=F32):
            return ctx.enter_context(nc.sbuf_tensor(name, shape, dt))

        def sem(name):
            return ctx.enter_context(nc.semaphore(name))

        bank = [ctx.enter_context(nc.psum_tensor(f"bank{i}", [128, BANK], F32)) for i in range(8)]

        ident = sb("ident", [128, 128])
        identb = sb("identb", [128, 128], BF16)
        maskb = sb("maskb", [128, HH, S], BF16)
        ones = sb("ones", [1, 128])
        head_mask = sb("head_mask", [HC, 2, HEADS])
        ln_cols = sb("ln_cols", [HC, 3, 2, 2])
        sinT = sb("sinT", [HC + 1, 2, 2, NP])
        patch_b = sb("patch_b", [1, C])
        wqkv_m = sb("wqkv_m", [HC + 1, 2, C + 2 * HD])
        wo_m = sb("wo_m", [HC + 1, 2, C])
        w_patch = sb("w_patch", [128, KP, C])
        w2t = sb("w2t", [128, KP, C])
        wqkv = [sb(f"wqkv{L}", [HC + 1, 2, 3 * C]) for L in range(2)]
        wproj = [sb(f"wproj{L}", [HC + 1, 2, C]) for L in range(2)]
        w_gate = sb("w_gate", [HC, 2, E])
        b2 = sb("b2", [E, C])
        iota8 = sb("iota8", [128, E])

        H = sb("H", [128, T + 1, C])
        U = sb("U", [128, T + 1, C])
        stat = sb("stat", [128, 2, 6])
        mean = sb("mean", [128, 5, T + 1, 1])
        mvs = sb("mvs", [128, 4, 2])
        veps = sb("veps", [128, 4, 1])
        rstd = sb("rstd", [128, 5, T + 1, 1])
        mhalf = sb("mhalf", [128, 1])
        MD = sb("MD", [128, C])
        XN = sb("XN", [128, 2, C])
        XT = sb("XT", [HC + 1, 2, 2, 128])

        def carve(region, specs):
            at, views = 0, []
            for rows, sizes in specs:
                names = "abcde"[0:len(sizes)]
                n = int(np.prod(sizes))
                views.append(region[0:rows, at:at + n].rearrange(
                    f"p ({' '.join(names)}) -> p {' '.join(names)}", **dict(zip(names, sizes))))
                at += n
            return views

        mixer_mem = sb("mixer_mem", [128, E * KP * C])
        w13, px, silu, gT = carve(mixer_mem, (
            (HC, (2, 2 * HID)), (128, (2, KP, 128)), (128, (2, KP, 128)), (128, (2, KP, 128))))
        w2r, = carve(mixer_mem, ((128, (E, KP, C)),))

        attn_specs = ((HC, (2, 2, HH, 2 * S)), (128, (B, PAIRS, 2, VW)), (HEADS, (B, HEADS * VW)),
                      (128, (2, HEADS * S)), (128, (2, PAIRS + 1, 128)))
        attn_mem = sb("attn_mem", [128, sum(int(np.prod(sizes)) for _, sizes in attn_specs)])
        KB, VB, VCB, P, PT = carve(attn_mem, attn_specs)
        w1r, = carve(attn_mem, ((HC + 1, (E, 2, HID)),))

        qkv_specs = ((HC, (2, T * 128 + B)), (HC, (2, B, S)), (S, (B, C)))
        qkv_mem = sb("qkv_mem", [128, sum(int(np.prod(sizes)) for _, sizes in qkv_specs)])
        qT, kT, VN = carve(qkv_mem, qkv_specs)
        Y0, Y1, hid, hT, XG = carve(qkv_mem, (
            (128, (T + 1, C)), (128, (T + 1, C)), (128, (2, HID)), (128, (2, KP, 128)), (128, (2, C))))
        Y = (Y0, Y1)
        zero = qkv_mem[:, qkv_mem.shape[1] - SLOTS * C // 128 // 3:]
        VC = sb("VC", [B, C])
        vcs = sb("vcs", [HEADS, 2, 2, HEADS * VW])
        qs = sb("qs", [HC, 2, 2, 128])
        mx = sb("mx", [128, 2, HEADS])
        rec = sb("rec", [NP, 2, 2 * HEADS])
        ON = sb("ON", [NP, 2, 2, C])
        OT = sb("OT", [HC + 1, 2, 2, 128])
        OTc = sb("OTc", [HC + 1, 2, B])
        QCB = sb("QCB", [HC, 2, B, HEADS])
        Pc = sb("Pc", [HEADS, B, S])
        mxc = sb("mxc", [HEADS, B])
        smc = sb("smc", [HEADS, B])
        PcT = sb("PcT", [S, B, HEADS])
        OCm = sb("OCm", [HC, 2, B, HEADS])
        qm = sb("qm", [HD, HEADS, NP])
        km = sb("km", [HD, NP])
        VM = sb("VM", [128, 2, VW])
        XA = sb("XA", [128, T + 1, C])
        lg = sb("lg", [128, T + 1, E])
        mx8 = sb("mx8", [128, T + 1, 8])
        ix8 = sb("ix8", [128, T + 1, 8], U32)
        ixf = sb("ixf", [128, T + 1, TOP])
        e2 = sb("e2", [128, T + 1, 1])
        g12 = sb("g12", [128, T + 1, TOP])
        hot = sb("hot", [128, TOP, T + 1, E])
        picked = sb("picked", [128, T + 1, E])
        gate = sb("gate", [128, T + 1, E])
        gate2 = sb("gate2", [128, T + 1, E])
        gateT = sb("gateT", [E, 2, 128])
        tri = sb("tri", [128, 128])
        ones128 = sb("ones128", [128, 128])
        steps = sb("steps", [128, T + 2])
        before = sb("before", [128, E, E])
        tile_no = sb("tile_no", [1, MT])
        rank = sb("rank", [128, T + 1, E])
        total = sb("total", [128, E])
        full = sb("full", [128, E, T + 2])
        tiles = sb("tiles", [128, E])
        ahead = sb("ahead", [128, E, E])
        first = sb("first", [128, E])
        last = sb("last", [1, E])
        past = sb("past", [1, MT, E])
        ownerf = sb("ownerf", [1, MT])
        owner = sb("owner", [1, MT], U32)
        place = sb("place", [128, TOP, T + 1, E])
        slotf = sb("slotf", [128, TOP, T + 1])
        slot = sb("slot", [128, TOP, T + 1], U32)
        YS = sb("YS", [128, 2, C])
        x_slots = nc.dram_tensor("x_slots", (SLOTS, C), F32, kind="Internal").ap()
        y_slots = nc.dram_tensor("y_slots", (SLOTS, C), F32, kind="Internal").ap()

        s_ld_const = sem("s_ld_const")
        s_ld_mixer = sem("s_ld_mixer")
        s_ld_up = sem("s_ld_up")
        s_ld_down = sem("s_ld_down")
        s_ld_attn = sem("s_ld_attn")
        s_ld_ffn = sem("s_ld_ffn")
        s_ld_px0 = sem("s_ld_px0")
        s_ld_px1 = sem("s_ld_px1")
        s_ld_cls = sem("s_ld_cls")
        s_out_done = sem("s_out_done")
        s_m_q = sem("s_m_q")
        s_m_k = sem("s_m_k")
        s_m_qc = sem("s_m_qc")
        s_m_s = sem("s_m_s")
        s_m_max = sem("s_m_max")
        s_m_sub = sem("s_m_sub")
        s_m_exp = sem("s_m_exp")
        s_m_t = sem("s_m_t")
        s_m_tc = sem("s_m_tc")
        s_m_o = sem("s_m_o")
        s_m_rec = sem("s_m_rec")
        s_m_norm = sem("s_m_norm")
        s_m_ot = sem("s_m_ot")
        s_m_otc = sem("s_m_otc")
        s_m_md = sem("s_m_md")
        s_m_mdc = sem("s_m_mdc")
        s_tok_ready = sem("s_tok_ready")
        s_z_ready = sem("s_z_ready")
        s_stat_ready = sem("s_stat_ready")
        s_mv_ready = sem("s_mv_ready")
        s_mean_ready = sem("s_mean_ready")
        s_veps_ready = sem("s_veps_ready")
        s_rstd_ready = sem("s_rstd_ready")
        s_xn_ready = sem("s_xn_ready")
        s_xt_psum = sem("s_xt_psum")
        s_xt_ready = sem("s_xt_ready")
        s_up1 = sem("s_up1")
        s_up3 = sem("s_up3")
        s_silu_ready = sem("s_silu_ready")
        s_g_ready = sem("s_g_ready")
        s_down_ready = sem("s_down_ready")
        s_res_ready = sem("s_res_ready")
        s_qk_psum = sem("s_qk_psum")
        s_v_psum = sem("s_v_psum")
        s_k_copied = sem("s_k_copied")
        s_q_copied = sem("s_q_copied")
        s_v_copied = sem("s_v_copied")
        s_vn_copied = sem("s_vn_copied")
        s_kb_loaded0 = sem("s_kb_loaded0")
        s_kb_loaded1 = sem("s_kb_loaded1")
        s_vcb_loaded = sem("s_vcb_loaded")
        s_vn_loaded = sem("s_vn_loaded")
        s_q_slot = sem("s_q_slot")
        s_vc_slot = sem("s_vc_slot")
        s_own_waits = sem("s_own_waits")
        s_s_psum = sem("s_s_psum")
        s_max_ready = sem("s_max_ready")
        s_sub_ready = sem("s_sub_ready")
        s_exp_ready = sem("s_exp_ready")
        s_pt_psum = sem("s_pt_psum")
        s_pta_copied = sem("s_pta_copied")
        s_ptb_copied = sem("s_ptb_copied")
        s_o_psum = sem("s_o_psum")
        s_rec_ready = sem("s_rec_ready")
        s_on_ready = sem("s_on_ready")
        s_ot_psum = sem("s_ot_psum")
        s_ot_copied = sem("s_ot_copied")
        s_proj_psum = sem("s_proj_psum")
        s_presets = sem("s_presets")
        s_kb_zero = sem("s_kb_zero")
        s_cls_otc = sem("s_cls_otc")
        s_c_qcb = sem("s_c_qcb")
        s_c_s = sem("s_c_s")
        s_c_max = sem("s_c_max")
        s_c_sub = sem("s_c_sub")
        s_c_exp = sem("s_c_exp")
        s_c_sum = sem("s_c_sum")
        s_c_rec = sem("s_c_rec")
        s_c_p = sem("s_c_p")
        s_c_pt = sem("s_c_pt")
        s_c_ptc = sem("s_c_ptc")
        s_c_o = sem("s_c_o")
        s_c_om = sem("s_c_om")
        s_lg_psum = sem("s_lg_psum")
        s_lg_copied = sem("s_lg_copied")
        s_mx8_ready = sem("s_mx8_ready")
        s_ix8_ready = sem("s_ix8_ready")
        s_r1 = sem("s_r1")
        s_r2 = sem("s_r2")
        s_r3 = sem("s_r3")
        s_r4 = sem("s_r4")
        s_r5 = sem("s_r5")
        s_r6 = sem("s_r6")
        s_gate_ready = sem("s_gate_ready")
        s_gt_psum = sem("s_gt_psum")
        s_gt_copied = sem("s_gt_copied")
        s_b2_psum = sem("s_b2_psum")
        s_b2_added = sem("s_b2_added")
        s_y_psum = sem("s_y_psum")

        s_x_zeroed = sem("s_x_zeroed")
        s_ld_w1 = sem("s_ld_w1")
        s_ld_w2 = sem("s_ld_w2")
        s_hot_cleared = sem("s_hot_cleared")
        s_hot_ready = sem("s_hot_ready")
        s_picked_ready = sem("s_picked_ready")
        s_rank_psum = sem("s_rank_psum")
        s_rank_copied = sem("s_rank_copied")
        s_total_copied = sem("s_total_copied")
        s_full_ready = sem("s_full_ready")
        s_tiles_ready = sem("s_tiles_ready")
        s_ahead_ready = sem("s_ahead_ready")
        s_first_ready = sem("s_first_ready")
        s_last_ready = sem("s_last_ready")
        s_past_ready = sem("s_past_ready")
        s_owner_f = sem("s_owner_f")
        s_owner_m = sem("s_owner_m")
        s_owner_ready = sem("s_owner_ready")
        s_base_ready = sem("s_base_ready")
        s_place_ready = sem("s_place_ready")
        s_slot_f = sem("s_slot_f")
        s_slot_ready = sem("s_slot_ready")
        s_xg_loaded0 = sem("s_xg_loaded0")
        s_xg_loaded1 = sem("s_xg_loaded1")
        s_scattered = sem("s_scattered")
        s_up_psum = sem("s_up_psum")
        s_hid_ready = sem("s_hid_ready")
        s_th_psum = sem("s_th_psum")
        s_hT_ready = sem("s_hT_ready")
        s_ys_ready = sem("s_ys_ready")
        s_ys_stored0 = sem("s_ys_stored0")
        s_ys_stored1 = sem("s_ys_stored1")
        s_gathered = [sem(f"s_gathered{t}") for t in range(T + 1)]
        s_summed = sem("s_summed")
        s_gates2 = sem("s_gates2")
        s_xa_turned = sem("s_xa_turned")

        ld_px = (s_ld_px0, s_ld_px1)
        kb_loaded = (s_kb_loaded0, s_kb_loaded1)
        xg_loaded = (s_xg_loaded0, s_xg_loaded1)
        ys_stored = (s_ys_stored0, s_ys_stored1)

        LN_BASE = {LN_TOK: 0, LN_ATT: 0, LN_OUTER: 2 * T + 1, LN_ONE: 2 * T + 1, LN_TWO: 4 * T + 3}

        def ln_at(n, t):
            if n == LN_TOK:
                at = 2 if is_tile(t, 0) else 2 * t + 1
            elif n == LN_ATT:
                at = 1 if is_tile(t, CLS) else 2 * T + 1 if is_tile(t, T - 1) else 2 * t + 4
            elif n == LN_OUTER:
                at = 1 if is_tile(t, CLS) else 2 * t + 3
            elif n == LN_ONE:
                at = 2 if is_tile(t, CLS) else 2 * t + 4
            else:
                at = t + 1
            return LN_BASE[n] + at

        def slot_before(n, t):
            if n in (LN_TOK, LN_TWO):
                return LN_BASE[n] if is_tile(t, 0, 1) else ln_at(n, t - 2)
            return LN_BASE[n] if is_tile(t, 0, CLS) else ln_at(n, CLS) if is_tile(t, 1) else ln_at(n, t - 2)

        def nth(t):
            return 0 if is_tile(t, CLS) else t + 1

        def xt_at(n, t):
            return {LN_TOK: 0, LN_ATT: T, LN_ONE: 2 * T + 1, LN_TWO: 3 * T + 2}[n] + \
                (t if n in (LN_TOK, LN_TWO) else nth(t)) + 1

        def turn_bank(n, u):
            return bank[5] if n == LN_TOK or u == 0 else bank[7]

        def res_at(L, t):
            return T + L * (T + 1) + (nth(t) if L == 0 else t) + 1

        def slot_of(t):
            return t % 2

        def tile_cols(t):
            return bass.ts(t, 128) if not (isinstance(t, int) and t == CLS) else slice(T * 128, T * 128 + B)

        def own_wait(eng):
            eng.sem_inc(s_own_waits, 1)

        def weights(u, r0, r1):
            return P[r0:r1, u, 0:HEADS * NP].rearrange("p (h j) -> p h j", h=HEADS)

        block = ctx.enter_context(nc.Block())

        N_CONST = 14
        N_MIX = 4

        @block.sync
        def _(sp):
            for dst, src in (
                (sinT, "sinT"), (patch_b, "patch_b"), (ident, "ident"), (identb, "identb"),
                (maskb, "maskb"), (head_mask, "head_mask"), (ln_cols, "ln_cols"), (ones, "ones"),
                (iota8, "iota8"), (tri, "tri"), (ones128, "ones128"), (steps, "steps"), (before, "before"), (tile_no, "tile_no"),
            ):
                sp.dma_start(dst[:], d[src]).then_inc(s_ld_const, 16)
            sp.dma_start(H[0:B, CLS, :], d["cls"]).then_inc(s_ld_cls, 16)
            for dst, src in ((wqkv_m, "wqkv_m"), (wo_m, "wo_m"), (VM, "vm0"), (w_patch, "w_patch")):
                sp.dma_start(dst[:], d[src]).then_inc(s_ld_mixer, 16)
            for t in range(2):
                sp.dma_start(px[:, t], d["patches"][t]).then_inc(ld_px[t], 16)
            sp.dma_start(w13[:], d["w13"]).then_inc(s_ld_up, 16)
            sp.dma_start(w2t[:], d["w2t"]).then_inc(s_ld_down, 16)
            for L in range(2):
                sp.dma_start(wqkv[L][:], d[f"wqkv{L}"]).then_inc(s_ld_attn, 16)
                sp.dma_start(wproj[L][:], d[f"wproj{L}"]).then_inc(s_ld_attn, 16)
            sp.dma_start(VB[:], d["vb0"]).then_inc(s_ld_attn, 16)
            sp.dma_start(VCB[:], d["vcb0"]).then_inc(s_ld_attn, 16)
            sp.dma_start(w_gate[:], d["w_gate"]).then_inc(s_ld_ffn, 16)
            sp.dma_start(b2[:], d["b2"]).then_inc(s_ld_ffn, 16)
            sp.wait_ge(s_kb_zero, 2)
            for k in range(3):
                sp.dma_start(x_slots[k * SLOTS // 3:(k + 1) * SLOTS // 3].rearrange("(p r) c -> p (r c)", p=128),
                             zero[:, :]).then_inc(s_x_zeroed, 16)
            with sp.Fori(0, (T - 2) // 2) as i:
                for u in range(2):
                    sp.wait_ge(s_tok_ready, 2 * i + u + 1)
                    sp.dma_start(px[:, u], d["patches"][2 * i + u + 2]).then_inc(ld_px[u], 16)
            sp.wait_ge(s_down_ready, T)
            for e in range(E):
                sp.dma_start(w2r[:, e], d["w2"][e]).then_inc(s_ld_w2, 16)
            for L in range(2):
                sp.wait_ge(s_v_copied, L * (T + 1) + 1)
                if L == 1:
                    sp.wait_ge(s_vc_slot, T)
                for h in range(HEADS):
                    sp.dma_start(VCB[h:h + 1, :, VW * h:VW * h + HD],
                                 VC[:, HD * h:HD * h + HD]).then_inc(s_vcb_loaded, 16)
                if L == 1:
                    sp.wait_ge(s_x_zeroed, 48)
                    sp.dma_start(VN[NP:S, :, :], VC[:, :]).then_inc(s_vn_loaded, 16)
                sp.wait_ge(s_kb_zero, 1)

                def spread_keys(t, u):
                    if is_tile(t, 0, 1):
                        sp.wait_ge(s_k_copied, L * (T + 1) + t + 2)
                    elif is_tile(t, 2):
                        sp.wait_ge(s_k_copied, (L + 1) * (T + 1))
                    if not is_tile(L * T + t, 0, 1):
                        sp.wait_ge(s_s_psum, L * T + t - 1)
                    for h in range(HH):
                        p0 = HD * h
                        sp.dma_start(KB[p0:p0 + HD, u, :, h, :],
                                     kT[p0:p0 + HD, :, bass.ts(t, 2), :].rearrange("p g j s -> p g (j s)")).then_inc(kb_loaded[u], 16)
                for t in range(4):
                    spread_keys(t, t % 2)
                with sp.Fori(2, T // 2) as i:
                    for u in range(2):
                        spread_keys(2 * i + u, u)
            sp.wait_ge(s_o_psum, 2 * T)
            for e in range(E):
                sp.dma_start(w1r[:, e], d["w1"][e]).then_inc(s_ld_w1, 16)
            sp.wait_ge(s_scattered, 16 * TOP * (T + 1))

            def slots_in(t, u):
                if not (isinstance(t, int) and t < 2):
                    sp.wait_ge(s_xt_psum, xt_at(LN_TWO, T) + t - 1)
                sp.dma_start(XG[:, u, :], x_slots[bass.ts(t, 128), :]).then_inc(xg_loaded[u], 16)

            slots_in(0, 0)
            slots_in(1, 1)
            with sp.Fori(0, (MT - 2) // 2) as i:
                for u in range(2):
                    slots_in(2 * i + u + 2, u)
            n_out = 0
            for t in range(T):
                sp.wait_ge(s_summed, TOP * (t + 1))
                for j in range(2):
                    sp.dma_start(d["out"][2 * t + j, 1:S, :], H[NP * j:NP * j + NP, t, :]).then_inc(s_out_done, 16)
                    n_out += 1
            sp.wait_ge(s_summed, TOP * (T + 1))
            sp.dma_start(d["out"][:, 0, :], H[0:B, CLS, :]).then_inc(s_out_done, 16)
            n_out += 1
            if dbg:
                for name, ap in (("H", H), ("U", U), ("MD", MD), ("gate", gate), ("rstd", rstd), ("kT", kT),("qT",qT)):
                    if name in dbg:
                        sp.dma_start(d["dbg_" + name], ap[:]).then_inc(s_out_done, 16)
                        n_out += 1
            sp.wait_ge(s_out_done, 16 * n_out)

        @block.tensor
        def _(pe):
            def both_halves(out, lhs, rhs, bias=True, start=True, stop=True):
                k = HC + 1 if bias else HC
                pe.matmul(out, lhs(0)[0:HC], rhs(0)[0:HC], start=start, stop=False)
                return pe.matmul(out, lhs(1)[0:k], rhs(1)[0:k], start=False, stop=stop)

            pe.wait_ge(s_ld_const, 16 * N_CONST)
            pe.wait_ge(s_ld_mixer, 16 * N_MIX)
            for h in range(HEADS):
                mm = both_halves(bank[h // HH][0:HD, NP * (h % HH):NP * (h % HH) + NP],
                                 lambda g: wqkv_m[:, g, HD * h:HD * h + HD], lambda g: sinT[:, g, 0, :])
            mm.then_inc(s_m_q, 1)
            both_halves(bank[2][0:HD, 0:NP], lambda g: wqkv_m[:, g, C:C + HD], lambda g: sinT[:, g, 0, :])
            both_halves(bank[2][:, NP:NP + HD], lambda g: sinT[:, g].rearrange("p a b -> p (a b)"),
                        lambda g: wqkv_m[:, g, C + HD:C + 2 * HD]).then_inc(s_m_k, 1)
            pe.wait_ge(s_m_qc, 4)
            for g in range(2):
                pe.matmul(bank[3 + g][0:NP, 0:HH * NP], identb[0:NP, 0:NP], maskb[0:NP, :, 0:NP],
                          start=True, stop=False)
                for j in range(HH):
                    mm = pe.matmul(bank[3 + g][0:NP, NP * j:NP * j + NP], qm[:, HH * g + j, :], km[:, :],
                                   start=False, stop=(j == HH - 1))
            mm.then_inc(s_m_s, 1)

            def tok(t, u):
                pe.wait_ge(ld_px[u], 8 * (t - u) + 16)
                if not (isinstance(t, int) and t == 0):
                    pe.wait_ge(s_z_ready, t)
                for k in range(KP):
                    mm = pe.matmul(bank[7][:, 0:C], px[:, u, k, :], w_patch[:, k, :],
                                   start=(k == 0), stop=(k == KP - 1))
                mm.then_inc(s_tok_ready, 1)
            tok(0, 0)

            pe.wait_ge(s_m_exp, 1)
            for p in range(PAIRS):
                mm = pe.transpose(bank[5][:, NP * p:NP * p + NP], P[0:NP, 0, 2 * NP * p:2 * NP * (p + 1)], ident[0:NP, 0:NP])
            mm.then_inc(s_m_t, 1)
            pe.wait_ge(s_m_tc, 1)
            for p in range(PAIRS):
                mm = pe.matmul(bank[6][0:NP, 2 * VW * p:2 * VW * p + 2 * VW], PT[:, 0, p, 0:NP], VM[:, :, :],
                               start=True, stop=True)
            mm.then_inc(s_m_o, 1)
            pe.wait_ge(s_m_norm, 1)
            for g in range(2):
                mm = pe.transpose(bank[5][0:HC, NP * g:NP * g + NP], ON[:, 0, 0, HC * g:HC * g + HC], ident[0:NP, 0:NP])
            mm.then_inc(s_m_ot, 1)
            pe.wait_ge(s_m_otc, 1)
            pe.wait_ge(s_presets, 4)
            both_halves(bank[6][:, 0:C], lambda g: OT[:, 0, g, :], lambda g: wo_m[:, g, :], stop=False)
            pe.matmul(bank[6][:, 0:C], ones[:, :], patch_b[:, :], start=False, stop=True).then_inc(s_m_md, 1)

            def turn(n, t, u):
                r = rows_of(t)
                pe.wait_ge(s_xn_ready, xt_at(n, t))
                if n == LN_TOK:
                    if not is_tile(t, 0):
                        pe.wait_ge(s_xt_ready, xt_at(n, t) - 1)
                elif is_tile(t, 0 if n == LN_TWO else CLS):
                    pe.wait_ge(s_xt_ready, xt_at(n, t) - 1)
                else:
                    pe.wait_ge(s_xt_ready, xt_at(n, t) - 2)
                for g in range(2):
                    x = XA[0:r, t] if n == LN_TWO else XN[0:r, u]
                    mm = pe.transpose(turn_bank(n, u)[0:HC, 128 * g:128 * g + r], x[:, HC * g:HC * g + HC], ident[0:r, 0:r])
                mm.then_inc(s_xt_psum, 1)

            def mixer(t, u):
                last = isinstance(t, int) and t == T - 1
                if not last:
                    tok(t + 1, 1 - u)
                pe.wait_ge(s_xt_ready, xt_at(LN_TOK, t))
                if not (isinstance(t, int) and t == 0):
                    pe.wait_ge(s_silu_ready, t)
                else:
                    pe.wait_ge(s_m_norm, 1)
                    pe.wait_ge(s_ld_up, 16)
                for w, done in ((0, s_up1), (1, s_up3)):
                    if w == 1 and not (isinstance(t, int) and t == 0):
                        pe.wait_ge(s_g_ready, t)
                    for m in range(KP):
                        mm = both_halves(bank[2 * w + m // 4][:, 128 * (m % 4):128 * (m % 4) + 128],
                                         lambda g: w13[:, g, HID * w + 128 * m:HID * w + 128 * m + 128],
                                         lambda g: XT[:, u, g, :], bias=False)
                    mm.then_inc(done, 1)
                if not last:
                    turn(LN_TOK, t + 1, 1 - u)
                pe.wait_ge(s_g_ready, t + 1)
                if not (isinstance(t, int) and t == 0):
                    pe.wait_ge(s_res_ready, t)
                else:
                    pe.wait_ge(s_ld_down, 16)
                for k in range(KP):
                    mm = pe.matmul(bank[6][:, 0:C], gT[:, u, k, :], w2t[:, k, :], start=(k == 0), stop=(k == KP - 1))
                mm.then_inc(s_down_ready, 1)

            turn(LN_TOK, 0, 0)
            in_pairs(pe, mixer)

            for L, n in ((0, LN_ATT), (1, LN_ONE)):
                base = L * (T + 1)

                def qkv(t, u):
                    cls = is_tile(t, CLS)
                    i = nth(t)
                    if not is_tile(t, T - 1):
                        turn(n, 0 if cls else t + 1, 1 - u)
                    r = rows_of(t)
                    qb, kb, vb = bank[u], bank[2 + u], bank[4 + 2 * u]
                    pe.wait_ge(s_xt_ready, xt_at(n, t))
                    if not is_tile(base + i, 0, 1):
                        pe.wait_ge(s_q_copied, base + i - 1)
                        pe.wait_ge(s_k_copied, base + i - 1)
                    for m in range(4):
                        mm = both_halves((qb, kb)[m // 2][0:HC, 128 * (m % 2):128 * (m % 2) + r], lambda g: wqkv[L][:, g, HC * m:HC * m + HC],
                                         lambda g: XT[:, u, g, 0:r])
                    mm.then_inc(s_qk_psum, 1)
                    if not is_tile(base + i, 0, 1):
                        pe.wait_ge(s_v_copied, base + i - 1)
                    if cls:
                        if L == 0:
                            for m in range(2):
                                both_halves(vb[0:HC, 256 + B * m:256 + B * m + B],
                                            lambda g: wqkv[L][:, g, 2 * C + HC * m:2 * C + HC * m + HC],
                                            lambda g: XT[:, u, g, 0:B])
                        mm = both_halves(vb[0:B, 0:C], lambda g: XT[:, u, g, 0:B], lambda g: wqkv[L][:, g, 2 * C:3 * C])
                    else:
                        both_halves(vb[:, 0:C], lambda g: XT[:, u, g, :], lambda g: wqkv[L][:, g, 2 * C:3 * C])

                        def by_head(ap, a):
                            return ap.rearrange("p (m a d) -> p m a d", m=PAIRS, a=2)[:, :, a, :]
                        both_halves(by_head(vb[NP:128, C:2 * C], 1), lambda g: XT[:, u, g, 0:NP],
                                    lambda g: by_head(wqkv[L][:, g, 2 * C:3 * C], 1))
                        if L == 0:
                            mm = both_halves(by_head(vb[0:NP, C:2 * C], 0), lambda g: XT[:, u, g, NP:128],
                                             lambda g: by_head(wqkv[L][:, g, 2 * C:3 * C], 0))
                        else:
                            mm = both_halves(vb[0:NP, C:2 * C], lambda g: XT[:, u, g, NP:128],
                                             lambda g: wqkv[L][:, g, 2 * C:3 * C])
                    mm.then_inc(s_v_psum, 1)

                if L == 0:
                    pe.wait_ge(s_ld_attn, 16 * 6)
                pe.wait_ge(s_res_ready, T + L * (T + 1))
                turn(n, CLS, 0)
                qkv(CLS, 0)
                in_pairs(pe, lambda t, u: qkv(t, 1 - u))

                def scores(t, u):
                    pe.wait_ge(s_q_slot, L * T + t + 1)
                    pe.wait_ge(kb_loaded[u], 16 * HH * (L * T // 2 + 1) + 8 * HH * (t - u))
                    if is_tile(t, 0):
                        pe.wait_ge(s_q_copied, base + T + 1)
                        pe.wait_ge(s_k_copied, base + T + 1)
                    elif not is_tile(t, 1):
                        pe.wait_ge(s_sub_ready, L * T + t - 1)
                    for g in range(2):
                        sc = bank[2 * u + g]
                        for j in range(2):
                            if L == 0:
                                pe.matmul(sc[NP * j:NP * j + NP, 0:HH * S], identb[:, NP * j:NP * j + NP],
                                          maskb[:, :, :], start=True, stop=False)
                            mm = pe.matmul(sc[NP * j:NP * j + NP, 0:HH * S], qs[:, u, g, NP * j:NP * j + NP],
                                           KB[:, u, g, :, S * j:S * j + S], start=(L == 1), stop=True)
                    mm.then_inc(s_s_psum, 1)

                def attend(t, u):
                    first = is_tile(t, 0)
                    pe.wait_ge(s_exp_ready, L * T + t + 1)
                    if first:
                        pe.wait_ge(s_v_copied, base + T + 1)
                    else:
                        pe.wait_ge(s_pta_copied, L * T + t)
                        pe.wait_ge(s_ptb_copied, L * T + t)
                    for p in range(PAIRS):
                        pe.transpose(bank[4 + p // 4][:, 128 * (p % 4):128 * (p % 4) + 128],
                                     P[:, u, 2 * NP * p:2 * NP * (p + 1)], ident[:, :])
                    pe.transpose(bank[5][0:HEADS, 256:384], P[:, u, HEADS * NP:], ident[:, :]).then_inc(s_pt_psum, 1)
                    if not first:
                        out_turn(t - 1, 1 - u)
                    if not is_tile(t, T - 2, T - 1):
                        scores(t + 2, u)
                    if not first:
                        project(t - 1, 1 - u)
                    pe.wait_ge(s_pta_copied, L * T + t + 1)
                    pe.wait_ge(s_ptb_copied, L * T + t + 1)
                    pe.wait_ge(s_vc_slot, L * T + t + 1)
                    for j in range(2):
                        o = bank[6][0:NP, HEADS * VW * j:HEADS * VW * (j + 1)]
                        pe.matmul(o, PT[0:HEADS, u, PAIRS, NP * j:NP * j + NP],
                                  vcs[:, u, j, :], start=True, stop=False)
                        for p in range(PAIRS):
                            mm = pe.matmul(o[:, 2 * VW * p:2 * VW * p + 2 * VW], PT[:, u, p, NP * j:NP * j + NP],
                                           VB[:, 2 * t + j, p].rearrange("p a b -> p (a b)"), start=False, stop=(p == PAIRS - 1))
                    mm.then_inc(s_o_psum, 1)

                def out_turn(t, u):
                    pe.wait_ge(s_on_ready, L * T + t + 1)
                    pe.wait_ge(s_res_ready, res_at(L, t) - 1)
                    own_wait(pe)
                    for g in range(2):
                        for j in range(2):
                            mm = pe.transpose(bank[7][0:HC, 128 * g + NP * j:128 * g + NP * j + NP],
                                              ON[:, u, j, HC * g:HC * g + HC], ident[0:NP, 0:NP])
                    mm.then_inc(s_ot_psum, 1)

                def project(t, u):
                    pe.wait_ge(s_ot_copied, L * T + t + 1)
                    both_halves(bank[7][:, 256:256 + C], lambda g: OT[:, u, g, :], lambda g: wproj[L][:, g, :]).then_inc(s_proj_psum, 1)

                def project_cls():
                    pe.wait_ge(s_cls_otc, L + 1)
                    both_halves(bank[7][0:B, 256:256 + C], lambda g: OTc[:, g, :], lambda g: wproj[L][:, g, :]).then_inc(s_proj_psum, 1)

                scores(0, 0)
                scores(1, 1)
                pe.wait_ge(s_xt_ready, xt_at(n, T - 1))
                if L == 0:
                    project_cls()
                in_pairs(pe, attend, tail=3)
                out_turn(T - 1, 1)
                project(T - 1, 1)

                if L == 1:
                    pe.wait_ge(s_c_qcb, 2)
                    pe.wait_ge(s_sub_ready, 2 * T)
                    pe.wait_ge(s_ptb_copied, 2 * T)
                    pe.wait_ge(s_pta_copied, 2 * T)
                    for b in range(B):
                        mm = both_halves(bank[2 + b // 7][0:HEADS, S * (b % 7):S * (b % 7) + S],
                                         lambda g: QCB[:, g, b, :], lambda g: kT[:, g, b, :], bias=False)
                    mm.then_inc(s_c_s, 1)
                    pe.wait_ge(s_c_p, 1)
                    for b in range(B):
                        mm = pe.transpose(bank[5][0:S, HEADS * b:HEADS * b + HEADS], Pc[:, b, :], ident[0:HEADS, 0:HEADS])
                    mm.then_inc(s_c_pt, 1)
                    pe.wait_ge(s_c_ptc, 1)
                    pe.wait_ge(s_vn_loaded, 16)
                    pe.wait_ge(s_vn_copied, T)
                    pe.wait_ge(s_on_ready, 2 * T)
                    for g in range(2):
                        for b in range(B):
                            c0 = (g * B + b) * HEADS
                            mm = pe.matmul(bank[6][0:HC, c0:c0 + HEADS], VN[:, b, HC * g:HC * g + HC], PcT[:, b, :],
                                           start=True, stop=True)
                    mm.then_inc(s_c_o, 1)
                    pe.wait_ge(s_res_ready, res_at(L, T - 1))
                    project_cls()

            pe.wait_ge(s_ld_ffn, 32)

            def route(t, u):
                if t < T:
                    turn(LN_TWO, t + 1, 1 - u)
                r = rows_of(t)
                pe.wait_ge(s_xt_ready, xt_at(LN_TWO, t))
                both_halves(bank[0][0:r, E * t:E * t + E], lambda g: XT[:, u, g, 0:r], lambda g: w_gate[:, g, :], bias=False)\
                    .then_inc(s_lg_psum, 1)

            pe.wait_ge(s_res_ready, res_at(1, CLS))
            turn(LN_TWO, 0, 0)
            for t in range(T + 1):
                route(t, t % 2)

            pe.wait_ge(s_picked_ready, 1)
            pe.wait_ge(s_lg_copied, 2)
            pe.matmul(bank[0][:, 0:(T + 1) * E], tri[:, :], picked[:, :, :],
                      start=True, stop=False)
            for t in range(T):
                pe.matmul(bank[0][:, (t + 1) * E:(T + 1) * E], ones128[:, :], bcast(picked[:, t, :], 1, T - t),
                          start=False, stop=(t == T - 1))
            pe.matmul(bank[1][:, 0:(T + 1) * E], ones128[:, :], picked[:, :, :], start=True, stop=True).then_inc(s_rank_psum, 1)

            def bias_out(t, u):
                r = rows_of(t)
                if t == 0:
                    pe.wait_ge(s_gate_ready, 1)
                    pe.wait_ge(s_cls_otc, 2)
                else:
                    pe.wait_ge(s_b2_added, t)
                pe.transpose(bank[6][0:E, 0:r], gate[0:r, t, :], ident[0:r, 0:r]).then_inc(s_gt_psum, 1)
                pe.wait_ge(s_gt_copied, t + 1)
                pe.matmul(bank[7][0:r, 0:C], gateT[:, u, 0:r], b2[:, :], start=True, stop=True).then_inc(s_b2_psum, 1)

            for t in range(T + 1):
                bias_out(t, t % 2)

            def turn_slots(t, u):
                pe.wait_ge(xg_loaded[u], 8 * (t - u) + 16)
                pe.wait_ge(s_xt_ready, xt_at(LN_TWO, T) + t)
                for g in range(2):
                    mm = pe.transpose(bank[5][0:HC, 128 * g:128 * g + 128], XG[:, u, HC * g:HC * g + HC], ident[:, :])
                mm.then_inc(s_xt_psum, 1)

            def expert_of(t):
                return pe.value_load(owner[0:1, bass.ds(t, 1)], min_val=0, max_val=E - 1)

            def up(t, u):
                e = expert_of(t)
                pe.wait_ge(s_xt_ready, xt_at(LN_TWO, T) + t + 1)
                if isinstance(t, int) and t == 0:
                    pe.wait_ge(s_rank_copied, 1)
                    pe.wait_ge(s_total_copied, 1)
                else:
                    pe.wait_ge(s_hid_ready, t)
                for n in range(2):
                    mm = both_halves(bank[n][:, 0:HID // 2], lambda g: XT[:, u, g, :],
                                     lambda g: w1r[:, bass.ds(e, 1), g, n * HID // 2:(n + 1) * HID // 2])
                mm.then_inc(s_up_psum, 1)

            def turn_hidden(t, u):
                pe.wait_ge(s_hid_ready, t + 1)
                if not (isinstance(t, int) and t == 0):
                    pe.wait_ge(s_hT_ready, t)
                for m in range(KP):
                    mm = pe.transpose(bank[2 + m // 4][:, 128 * (m % 4):128 * (m % 4) + 128], hid[:, u, 128 * m:128 * m + 128], ident[:, :])
                mm.then_inc(s_th_psum, 1)

            def down(t, u):
                e = expert_of(t)
                pe.wait_ge(s_hT_ready, t + 1)
                if not (isinstance(t, int) and t == 0):
                    pe.wait_ge(s_ys_ready, t)
                for m in range(KP):
                    mm = pe.matmul(bank[4][:, 0:C], hT[:, u, m, :], w2r[:, bass.ds(e, 1), m, :], start=(m == 0), stop=(m == KP - 1))
                mm.then_inc(s_y_psum, 1)

            def expert(t, u):
                first = isinstance(t, int) and t == 0
                if not first:
                    turn_hidden(t - 1, 1 - u)
                up(t, u)
                if not (isinstance(t, int) and t == MT - 1):
                    turn_slots(t + 1, 1 - u)
                if not first:
                    down(t - 1, 1 - u)

            pe.wait_ge(s_owner_ready, 1)
            pe.wait_ge(s_ld_w1, 16 * E)
            pe.wait_ge(s_ld_w2, 16 * E)
            turn_slots(0, 0)
            in_pairs(pe, expert, MT)
            turn_hidden(MT - 1, (MT - 1) % 2)
            down(MT - 1, (MT - 1) % 2)

        @block.vector
        def _(dve):
            def stats(n, t, s, src):
                r = rows_of(t)
                at = ln_at(n, t)
                own_wait(dve)
                dve.bn_stats(stat[0:r, 0, :], src).then_inc(s_stat_ready, 1)
                if not is_tile(slot_before(n, t), 0):
                    dve.wait_ge(s_veps_ready, slot_before(n, t))
                dve.wait_ge(s_stat_ready, at)
                own_wait(dve)
                dve.bn_aggr(mvs[0:r, s, :], stat[0:r, 0, :]).then_inc(s_mv_ready, 1)
                dve.wait_ge(s_mv_ready, at)
                dve.tensor_copy(mean[0:r, n, t], mvs[0:r, s, 0:1]).then_inc(s_mean_ready, 1)
                dve.wait_ge(s_mean_ready, at)

            def normed(n, t, out, src):
                r = rows_of(t)
                dve.wait_ge(s_rstd_ready, ln_at(n, t))
                return dve.tensor_scalar(out, src, mean[0:r, n, t], rstd[0:r, n, t], ALU.subtract, ALU.mult)

            def to_slot(n, t, u, src):
                at = xt_at(n, t)
                if not (n == LN_TOK and is_tile(t, 0, 1)):
                    dve.wait_ge(s_xt_psum, at - 2)
                normed(n, t, XN[0:rows_of(t), u, :], src).then_inc(s_xn_ready, 1)

            dve.wait_ge(s_m_q, 1)
            dve.tensor_copy(qm[:, 0:HH, :], bank[0][0:HD, 0:HH * NP]).then_inc(s_m_qc, 1)
            dve.tensor_copy(qm[:, HH:HEADS, :], bank[1][0:HD, 0:HH * NP]).then_inc(s_m_qc, 1)
            dve.wait_ge(s_m_k, 1)
            dve.tensor_copy(km[:, :], bank[2][0:HD, 0:NP]).then_inc(s_m_qc, 1)
            dve.tensor_copy(VM[0:NP, 0, 0:HD], bank[2][0:NP, NP:NP + HD])
            dve.tensor_copy(VM[NP:128, 1, 0:HD], bank[2][NP:128, NP:NP + HD]).then_inc(s_m_qc, 1)
            dve.wait_ge(s_m_s, 1)
            for g in range(2):
                dve.reduce_max(mx[0:NP, 0, HH * g:HH * g + HH], bank[3 + g][0:NP, 0:HH * NP].rearrange("p (h j) -> p h j", h=HH),
                               AX_X).then_inc(s_m_max, 1)
            dve.wait_ge(s_m_max, 2)
            for g in range(2):
                dve.tensor_tensor(weights(0, 0, NP)[:, HH * g:HH * g + HH, :], bank[3 + g][0:NP, 0:HH * NP].rearrange("p (h j) -> p h j", h=HH),
                                  bcast(mx[0:NP, 0, HH * g:HH * g + HH], 2, NP), ALU.subtract).then_inc(s_m_sub, 1)
            dve.wait_ge(s_m_t, 1)
            dve.tensor_copy(PT[:, 0, 0:PAIRS, 0:NP], bank[5][:, 0:PAIRS * NP].rearrange("p (a b) -> p a b", a=PAIRS)).then_inc(s_m_tc, 1)
            dve.wait_ge(s_m_o, 1)
            o = bank[6][0:NP, 0:HEADS * VW].rearrange("p (h v) -> p h v", h=HEADS)
            dve.reciprocal(rec[:, 0, 0:HEADS], o[:, :, HD]).then_inc(s_m_rec, 1)
            dve.wait_ge(s_m_rec, 1)
            dve.tensor_tensor(ON[:, 0, 0].rearrange("p (h v) -> p h v", h=HEADS), o[:, :, 0:HD],
                              bcast(rec[:, 0, 0:HEADS], 2, HD), ALU.mult).then_inc(s_m_norm, 1)
            dve.wait_ge(s_m_ot, 1)
            dve.tensor_copy(OT[0:HC, 0].rearrange("p g (a b) -> p g a b", a=2),
                            bcast(bank[5][0:HC, 0:2 * NP].rearrange("p (g b) -> p g b", g=2), 2, 2)).then_inc(s_m_otc, 1)
            dve.wait_ge(s_m_md, 1)
            dve.tensor_copy(MD[:, :], bank[6][:, 0:C]).then_inc(s_m_mdc, 1)
            dve.wait_ge(s_m_mdc, 1)

            def z_of(t, u):
                dve.wait_ge(s_tok_ready, t + 1)
                dve.tensor_tensor(H[:, t, :], bank[7][:, 0:C], MD[:, :], ALU.add).then_inc(s_z_ready, 1)
                dve.wait_ge(s_z_ready, t + 1)
                stats(LN_TOK, t, u, H[:, t, :])
                to_slot(LN_TOK, t, u, H[:, t, :])

            def mixer(t, u):
                if not (isinstance(t, int) and t == T - 1):
                    z_of(t + 1, 1 - u)
                dve.wait_ge(s_silu_ready, t + 1)
                dve.wait_ge(s_up3, t + 1)
                if not (isinstance(t, int) and t < 2):
                    dve.wait_ge(s_down_ready, t - 1)
                dve.tensor_tensor(gT[:, u, 0:4, :], bank[2][:, :], silu[:, u, 0:4, :], ALU.mult)
                dve.tensor_tensor(gT[:, u, 4:6, :], bank[3][:, 0:256], silu[:, u, 4:6, :], ALU.mult).then_inc(s_g_ready, 1)
                dve.wait_ge(s_down_ready, t + 1)
                dve.tensor_tensor(H[:, t, :], bank[6][:, 0:C], H[:, t, :], ALU.add).then_inc(s_res_ready, 1)
                dve.wait_ge(s_res_ready, t + 1)
                stats(LN_ATT, t, 3 - u, H[:, t, :])

            dve.wait_ge(s_ld_cls, 16)
            stats(LN_ATT, CLS, 2, H[0:B, CLS, :])
            z_of(0, 0)
            in_pairs(dve, mixer)

            for L, n in ((0, LN_ATT), (1, LN_ONE)):
                base = L * (T + 1)
                X = H if L == 0 else U

                def qkv(t, u):
                    cls = is_tile(t, CLS)
                    at = base + nth(t) + 1
                    if not is_tile(t, T - 1):
                        nxt = 0 if cls else t + 1
                        to_slot(n, nxt, 1 - u, X[0:rows_of(nxt), nxt, :])
                    r = rows_of(t)
                    qb, vb = bank[u], bank[4 + 2 * u]
                    dve.wait_ge(s_qk_psum, at)
                    if cls and L == 1:
                        dve.wait_ge(s_q_slot, T)
                    dve.tensor_copy(qT[:, :, tile_cols(t)], qb[0:HC, 0:256].rearrange("p (a b) -> p a b", a=2)[:, :, 0:r])\
                        .then_inc(s_q_copied, 1)
                    dve.wait_ge(s_v_psum, at)
                    if cls:
                        if L == 0:
                            dve.wait_ge(s_ld_attn, 16 * 6)
                            dve.tensor_copy(OTc[0:HC, :, :], vb[0:HC, 256:256 + 2 * B].rearrange("p (a b) -> p a b", a=2))\
                                .then_inc(s_cls_otc, 1)
                        else:
                            dve.wait_ge(s_o_psum, T)
                            dve.wait_ge(s_vcb_loaded, 16 * HEADS)
                            dve.wait_ge(s_x_zeroed, 48)
                        dve.tensor_copy(VC[:, :], vb[0:B, 0:C]).then_inc(s_v_copied, 1)
                    else:
                        v = vb[:, 0:2 * C].rearrange("p (j m a d) -> p j m a d", j=2, m=PAIRS, a=2)
                        dve.tensor_copy(VB[0:NP, bass.ts(t, 2), :, 0, 0:HD], v[0:NP, :, :, 0, :])
                        for j in range(2):
                            mm = dve.tensor_copy(VB[NP:128, 2 * t + j, :, 1, 0:HD], v[NP:128, 1 - j, :, 1, :])
                        if L == 1:
                            dve.tensor_copy(VN[0:NP, bass.ts(t, 2), :], vb[0:NP, 0:2 * C]).then_inc(s_vn_copied, 1)
                            dve.wait_ge(s_vn_copied, t + 1)
                            dve.sem_inc(s_v_copied, 1)
                        else:
                            mm.then_inc(s_v_copied, 1)

                to_slot(n, CLS, 0, X[0:B, CLS, :])
                qkv(CLS, 0)
                in_pairs(dve, lambda t, u: qkv(t, 1 - u), tail=3)

                def shifted(t, u):
                    dve.wait_ge(s_s_psum, L * T + t + 1)
                    for g in range(2):
                        mm = dve.reduce_max(mx[:, u, HH * g:HH * g + HH], bank[2 * u + g][:, 0:HH * S].rearrange("p (h j) -> p h j", h=HH), AX_X)
                    mm.then_inc(s_max_ready, 1)
                    dve.wait_ge(s_max_ready, L * T + t + 1)
                    if not is_tile(L * T + t, 0, 1):
                        dve.wait_ge(s_pt_psum, L * T + t - 1)
                    for g in range(2):
                        sc = bank[2 * u + g][:, 0:HH * S].rearrange("p (h j) -> p h j", h=HH)
                        m = mx[:, u, HH * g:HH * g + HH]
                        dve.tensor_tensor(weights(u, 0, 128)[:, HH * g:HH * g + HH, :], sc[:, :, 0:NP], bcast(m, 2, NP), ALU.subtract)
                        c0 = HEADS * NP + HH * g
                        mm = dve.tensor_tensor(P[:, u, c0:c0 + HH], sc[:, :, NP], m, ALU.subtract)
                    mm.then_inc(s_sub_ready, 1)

                def residual(t, u):
                    r = rows_of(t)
                    dve.wait_ge(s_proj_psum, res_at(L, t) - T)
                    dve.tensor_tensor(X[0:r, t, :], bank[7][0:r, 256:256 + C], X[0:r, t, :], ALU.add).then_inc(s_res_ready, 1)
                    dve.wait_ge(s_res_ready, res_at(L, t))
                    stats(LN_OUTER if L == 0 else LN_TWO, t, u, X[0:r, t, :])

                def outer(t, u):
                    r = rows_of(t)
                    normed(LN_OUTER, t, U[0:r, t, :], H[0:r, t, :]).then_inc(s_z_ready, 1)
                    dve.wait_ge(s_z_ready, T + nth(t) + 1)
                    stats(LN_ONE, t, 2 + u, U[0:r, t, :])

                def attend(t, u):
                    first = is_tile(t, 0)
                    dve.wait_ge(s_pt_psum, L * T + t + 1)
                    if not is_tile(L * T + t, 0, 1):
                        dve.wait_ge(s_o_psum, L * T + t - 1)
                    dve.tensor_copy(PT[:, u, 4:6, :], bank[5][:, 0:256])
                    dve.tensor_copy(PT[0:HEADS, u, 6, :], bank[5][0:HEADS, 256:384]).then_inc(s_ptb_copied, 1)
                    if not is_tile(t, T - 1):
                        shifted(t + 1, 1 - u)
                    if L == 0 and first:
                        outer(CLS, 0)
                    elif L == 0 and not is_tile(t, 1):
                        outer(t - 2, 1 - u)
                    if not first:
                        residual(t - 1, u if L == 0 else 1 - u)
                    dve.wait_ge(s_o_psum, L * T + t + 1)
                    o = bank[6][0:NP, 0:2 * HEADS * VW].rearrange("p (h v) -> p h v", v=VW)
                    dve.reciprocal(rec[:, u, :], o[:, :, HD]).then_inc(s_rec_ready, 1)
                    dve.wait_ge(s_rec_ready, L * T + t + 1)
                    dve.tensor_tensor(ON[:, u].rearrange("p j (h v) -> p (j h) v", v=HD), o[:, :, 0:HD],
                                      bcast(rec[:, u, :], 2, HD), ALU.mult).then_inc(s_on_ready, 1)

                shifted(0, 0)
                if L == 0:
                    residual(CLS, 0)
                attend(0, 0)
                attend(1, 1)
                with dve.Fori(1, (T - 2) // 2) as i:
                    for u in range(2):
                        attend(2 * i + u, u)
                for t in range(T - 2, T):
                    attend(t, t % 2)
                if L == 0:
                    outer(T - 2, 1)
                residual(T - 1, 0 if L == 0 else 1)
                if L == 0:
                    outer(T - 1, 0)
                if L == 1:
                    dve.wait_ge(s_c_s, 1)
                    spans = ((0, 7), (7, 14), (14, 16))
                    sc = [bank[2 + i][0:HEADS, 0:S * (b1 - b0)].rearrange("p (b j) -> p b j", j=S) for i, (b0, b1) in enumerate(spans)]
                    for i, (b0, b1) in enumerate(spans):
                        dve.reduce_max(mxc[:, b0:b1], sc[i], AX_X).then_inc(s_c_max, 1)
                    dve.wait_ge(s_c_max, 3)
                    for i, (b0, b1) in enumerate(spans):
                        dve.tensor_tensor(Pc[:, b0:b1, :], sc[i], bcast(mxc[:, b0:b1], 2, S), ALU.subtract).then_inc(s_c_sub, 1)
                    dve.wait_ge(s_c_exp, 1)
                    dve.reduce_sum(smc[:, :], Pc[:, :, :], AX_X).then_inc(s_c_sum, 1)
                    dve.wait_ge(s_c_sum, 1)
                    dve.reciprocal(mxc[:, :], smc[:, :]).then_inc(s_c_rec, 1)
                    dve.wait_ge(s_c_rec, 1)
                    dve.tensor_tensor(Pc[:, :, :], Pc[:, :, :], bcast(mxc[:, :], 2, S), ALU.mult).then_inc(s_c_p, 1)
                    dve.wait_ge(s_c_pt, 1)
                    dve.tensor_copy(PcT[:, :, :], bank[5][0:S, 0:B * HEADS]).then_inc(s_c_ptc, 1)
                    dve.wait_ge(s_c_o, 1)
                    for g in range(2):
                        dve.tensor_tensor(OCm[:, g], bank[6][0:HC, g * B * HEADS:(g + 1) * B * HEADS].rearrange("p (b h) -> p b h", b=B),
                                          bcast(head_mask[:, g, :], 1, B), ALU.mult).then_inc(s_c_om, 1)
                    dve.wait_ge(s_c_om, 2)
                    dve.reduce_sum(OTc[0:HC, :, :], OCm[:, :, :, :], AX_X).then_inc(s_cls_otc, 1)
                    residual(CLS, 0)

            def best(t):
                r = rows_of(t)
                dve.max(mx8[0:r, t, :], lg[0:r, t, :]).then_inc(s_mx8_ready, 1)
                dve.wait_ge(s_mx8_ready, t + 1)
                dve.max_index(ix8[0:r, t, :], mx8[0:r, t, :], lg[0:r, t, :]).then_inc(s_ix8_ready, 1)

            def router_norm(t):
                r = rows_of(t)
                normed(LN_TWO, t, XA[0:r, t, :], U[0:r, t, :]).then_inc(s_xn_ready, 1)
            for t in range(T + 1):
                router_norm(t)
            dve.wait_ge(s_lg_psum, T + 1)
            dve.tensor_copy(lg[:, 0:T, :], bank[0][:, 0:T * E]).then_inc(s_lg_copied, 1)
            dve.tensor_copy(lg[0:B, T, :], bank[0][0:B, T * E:(T + 1) * E]).then_inc(s_lg_copied, 1)
            dve.wait_ge(s_lg_copied, 2)
            for t in range(T + 1):
                best(t)
            dve.wait_ge(s_ix8_ready, T + 1)
            dve.wait_ge(s_hot_cleared, 3)
            for k, (r, ts) in enumerate(((128, slice(0, T)), (B, slice(T, T + 1)))):
                nt = T if k == 0 else 1
                dve.tensor_copy(ixf[0:r, ts, :], ix8[0:r, ts, 0:TOP]).then_inc(s_r1, 1)
                dve.tensor_tensor(e2[0:r, ts, :], mx8[0:r, ts, 1:2], mx8[0:r, ts, 0:1], ALU.subtract).then_inc(s_r2, 1)
                dve.wait_ge(s_r1, k + 1)
                for j in range(TOP):
                    dve.tensor_tensor(hot[0:r, j, ts, :], bcast(iota8[0:r, :], 1, nt), ixf[0:r, ts, j:j + 1].to_broadcast([r, nt, E]),
                                      ALU.is_equal).then_inc(s_hot_ready, 1)
            dve.wait_ge(s_hot_ready, 2 * TOP)
            dve.tensor_tensor(picked[:, :, :], hot[:, 0], hot[:, 1], ALU.add).then_inc(s_picked_ready, 1)
            for k, (r, ts) in enumerate(((128, slice(0, T)), (B, slice(T, T + 1)))):
                nt = T if k == 0 else 1
                dve.wait_ge(s_r3, k + 1)
                dve.tensor_scalar(g12[0:r, ts, 0:1], e2[0:r, ts, :], 1.0, None, ALU.add).then_inc(s_r4, 1)
                dve.wait_ge(s_r4, k + 1)
                dve.reciprocal(g12[0:r, ts, 0:1], g12[0:r, ts, 0:1]).then_inc(s_r5, 1)
                dve.wait_ge(s_r5, k + 1)
                dve.tensor_tensor(g12[0:r, ts, 1:2], e2[0:r, ts, :], g12[0:r, ts, 0:1], ALU.mult).then_inc(s_r6, 1)
                dve.wait_ge(s_r6, k + 1)
                for j, out in enumerate((gate, gate2)):
                    dve.tensor_tensor(out[0:r, ts, :], hot[0:r, j, ts, :], g12[0:r, ts, j:j + 1].to_broadcast([r, nt, E]),
                                      ALU.mult).then_inc(s_gates2, 1)
                dve.wait_ge(s_gates2, 2 * k + 2)
                dve.tensor_tensor(gate[0:r, ts, :], gate[0:r, ts, :], gate2[0:r, ts, :], ALU.add).then_inc(s_base_ready, 1)
            dve.wait_ge(s_rank_psum, 1)
            dve.tensor_copy(rank[:, :, :], bank[0][:, 0:(T + 1) * E]).then_inc(s_rank_copied, 1)
            dve.reduce_sum(total[:, :], bank[1][:, 0:(T + 1) * E].rearrange("p (t e) -> p e t", e=E), AX_X).then_inc(s_total_copied, 1)
            dve.wait_ge(s_total_copied, 1)
            dve.tensor_tensor(full[:, :, :], bcast(total[:, :], 2, T + 2), bcast(steps[:, :], 1, E), ALU.is_gt).then_inc(s_full_ready, 1)
            dve.wait_ge(s_full_ready, 1)
            dve.reduce_sum(tiles[:, :], full[:, :, :], AX_X).then_inc(s_tiles_ready, 1)
            dve.wait_ge(s_tiles_ready, 1)
            dve.tensor_tensor(ahead[:, :, :], before[:, :, :], bcast(tiles[:, :], 1, E), ALU.mult).then_inc(s_ahead_ready, 1)
            dve.wait_ge(s_ahead_ready, 1)
            dve.reduce_sum(first[:, :], ahead[:, :, :], AX_X).then_inc(s_first_ready, 1)
            dve.wait_ge(s_first_ready, 1)
            dve.scalar_tensor_tensor(out=rank[:, :, :], in0=bcast(first[:, :], 1, T + 1), scalar=128.0, in1=rank[:, :, :],
                                     op0=ALU.mult, op1=ALU.add).then_inc(s_rank_copied, 1)
            dve.wait_ge(s_rank_copied, 2)
            for j in range(TOP):
                dve.tensor_tensor(place[:, j], hot[:, j], rank[:, :, :], ALU.mult).then_inc(s_place_ready, 1)
            dve.wait_ge(s_place_ready, TOP)
            dve.reduce_sum(slotf[:, :, :], place[:, :, :, :], AX_X).then_inc(s_slot_f, 1)
            dve.wait_ge(s_slot_f, 1)
            dve.tensor_copy(slot[:, :, :], slotf[:, :, :]).then_inc(s_slot_ready, 1)
            dve.tensor_tensor(last[:, :], first[0:1, :], tiles[0:1, :], ALU.add).then_inc(s_last_ready, 1)
            dve.wait_ge(s_last_ready, 1)
            dve.tensor_tensor(past[:, :, :], bcast(last[:, :], 1, MT), bcast(tile_no[:, :], 2, E), ALU.is_le).then_inc(s_past_ready, 1)
            dve.wait_ge(s_past_ready, 1)
            dve.reduce_sum(ownerf[:, :], past[:, :, :], AX_X).then_inc(s_owner_f, 1)
            dve.wait_ge(s_owner_f, 1)
            dve.tensor_scalar(ownerf[:, :], ownerf[:, :], float(E - 1), None, ALU.min).then_inc(s_owner_m, 1)
            dve.wait_ge(s_owner_m, 1)
            dve.tensor_copy(owner[:, :], ownerf[:, :]).then_inc(s_owner_ready, 1)
            dve.wait_ge(s_base_ready, 2)
            dve.sem_inc(s_gate_ready, 1)
            for t in range(T + 1):
                r = rows_of(t)
                dve.wait_ge(s_gt_psum, t + 1)
                dve.tensor_copy(gateT[:, t % 2, 0:r], bank[6][0:E, 0:r]).then_inc(s_gt_copied, 1)
                dve.tensor_tensor(H[0:r, t, :], H[0:r, t, :], U[0:r, t, :], ALU.add).then_inc(s_c_om, 1)
                dve.wait_ge(s_c_om, 3 + t)
                dve.wait_ge(s_b2_psum, t + 1)
                dve.tensor_tensor(H[0:r, t, :], bank[7][0:r, 0:C], H[0:r, t, :], ALU.add).then_inc(s_b2_added, 1)
            def hidden_out(t, u):
                dve.wait_ge(s_th_psum, t + 1)
                if not (isinstance(t, int) and t < 2):
                    dve.wait_ge(s_y_psum, t - 1)
                dve.tensor_copy(hT[:, u, 0:4, :], bank[2][:, :])
                dve.tensor_copy(hT[:, u, 4:6, :], bank[3][:, 0:256]).then_inc(s_hT_ready, 1)

            def y_out(t, u):
                dve.wait_ge(s_y_psum, t + 1)
                if not (isinstance(t, int) and t < 2):
                    dve.wait_ge(ys_stored[u], 8 * (t - u))
                dve.tensor_copy(YS[:, u, :], bank[4][:, 0:C]).then_inc(s_ys_ready, 1)

            def expert(t, u):
                hidden_out(t, u)
                y_out(t, u)
            in_pairs(dve, expert, MT)
            for t in range(T + 1):
                r = rows_of(t)
                dve.wait_ge(s_gathered[t], 16 * TOP)
                for j in range(TOP):
                    if j:
                        dve.wait_ge(s_summed, TOP * t + j)
                    dve.scalar_tensor_tensor(out=H[0:r, t, :], in0=Y[j][0:r, t, :], scalar=g12[0:r, t, j:j + 1],
                                             in1=H[0:r, t, :], op0=ALU.mult, op1=ALU.add).then_inc(s_summed, 1)

        @block.scalar
        def _(act):
            act.wait_ge(s_m_sub, 2)
            act.activation(P[0:NP, 0, 0:HEADS * NP], P[0:NP, 0, 0:HEADS * NP], ACT.Exp, scale=SCALE).then_inc(s_m_exp, 1)

            def turned(n, t, u, cols):
                r = rows_of(t)
                act.wait_ge(s_xt_psum, xt_at(n, t))
                for g in range(2):
                    src = turn_bank(n, u)[0:HC, 128 * g:128 * g + r]
                    dst = XT[0:HC, u, g, 0:r]
                    if cols is None:
                        a = act.activation(dst, src, ACT.Copy)
                    else:
                        a = act.activation(dst, src, ACT.Identity, bias=ln_cols[:, cols, 1, g:g + 1], scale=ln_cols[:, cols, 0, g:g + 1])
                a.then_inc(s_xt_ready, 1)

            act.wait_ge(s_ld_const, 16 * N_CONST)
            turned(LN_TOK, 0, 0, 0)

            def mixer(t, u):
                act.wait_ge(s_up1, t + 1)
                if not (isinstance(t, int) and t < 2):
                    act.wait_ge(s_g_ready, t - 1)
                act.activation(silu[:, u, 0:4, :], bank[0][:, :], ACT.Silu)
                act.activation(silu[:, u, 4:6, :], bank[1][:, 0:256], ACT.Silu).then_inc(s_silu_ready, 1)
                if not (isinstance(t, int) and t == T - 1):
                    turned(LN_TOK, t + 1, 1 - u, 0)
            in_pairs(act, mixer)

            for L, n in ((0, LN_ATT), (1, LN_ONE)):
                base = L * (T + 1)
                cols = None if L == 0 else 1

                def qkv(t, u):
                    cls = is_tile(t, CLS)
                    at = base + nth(t) + 1
                    if not is_tile(t, T - 1):
                        if not (base == 0 and cls):
                            act.wait_ge(s_v_psum, at - 1)
                        turned(n, 0 if cls else t + 1, 1 - u, cols)
                    act.wait_ge(s_qk_psum, at)
                    if L == 1 and cls:
                        for u2 in range(2):
                            act.wait_ge(kb_loaded[u2], 16 * HH * (T // 2))
                    src = bank[2 + u][0:HC, 0:256].rearrange("p (a c) -> p a c", a=2)
                    if cls:
                        act.activation(kT[:, :, :, NP], src[:, :, 0:B], ACT.Copy).then_inc(s_k_copied, 1)
                    else:
                        for g in range(2):
                            a = act.activation(kT[:, g, bass.ts(t, 2), 0:NP], src[:, g, :].rearrange("p (j c) -> p j c", j=2), ACT.Copy)
                        a.then_inc(s_k_copied, 1)
                if L == 0:
                    act.wait_ge(s_up3, T)
                else:
                    act.wait_ge(s_v_psum, base)
                turned(n, CLS, 0, cols)
                qkv(CLS, 0)
                in_pairs(act, lambda t, u: qkv(t, 1 - u))

                def exponentials(t, u):
                    act.wait_ge(s_sub_ready, L * T + t + 1)
                    act.activation(P[:, u], P[:, u], ACT.Exp, scale=SCALE).then_inc(s_exp_ready, 1)

                def attend(t, u):
                    act.wait_ge(s_pt_psum, L * T + t + 1)
                    if not is_tile(L * T + t, 0, 1):
                        act.wait_ge(s_o_psum, L * T + t - 1)
                    act.activation(PT[:, u, 0:4, :], bank[4][:, :], ACT.Copy).then_inc(s_pta_copied, 1)
                    if not is_tile(t, 0):
                        turned_out(t - 1, 1 - u)
                    if not is_tile(t, T - 1):
                        exponentials(t + 1, 1 - u)

                def turned_out(t, u):
                    act.wait_ge(s_ot_psum, L * T + t + 1)
                    if not is_tile(t, 0, 1):
                        act.wait_ge(s_proj_psum, res_at(L, t) - T - 2)
                    act.activation(OT[0:HC, u], bank[7][0:HC, 0:256].rearrange("p (a c) -> p a c", a=2), ACT.Copy).then_inc(s_ot_copied, 1)

                exponentials(0, 0)
                in_pairs(act, attend)
                turned_out(T - 1, 1)
                if L == 1:
                    act.wait_ge(s_c_sub, 3)
                    act.activation(Pc[:, :, :], Pc[:, :, :], ACT.Exp, scale=SCALE).then_inc(s_c_exp, 1)

            def route(t, u):
                if t > 0:
                    act.wait_ge(s_lg_psum, t)
                turned(LN_TWO, t + 1, 1 - u, 2)
            turned(LN_TWO, 0, 0, 2)
            for t in range(T):
                route(t, t % 2)
            for k, (r, ts) in enumerate(((128, slice(0, T)), (B, slice(T, T + 1)))):
                act.wait_ge(s_r2, k + 1)
                act.activation(e2[0:r, ts, :], e2[0:r, ts, :], ACT.Exp).then_inc(s_r3, 1)

            def slots_turned(t, u):
                act.wait_ge(s_xt_psum, xt_at(LN_TWO, T) + t + 1)
                if isinstance(t, int) and t < 2:
                    act.wait_ge(s_lg_psum, T + 1)
                else:
                    act.wait_ge(s_up_psum, t - 1)
                for g in range(2):
                    a = act.activation(XT[0:HC, u, g, :], bank[5][0:HC, 128 * g:128 * g + 128], ACT.Identity,
                                       bias=ln_cols[:, 2, 1, g:g + 1], scale=ln_cols[:, 2, 0, g:g + 1])
                a.then_inc(s_xt_ready, 1)

            def slots_out(t, u):
                act.wait_ge(s_ys_ready, t + 1)
                act.dma_start(y_slots[bass.ts(t, 128), :], YS[:, u, :]).then_inc(ys_stored[u], 16)

            def expert(t, u):
                act.wait_ge(s_up_psum, t + 1)
                if not (isinstance(t, int) and t < 2):
                    act.wait_ge(s_th_psum, t - 1)
                for n in range(2):
                    a = act.activation(hid[:, u, n * HID // 2:(n + 1) * HID // 2], bank[n][:, 0:HID // 2], ACT.Gelu)
                a.then_inc(s_hid_ready, 1)
                if not is_tile(t, MT - 1):
                    slots_turned(t + 1, 1 - u)
                if not is_tile(t, 0, 1):
                    slots_out(t - 2, u)
            slots_turned(0, 0)
            expert(0, 0)
            expert(1, 1)
            with act.Fori(1, (MT - 2) // 2) as i:
                for u in range(2):
                    expert(2 * i + u, u)
            for t in range(MT - 2, MT):
                expert(t, t % 2)
            for t in range(MT - 2, MT):
                slots_out(t, t % 2)

        @block.gpsimd
        def _(pool):
            for n, (buf, value) in enumerate(((mhalf[:, :], -0.5), (OT[HC:HC + 1], 1.0), (OTc[HC:HC + 1], 1.0), (XT[HC:HC + 1], 1.0))):
                pool.memset(buf, value).then_inc(s_presets, 1)
                pool.wait_ge(s_presets, n + 1)
            pool.memset(KB[:], 0.0).then_inc(s_kb_zero, 1)
            pool.memset(zero[:], 0.0).then_inc(s_kb_zero, 1)
            pool.wait_ge(s_kb_zero, 2)
            for k, buf in enumerate((hot, g12, slotf)):
                pool.memset(buf[:], 0.0).then_inc(s_hot_cleared, 1)
                pool.wait_ge(s_hot_cleared, k + 1)

            def inv_std(n, t, s):
                r = rows_of(t)
                at = ln_at(n, t)
                pool.wait_ge(s_mv_ready, at)
                own_wait(pool)
                pool.tensor_scalar(veps[0:r, s], mvs[0:r, s, 1:2], LN_EPS, None, ALU.add).then_inc(s_veps_ready, 1)
                pool.wait_ge(s_veps_ready, at)
                pool.tensor_tensor(rstd[0:r, n, t], veps[0:r, s], mhalf[0:r, :], ALU.pow).then_inc(s_rstd_ready, 1)
                pool.wait_ge(s_rstd_ready, at)

            def mixer(t, u):
                if not is_tile(t, T - 1):
                    inv_std(LN_TOK, t + 1, 1 - u)
                inv_std(LN_ATT, t, 3 - u)
            inv_std(LN_ATT, CLS, 2)
            inv_std(LN_TOK, 0, 0)
            in_pairs(pool, mixer)
            for L in range(2):
                if L == 1:
                    pool.wait_ge(s_q_copied, T + 2)
                    for g in range(2):
                        pool.tensor_tensor(QCB[:, g], qT[:, g, T * 128:T * 128 + B].unsqueeze(2).to_broadcast([HC, B, HEADS]),
                                           bcast(head_mask[:, g, :], 1, B), ALU.mult).then_inc(s_c_qcb, 1)
                    pool.wait_ge(s_c_qcb, 2)

                def queries(t, u):
                    if is_tile(t, 2):
                        pool.wait_ge(s_q_copied, (L + 1) * (T + 1))
                    elif is_tile(t, 0, 1):
                        pool.wait_ge(s_q_copied, L * (T + 1) + t + 2)
                    if not is_tile(L * T + t, 0, 1):
                        pool.wait_ge(s_s_psum, L * T + t - 1)
                    pool.tensor_copy(qs[:, u], qT[:, :, bass.ts(t, 128)]).then_inc(s_q_slot, 1)
                    pool.wait_ge(s_q_slot, L * T + t + 1)

                def cls_values(t, u):
                    if is_tile(t, 0):
                        pool.wait_ge(s_vcb_loaded, 16 * HEADS * (L + 1))
                    if not is_tile(L * T + t, 0, 1):
                        pool.wait_ge(s_o_psum, L * T + t - 1)
                    pool.tensor_copy(vcs[:, u], VCB[:, bass.ts(t, 2), :]).then_inc(s_vc_slot, 1)
                    pool.wait_ge(s_vc_slot, L * T + t + 1)

                def attend(t, u):
                    if not is_tile(t, T - 2, T - 1):
                        queries(t + 2, u)
                    if not is_tile(t, T - 1):
                        cls_values(t + 1, 1 - u)
                    if L == 0:
                        if is_tile(t, 0):
                            inv_std(LN_OUTER, CLS, 0)
                            inv_std(LN_ONE, CLS, 2)
                        elif not is_tile(t, 1):
                            inv_std(LN_ONE, t - 2, 3 - u)
                        if not is_tile(t, 0):
                            inv_std(LN_OUTER, t - 1, u)
                    elif not is_tile(t, 0):
                        inv_std(LN_TWO, t - 1, 1 - u)

                queries(0, 0)
                queries(1, 1)
                cls_values(0, 0)
                attend(0, 0)
                attend(1, 1)
                with pool.Fori(1, (T - 2) // 2) as i:
                    for u in range(2):
                        attend(2 * i + u, u)
                for t in range(T - 2, T):
                    attend(t, t % 2)
                if L == 0:
                    inv_std(LN_ONE, T - 2, 3)
                    inv_std(LN_OUTER, T - 1, 0)
                    inv_std(LN_ONE, T - 1, 2)
                else:
                    inv_std(LN_TWO, T - 1, 1)
                    inv_std(LN_TWO, CLS, 0)

            pool.wait_ge(s_slot_ready, 1)
            pool.wait_ge(s_x_zeroed, 48)
            pool.wait_ge(s_xn_ready, xt_at(LN_TWO, T))
            for t in range(T + 1):
                r = rows_of(t)
                for j in range(TOP):
                    pool.indirect_dma_start(x_slots, bass.IndirectOffsetOnAxis(slot[0:r, j, t:t + 1], 0), XA[0:r, t, :],
                                            None).then_inc(s_scattered, 16)
            for u in range(2):
                pool.wait_ge(ys_stored[u], 16 * (MT // 2))
            for t in range(T + 1):
                r = rows_of(t)
                for j in range(TOP):
                    pool.indirect_dma_start(Y[j][0:r, t, :], None, y_slots,
                                            bass.IndirectOffsetOnAxis(slot[0:r, j, t:t + 1], 0)).then_inc(s_gathered[t], 16)


def kernel(x, cls_tok, **w):
    import concourse.bacc as bacc
    from concourse.bass_utils import run_bass_kernel_spmd

    arrays = {f"in_{n}": a for n, a in layout(x, cls_tok, w).items()}
    nc = bacc.Bacc("TRN2", target_bir_lowering=False, num_devices=1)
    d = {n[3:]: nc.dram_tensor(n, a.shape, mybir.dt.from_np(a.dtype), kind="ExternalInput").ap() for n, a in arrays.items()}
    d["out"] = nc.dram_tensor("out", (B, S, C), F32, kind="ExternalOutput").ap()
    build(nc, d)
    return run_bass_kernel_spmd(nc, [arrays], core_ids=[0]).results[0]["out"]


def layout(x, cls_tok, w):
    def halves(a, bias=None, row=False):
        a = np.asarray(a)
        out = np.zeros((HC + int(row or bias is not None), 2, a.shape[1]), np.float32)
        out[0:HC] = a.reshape(2, HC, a.shape[1]).transpose(1, 0, 2)
        if bias is not None:
            out[HC, 1] = np.asarray(bias)
        return out

    def chunks(a):
        a = np.asarray(a)
        return np.ascontiguousarray(a.reshape(KP, 128, a.shape[1]).transpose(1, 0, 2))

    side, patch = 8, 16
    p = np.asarray(x).reshape(B, 3, side, patch, side, patch).transpose(0, 2, 4, 3, 5, 1)
    p = p.reshape(T, 128, KP, 128).transpose(0, 3, 2, 1)

    scales = np.linspace(1.0, 5.0, C // 4)
    seq = np.linspace(-1.0, 1.0, side)[:, None] * scales[None, :] * np.pi
    xs = np.broadcast_to(seq[:, None, :], (side, side, C // 4))
    ys = np.broadcast_to(seq[None, :, :], (side, side, C // 4))
    sin = np.repeat(np.concatenate([np.sin(xs), np.sin(ys)], -1).reshape(NP, C // 2), 2, axis=-1)
    sinT = halves(np.tile(sin.T.astype(np.float32), (1, 2)), row=True)
    sinT[HC] = 1.0

    i, j = np.arange(128)[:, None] % NP, np.arange(S)[None, :]
    mask = np.where((j <= i) | (j == NP), 0.0, -1e30)
    mask = np.broadcast_to(mask[:, None, :], (128, HH, S)).astype(np.dtype("bfloat16"))
    head_mask = np.zeros((HC, 2, HEADS), np.float32)
    for h in range(HEADS):
        head_mask[HD * (h % HH):HD * (h % HH) + HD, h // HH, h] = 1.0
    vb0 = np.zeros((128, B, PAIRS, 2, VW), np.float32)
    vb0[0:NP, :, :, 0, HD] = 1.0
    vb0[NP:128, :, :, 1, HD] = 1.0
    vcb0 = np.zeros((HEADS, B, HEADS * VW), np.float32)
    for h in range(HEADS):
        vcb0[h, :, VW * h + HD] = 1.0
    cols = np.stack([np.stack([np.asarray(w[n]).reshape(2, HC).T for n in pair], 1) for pair in (
        ("L0_tok_ln_g", "L0_tok_ln_b"), ("L0_ffn_ln1_g", "L0_ffn_ln1_b"), ("L0_ffn_ln2_g", "L0_ffn_ln2_b"))], 1)
    return {
        "patches": np.ascontiguousarray(p),
        "cls": np.ascontiguousarray(np.broadcast_to(np.asarray(cls_tok).reshape(1, C), (B, C))),
        "sinT": sinT.reshape(HC + 1, 2, 2, NP),
        "ident": np.eye(128, dtype=np.float32),
        "identb": np.eye(128).astype(np.dtype("bfloat16")),
        "maskb": np.ascontiguousarray(mask),
        "ones": np.ones((1, 128), np.float32),
        "head_mask": head_mask,
        "iota8": np.broadcast_to(np.arange(E, dtype=np.float32), (128, E)).copy(),
        "tri": np.triu(np.ones((128, 128), np.float32), 1),
        "ones128": np.ones((128, 128), np.float32),
        "steps": np.broadcast_to(128.0 * np.arange(T + 2, dtype=np.float32), (128, T + 2)).copy(),
        "before": np.broadcast_to(np.tril(np.ones((E, E), np.float32), -1), (128, E, E)).copy(),
        "tile_no": np.arange(MT, dtype=np.float32).reshape(1, MT),
        "vm0": vb0[:, 0, 0].copy(),
        "vb0": vb0,
        "vcb0": vcb0,
        "ln_cols": np.ascontiguousarray(cols),
        "patch_b": np.asarray(w["L0_tok_patch_b"]).reshape(1, C),
        "w_patch": chunks(w["L0_tok_patch_w"]),
        "wqkv_m": halves(w["L0_tok_wqkv"], w["L0_tok_bqkv"]),
        "wo_m": halves(w["L0_tok_wo"], w["L0_tok_bo"]),
        "w13": halves(np.concatenate([np.asarray(w["L0_tok_w1"]), np.asarray(w["L0_tok_w3"])], 1)),
        "w2t": chunks(w["L0_tok_w2"]),
        "wqkv0": halves(w["L0_attn_w_attn"], w["L0_attn_b_attn"]),
        "wproj0": halves(w["L0_attn_w_proj"], w["L0_attn_b_proj"]),
        "wqkv1": halves(w["L0_ffn_qkv_w"], w["L0_ffn_qkv_b"]),
        "wproj1": halves(w["L0_ffn_proj_w"], w["L0_ffn_proj_b"]),
        "w_gate": halves(w["L0_ffn_gate_w"]),
        "w1": np.stack([halves(np.asarray(w["L0_ffn_w1"])[e], np.asarray(w["L0_ffn_b1"])[e]) for e in range(E)]),
        "w2": np.stack([chunks(np.asarray(w["L0_ffn_w2"])[e]) for e in range(E)]),
        "b2": np.asarray(w["L0_ffn_b2"]),
    }
```

```python
from contextlib import ExitStack

import numpy as np
import concourse.bass as bass
from concourse import mybir

F32 = mybir.dt.float32
BF16 = mybir.dt.bfloat16
U32 = mybir.dt.uint32
ALU = mybir.AluOpType
ACT = mybir.ActivationFunctionType
AX_X = mybir.AxisListType.X

B = 16
NP = 64
S = NP + 1
C = 192
HC = C // 2
HEADS = 12
HD = C // HEADS
HH = HEADS // 2
PAIRS = HEADS // 2
VW = HD + 1
T = B * NP // 128
CLS = T
HID = 4 * C
KP = HID // 128
E = 8
TOP = 2
MT = (TOP * B * S + E * 127) // 128
SLOTS = MT * 128
ROW = C + 1 + E
FILLS = 3
LN_EPS = 1e-5
SCALE = 0.25
BANK = 512
LN_TOK, LN_ATT, LN_OUTER, LN_ONE, LN_TWO = range(5)


def rows_of(t):
    return B if is_tile(t, CLS) else 128


def bcast(ap, at, n):
    a = ap.unsqueeze(at)
    shape = list(a.shape)
    shape[at] = n
    return a.to_broadcast(shape)


def in_pairs(eng, step, n=T, tail=2):
    assert (n - 2 - tail) % 2 == 0
    step(0, 0)
    step(1, 1)
    with eng.Fori(1, (n - tail) // 2) as i:
        step(2 * i, 0)
        step(2 * i + 1, 1)
    for t in range(n - tail, n):
        step(t, t % 2)


def is_tile(t, *which):
    return isinstance(t, int) and t in which


def build(nc, d):
    with ExitStack() as ctx:
        def sb(name, shape, dt=F32):
            return ctx.enter_context(nc.sbuf_tensor(name, shape, dt))

        def sem(name):
            return ctx.enter_context(nc.semaphore(name))

        bank = [ctx.enter_context(nc.psum_tensor(f"bank{i}", [128, BANK], F32)) for i in range(8)]

        ident = sb("ident", [128, 128])
        identb = sb("identb", [128, 128], BF16)
        maskb = sb("maskb", [128, HH, S], BF16)
        ones = sb("ones", [1, 128])
        head_mask = sb("head_mask", [HC, 2, HEADS])
        ln_cols = sb("ln_cols", [HC, 3, 2, 2])
        sinT = sb("sinT", [HC + 1, 2, 2, NP])
        patch_b = sb("patch_b", [1, C])
        wqkv_m = sb("wqkv_m", [HC + 1, 2, C + 2 * HD])
        wo_m = sb("wo_m", [HC + 1, 2, C])
        w_patch = sb("w_patch", [128, KP, C])
        w2t = sb("w2t", [128, KP, C])
        wqkv = [sb(f"wqkv{L}", [HC + 1, 2, 3 * C]) for L in range(2)]
        wproj = [sb(f"wproj{L}", [HC + 1, 2, C]) for L in range(2)]
        w_gate = sb("w_gate", [HC, 2, E])
        b2 = sb("b2", [E, C])
        iota8 = sb("iota8", [128, E])

        H = sb("H", [128, T + 1, C])
        U = sb("U", [128, T + 1, C])
        stat = sb("stat", [128, 2, 6])
        mean = sb("mean", [128, 5, T + 1, 1])
        mvs = sb("mvs", [128, 4, 2])
        veps = sb("veps", [128, 4, 1])
        rstd = sb("rstd", [128, 5, T + 1, 1])
        mhalf = sb("mhalf", [128, 1])
        MD = sb("MD", [128, C])
        XN = sb("XN", [128, 2, C])
        XT = sb("XT", [HC + 1, 2, 2, 128])

        def carve(region, specs):
            at, views = 0, []
            for rows, sizes in specs:
                names = "abcde"[0:len(sizes)]
                n = int(np.prod(sizes))
                views.append(region[0:rows, at:at + n].rearrange(
                    f"p ({' '.join(names)}) -> p {' '.join(names)}", **dict(zip(names, sizes))))
                at += n
            return views

        mixer_mem = sb("mixer_mem", [128, E * KP * C])
        w13, px, silu, gT = carve(mixer_mem, (
            (HC, (2, 2 * HID)), (128, (2, KP, 128)), (128, (2, KP, 128)), (128, (2, KP, 128))))
        w2r, = carve(mixer_mem, ((128, (E, KP, C)),))

        attn_specs = ((HC, (2, 2, HH, 2 * S)), (128, (B, PAIRS, 2, VW)), (HEADS, (B, HEADS * VW)),
                      (128, (2, HEADS * S)), (128, (2, PAIRS + 1, 128)))
        attn_mem = sb("attn_mem", [128, sum(int(np.prod(sizes)) for _, sizes in attn_specs)])
        KB, VB, VCB, P, PT = carve(attn_mem, attn_specs)
        w1r, = carve(attn_mem, ((HC + 1, (E, 2, HID)),))

        qkv_specs = ((HC, (2, T * 128 + B)), (HC, (2, B, S)), (S, (B, C)))
        qkv_mem = sb("qkv_mem", [128, sum(int(np.prod(sizes)) for _, sizes in qkv_specs)])
        qT, kT, VN = carve(qkv_mem, qkv_specs)
        hid, hT, XG = carve(qkv_mem, ((128, (2, HID)), (128, (2, KP, 128)), (128, (2, ROW))))
        empty, = carve(qkv_mem[:, 2 * (T * 128 + B) + 2 * B * S:], ((128, (SLOTS // 128 // FILLS, ROW)),))
        VC = sb("VC", [B, C])
        vcs = sb("vcs", [HEADS, 2, 2, HEADS * VW])
        qs = sb("qs", [HC, 2, 2, 128])
        mx = sb("mx", [128, 2, HEADS])
        rec = sb("rec", [NP, 2, 2 * HEADS])
        ON = sb("ON", [NP, 2, 2, C])
        OT = sb("OT", [HC + 1, 2, 2, 128])
        OTc = sb("OTc", [HC + 1, 2, B])
        QCB = sb("QCB", [HC, 2, B, HEADS])
        Pc = sb("Pc", [HEADS, B, S])
        mxc = sb("mxc", [HEADS, B])
        smc = sb("smc", [HEADS, B])
        PcT = sb("PcT", [S, B, HEADS])
        OCm = sb("OCm", [HC, 2, B, HEADS])
        qm = sb("qm", [HD, HEADS, NP])
        km = sb("km", [HD, NP])
        VM = sb("VM", [128, 2, VW])
        XA = sb("XA", [128, T + 1, ROW])
        out_row = sb("out_row", [128, T + 1])
        spare_row = sb("spare_row", [128, SLOTS // 128 // FILLS])
        lg = sb("lg", [128, T + 1, E])
        mx8 = sb("mx8", [128, T + 1, 8])
        ix8 = sb("ix8", [128, T + 1, 8], U32)
        ixf = sb("ixf", [128, T + 1, TOP])
        e2 = sb("e2", [128, T + 1, 1])
        g12 = sb("g12", [128, T + 1, TOP])
        hot = sb("hot", [128, TOP, T + 1, E])
        picked = sb("picked", [128, T + 1, E], BF16)
        gate = XA[:, :, C + 1:]
        gate1 = sb("gate1", [128, T + 1, E])
        gate2 = sb("gate2", [128, T + 1, E])
        gateT = sb("gateT", [E, 2, 128])
        tri = sb("tri", [128, 128], BF16)
        ones128 = sb("ones128", [128, 128], BF16)
        steps = sb("steps", [128, T + 2])
        before = sb("before", [128, E, E])
        tile_no = sb("tile_no", [128, MT])
        rank = sb("rank", [128, T + 1, E])
        total = sb("total", [128, E])
        full = sb("full", [128, E, T + 2])
        tiles = sb("tiles", [128, E])
        ahead = sb("ahead", [128, E, E])
        first = sb("first", [128, E])
        last = sb("last", [128, E])
        past = sb("past", [128, MT, E])
        own = sb("own", [128, MT, E])
        meta = sb("meta", [128, 2, 1])
        to_row = sb("to_row", [128, 2, 1], U32)
        picks = sb("picks", [128, 2, E])
        weight = sb("weight", [128, 2, 1])
        ownerf = sb("ownerf", [1, MT])
        owner = sb("owner", [1, MT], U32)
        place = sb("place", [128, TOP, T + 1, E])
        slotf = sb("slotf", [128, TOP, T + 1])
        slot = sb("slot", [128, TOP, T + 1], U32)
        YS = sb("YS", [128, 2, C])
        x_slots = nc.dram_tensor("x_slots", (SLOTS, ROW), F32, kind="Internal").ap()

        s_ld_const = sem("s_ld_const")
        s_ld_mixer = sem("s_ld_mixer")
        s_ld_patch = sem("s_ld_patch")
        s_ld_tables = sem("s_ld_tables")
        s_ld_up = sem("s_ld_up")
        s_ld_down = sem("s_ld_down")
        s_ld_attn = sem("s_ld_attn")
        s_ld_ffn = sem("s_ld_ffn")
        s_ld_px0 = sem("s_ld_px0")
        s_ld_px1 = sem("s_ld_px1")
        s_ld_cls = sem("s_ld_cls")
        s_out_done = sem("s_out_done")
        s_m_q = sem("s_m_q")
        s_m_k = sem("s_m_k")
        s_m_qc = sem("s_m_qc")
        s_m_s = sem("s_m_s")
        s_m_max = sem("s_m_max")
        s_m_sub = sem("s_m_sub")
        s_m_exp = sem("s_m_exp")
        s_m_t = sem("s_m_t")
        s_m_tc = sem("s_m_tc")
        s_m_o = sem("s_m_o")
        s_m_rec = sem("s_m_rec")
        s_m_norm = sem("s_m_norm")
        s_m_ot = sem("s_m_ot")
        s_m_otc = sem("s_m_otc")
        s_m_md = sem("s_m_md")
        s_m_mdc = sem("s_m_mdc")
        s_tok_ready = sem("s_tok_ready")
        s_z_ready = sem("s_z_ready")
        s_stat_ready = sem("s_stat_ready")
        s_mv_ready = sem("s_mv_ready")
        s_mean_ready = sem("s_mean_ready")
        s_veps_ready = sem("s_veps_ready")
        s_rstd_ready = sem("s_rstd_ready")
        s_xn_ready = sem("s_xn_ready")
        s_xt_psum = sem("s_xt_psum")
        s_xt_ready = sem("s_xt_ready")
        s_up1 = sem("s_up1")
        s_up3 = sem("s_up3")
        s_silu_ready = sem("s_silu_ready")
        s_g_ready = sem("s_g_ready")
        s_down_ready = sem("s_down_ready")
        s_res_ready = sem("s_res_ready")
        s_qk_psum = sem("s_qk_psum")
        s_v_psum = sem("s_v_psum")
        s_k_copied = sem("s_k_copied")
        s_q_copied = sem("s_q_copied")
        s_v_copied = sem("s_v_copied")
        s_vn_copied = sem("s_vn_copied")
        s_kb_loaded0 = sem("s_kb_loaded0")
        s_kb_loaded1 = sem("s_kb_loaded1")
        s_vcb_loaded = sem("s_vcb_loaded")
        s_vn_loaded = sem("s_vn_loaded")
        s_q_slot = sem("s_q_slot")
        s_vc_slot = sem("s_vc_slot")
        s_own_waits = sem("s_own_waits")
        s_s_psum = sem("s_s_psum")
        s_max_ready = sem("s_max_ready")
        s_sub_ready = sem("s_sub_ready")
        s_exp_ready = sem("s_exp_ready")
        s_pt_psum = sem("s_pt_psum")
        s_pt_copied = sem("s_pt_copied")
        s_o_psum = sem("s_o_psum")
        s_rec_ready = sem("s_rec_ready")
        s_on_ready = sem("s_on_ready")
        s_ot_psum = sem("s_ot_psum")
        s_ot_copied = sem("s_ot_copied")
        s_proj_psum = sem("s_proj_psum")
        s_presets = sem("s_presets")
        s_kb_zero = sem("s_kb_zero")
        s_cls_otc = sem("s_cls_otc")
        s_c_qcb = sem("s_c_qcb")
        s_c_s = sem("s_c_s")
        s_c_max = sem("s_c_max")
        s_c_sub = sem("s_c_sub")
        s_c_exp = sem("s_c_exp")
        s_c_sum = sem("s_c_sum")
        s_c_rec = sem("s_c_rec")
        s_c_p = sem("s_c_p")
        s_c_pt = sem("s_c_pt")
        s_c_ptc = sem("s_c_ptc")
        s_c_o = sem("s_c_o")
        s_c_om = sem("s_c_om")
        s_lg_psum = sem("s_lg_psum")
        s_lg_copied = sem("s_lg_copied")
        s_mx8_ready = sem("s_mx8_ready")
        s_ix8_ready = sem("s_ix8_ready")
        s_r1 = sem("s_r1")
        s_r2 = sem("s_r2")
        s_r3 = sem("s_r3")
        s_r4 = sem("s_r4")
        s_r5 = sem("s_r5")
        s_r6 = sem("s_r6")
        s_gate_ready = sem("s_gate_ready")
        s_gt_psum = sem("s_gt_psum")
        s_gt_copied = sem("s_gt_copied")
        s_b2_psum = sem("s_b2_psum")
        s_b2_added = sem("s_b2_added")
        s_y_psum = sem("s_y_psum")

        s_x_zeroed = sem("s_x_zeroed")
        s_ld_w1 = sem("s_ld_w1")
        s_ld_w2 = sem("s_ld_w2")
        s_hot_cleared = sem("s_hot_cleared")
        s_hot_ready = sem("s_hot_ready")
        s_picked_ready = sem("s_picked_ready")
        s_rank_psum = sem("s_rank_psum")
        s_rank_copied = sem("s_rank_copied")
        s_total_copied = sem("s_total_copied")
        s_full_ready = sem("s_full_ready")
        s_tiles_ready = sem("s_tiles_ready")
        s_ahead_ready = sem("s_ahead_ready")
        s_first_ready = sem("s_first_ready")
        s_last_ready = sem("s_last_ready")
        s_past_ready = sem("s_past_ready")
        s_owner_f = sem("s_owner_f")
        s_owner_m = sem("s_owner_m")
        s_owner_ready = sem("s_owner_ready")
        s_place_ready = sem("s_place_ready")
        s_slot_f = sem("s_slot_f")
        s_slot_ready = sem("s_slot_ready")
        s_xg_loaded0 = sem("s_xg_loaded0")
        s_xg_loaded1 = sem("s_xg_loaded1")
        s_scattered = sem("s_scattered")
        s_up_psum = sem("s_up_psum")
        s_hid_ready = sem("s_hid_ready")
        s_th_psum = sem("s_th_psum")
        s_hT_ready = sem("s_hT_ready")
        s_ys_ready = sem("s_ys_ready")
        s_added = sem("s_added")
        s_meta_ready = sem("s_meta_ready")
        s_picks_ready = sem("s_picks_ready")
        s_own_first = sem("s_own_first")
        s_own_ready = sem("s_own_ready")
        s_rows_written = sem("s_rows_written")
        s_gates2 = sem("s_gates2")

        ld_px = (s_ld_px0, s_ld_px1)
        kb_loaded = (s_kb_loaded0, s_kb_loaded1)
        xg_loaded = (s_xg_loaded0, s_xg_loaded1)

        LN_BASE = {LN_TOK: 0, LN_ATT: 0, LN_OUTER: 2 * T + 1, LN_ONE: 2 * T + 1, LN_TWO: 4 * T + 3}

        def ln_at(n, t):
            if n == LN_TOK:
                at = t + 2 if is_tile(t, 0, 1) else 2 * t
            elif n == LN_ATT:
                at = 1 if is_tile(t, CLS) else T + 2 + t if is_tile(t, T - 2, T - 1) else 2 * t + 5
            elif n == LN_OUTER:
                at = 1 if is_tile(t, CLS) else 2 * t + 3
            elif n == LN_ONE:
                at = 2 if is_tile(t, CLS) else 2 * t + 4
            else:
                at = t + 1
            return LN_BASE[n] + at

        def slot_before(n, t):
            if n in (LN_TOK, LN_TWO):
                return LN_BASE[n] if is_tile(t, 0, 1) else ln_at(n, t - 2)
            return LN_BASE[n] if is_tile(t, 0, CLS) else ln_at(n, CLS) if is_tile(t, 1) else ln_at(n, t - 2)

        def nth(t):
            return 0 if is_tile(t, CLS) else t + 1

        def xt_at(n, t):
            return {LN_TOK: 0, LN_ATT: T, LN_ONE: 2 * T + 1, LN_TWO: 3 * T + 2}[n] + \
                (t if n in (LN_TOK, LN_TWO) else nth(t)) + 1

        def turn_bank(n, u):
            return bank[5] if n == LN_TOK or u == 0 else bank[4] if n == LN_TWO else bank[7]

        def res_at(L, t):
            return T + L * (T + 1) + (nth(t) if L == 0 else t) + 1

        def tile_cols(t):
            return bass.ts(t, 128) if not is_tile(t, CLS) else slice(T * 128, T * 128 + B)

        def own_wait(eng):
            eng.sem_inc(s_own_waits, 1)

        def weights(u, r0, r1):
            return P[r0:r1, u, 0:HEADS * NP].rearrange("p (h j) -> p h j", h=HEADS)

        block = ctx.enter_context(nc.Block())

        LG_TILES = ((0, T // 2), (T // 2, T - 1), (T - 1, T + 1))
        SPANS = ((128, slice(0, T - 1)), (128, slice(T - 1, T)), (B, slice(T, T + 1)))
        ROUTED = 3
        N_CONST = 7
        N_TABLES = 9

        @block.sync
        def _(sp):
            for dst, src in ((wqkv_m, "wqkv_m"), (VM, "vm0"), (wo_m, "wo_m")):
                sp.dma_start(dst[:], d[src]).then_inc(s_ld_mixer, 16)
            for dst, src in (
                (sinT, "sinT"), (identb, "identb"), (maskb, "maskb"), (ident, "ident"), (patch_b, "patch_b"),
                (ones, "ones"), (ln_cols, "ln_cols"),
            ):
                sp.dma_start(dst[:], d[src]).then_inc(s_ld_const, 16)
            sp.dma_start(px[:, 0], d["patches"][0]).then_inc(ld_px[0], 16)
            sp.dma_start(w_patch[:], d["w_patch"]).then_inc(s_ld_patch, 16)
            sp.dma_start(px[:, 1], d["patches"][1]).then_inc(ld_px[1], 16)
            sp.dma_start(H[0:B, CLS, :], d["cls"]).then_inc(s_ld_cls, 16)
            sp.dma_start(w13[:], d["w13"]).then_inc(s_ld_up, 16)
            sp.dma_start(w2t[:], d["w2t"]).then_inc(s_ld_down, 16)
            for dst, src in (
                (spare_row, "spare_row"), (out_row, "out_row"), (head_mask, "head_mask"), (iota8, "iota8"), (tri, "tri"),
                (ones128, "ones128"), (steps, "steps"), (before, "before"), (tile_no, "tile_no"),
            ):
                sp.dma_start(dst[:], d[src]).then_inc(s_ld_tables, 16)
            for L in range(2):
                sp.dma_start(wqkv[L][:], d[f"wqkv{L}"]).then_inc(s_ld_attn, 16)
                sp.dma_start(wproj[L][:], d[f"wproj{L}"]).then_inc(s_ld_attn, 16)
            sp.dma_start(VB[:], d["vb0"]).then_inc(s_ld_attn, 16)
            sp.dma_start(VCB[:], d["vcb0"]).then_inc(s_ld_attn, 16)
            sp.dma_start(w_gate[:], d["w_gate"]).then_inc(s_ld_ffn, 16)
            sp.dma_start(b2[:], d["b2"]).then_inc(s_ld_ffn, 16)
            sp.wait_ge(s_kb_zero, 3)
            for k in range(FILLS):
                sp.dma_start(x_slots[k * SLOTS // FILLS:(k + 1) * SLOTS // FILLS].rearrange("(p r) c -> p r c", p=128),
                             empty[:, :, :]).then_inc(s_x_zeroed, 16)
            with sp.Fori(0, (T - 2) // 2) as i:
                for u in range(2):
                    sp.wait_ge(s_tok_ready, 2 * i + u + 1)
                    sp.dma_start(px[:, u], d["patches"][2 * i + u + 2]).then_inc(ld_px[u], 16)
            sp.wait_ge(s_down_ready, T)
            for e in range(E):
                sp.dma_start(w2r[:, e], d["w2"][e]).then_inc(s_ld_w2, 16)
            for L in range(2):
                sp.wait_ge(s_v_copied, L * (T + 1) + 1)
                if L == 1:
                    sp.wait_ge(s_vc_slot, T)
                for h in range(HEADS):
                    sp.dma_start(VCB[h:h + 1, :, VW * h:VW * h + HD],
                                 VC[:, HD * h:HD * h + HD]).then_inc(s_vcb_loaded, 16)
                if L == 1:
                    sp.wait_ge(s_x_zeroed, 16 * FILLS)
                    sp.dma_start(VN[NP:S, :, :], VC[:, :]).then_inc(s_vn_loaded, 16)
                sp.wait_ge(s_kb_zero, 1)

                def spread_keys(t, u):
                    if is_tile(t, 0, 1):
                        sp.wait_ge(s_k_copied, L * (T + 1) + t + 2)
                    elif is_tile(t, 2):
                        sp.wait_ge(s_k_copied, (L + 1) * (T + 1))
                    if not is_tile(L * T + t, 0, 1):
                        sp.wait_ge(s_s_psum, L * T + t - 1)
                    for h in range(HH):
                        p0 = HD * h
                        sp.dma_start(KB[p0:p0 + HD, u, :, h, :],
                                     kT[p0:p0 + HD, :, bass.ts(t, 2), :].rearrange("p g j s -> p g (j s)")).then_inc(kb_loaded[u], 16)
                for t in range(4):
                    spread_keys(t, t % 2)
                with sp.Fori(2, T // 2) as i:
                    for u in range(2):
                        spread_keys(2 * i + u, u)
            sp.wait_ge(s_o_psum, 2 * T)
            for e in range(E):
                sp.dma_start(w1r[:, e], d["w1"][e]).then_inc(s_ld_w1, 16)
            sp.wait_ge(s_scattered, 16 * TOP * (T + 1))

            def slots_in(t, u):
                if not is_tile(t, 0, 1):
                    sp.wait_ge(s_meta_ready, t - 1)
                sp.dma_start(XG[:, u, :], x_slots[bass.ts(t, 128), :]).then_inc(xg_loaded[u], 16)

            slots_in(0, 0)
            slots_in(1, 1)
            with sp.Fori(0, (MT - 2) // 2) as i:
                for u in range(2):
                    slots_in(2 * i + u + 2, u)
            sp.wait_ge(s_out_done, 16 * (2 * T + 1))
            sp.wait_ge(s_added, 16 * MT)

        @block.tensor
        def _(pe):
            def both_halves(out, lhs, rhs, bias=True, start=True, stop=True):
                k = HC + 1 if bias else HC
                pe.matmul(out, lhs(0)[0:HC], rhs(0)[0:HC], start=start, stop=False)
                return pe.matmul(out, lhs(1)[0:k], rhs(1)[0:k], start=False, stop=stop)

            pe.wait_ge(s_ld_const, 16 * N_CONST)
            pe.wait_ge(s_ld_mixer, 16 * 3)
            for h in range(HEADS):
                mm = both_halves(bank[h // HH][0:HD, NP * (h % HH):NP * (h % HH) + NP],
                                 lambda g: wqkv_m[:, g, HD * h:HD * h + HD], lambda g: sinT[:, g, 0, :])
            mm.then_inc(s_m_q, 1)
            both_halves(bank[2][0:HD, 0:NP], lambda g: wqkv_m[:, g, C:C + HD], lambda g: sinT[:, g, 0, :])
            both_halves(bank[2][:, NP:NP + HD], lambda g: sinT[:, g].rearrange("p a b -> p (a b)"),
                        lambda g: wqkv_m[:, g, C + HD:C + 2 * HD]).then_inc(s_m_k, 1)
            pe.wait_ge(s_m_qc, 4)
            for g in range(2):
                pe.matmul(bank[3 + g][0:NP, 0:HH * NP], identb[0:NP, 0:NP], maskb[0:NP, :, 0:NP],
                          start=True, stop=False)
                for j in range(HH):
                    mm = pe.matmul(bank[3 + g][0:NP, NP * j:NP * j + NP], qm[:, HH * g + j, :], km[:, :],
                                   start=False, stop=(j == HH - 1))
            mm.then_inc(s_m_s, 1)

            def tok(t, u):
                pe.wait_ge(ld_px[u], 8 * (t - u) + 16)
                if is_tile(t, 0):
                    pe.wait_ge(s_ld_patch, 16)
                else:
                    pe.wait_ge(s_z_ready, t)
                for k in range(KP):
                    mm = pe.matmul(bank[7][:, 0:C], px[:, u, k, :], w_patch[:, k, :],
                                   start=(k == 0), stop=(k == KP - 1))
                mm.then_inc(s_tok_ready, 1)
            tok(0, 0)

            pe.wait_ge(s_m_exp, 1)
            for p in range(PAIRS):
                mm = pe.transpose(bank[5][:, NP * p:NP * p + NP], P[0:NP, 0, 2 * NP * p:2 * NP * (p + 1)], ident[0:NP, 0:NP])
            mm.then_inc(s_m_t, 1)
            pe.wait_ge(s_m_tc, 1)
            for p in range(PAIRS):
                mm = pe.matmul(bank[6][0:NP, 2 * VW * p:2 * VW * p + 2 * VW], PT[:, 0, p, 0:NP], VM[:, :, :],
                               start=True, stop=True)
            mm.then_inc(s_m_o, 1)
            pe.wait_ge(s_m_norm, 1)
            for g in range(2):
                mm = pe.transpose(bank[5][0:HC, NP * g:NP * g + NP], ON[:, 0, 0, HC * g:HC * g + HC], ident[0:NP, 0:NP])
            mm.then_inc(s_m_ot, 1)
            pe.wait_ge(s_m_otc, 1)
            pe.wait_ge(s_presets, 4)
            both_halves(bank[6][:, 0:C], lambda g: OT[:, 0, g, :], lambda g: wo_m[:, g, :], stop=False)
            pe.matmul(bank[6][:, 0:C], ones[:, :], patch_b[:, :], start=False, stop=True).then_inc(s_m_md, 1)

            def turn(n, t, u):
                r = rows_of(t)
                pe.wait_ge(s_xn_ready, xt_at(n, t))
                if n == LN_TOK:
                    if not is_tile(t, 0):
                        pe.wait_ge(s_xt_ready, xt_at(n, t) - 1)
                elif is_tile(t, 0 if n == LN_TWO else CLS):
                    pe.wait_ge(s_xt_ready, xt_at(n, t) - 1)
                else:
                    pe.wait_ge(s_xt_ready, xt_at(n, t) - 2)
                for g in range(2):
                    x = XA[0:r, t] if n == LN_TWO else XN[0:r, u]
                    mm = pe.transpose(turn_bank(n, u)[0:HC, 128 * g:128 * g + r], x[:, HC * g:HC * g + HC], ident[0:r, 0:r])
                mm.then_inc(s_xt_psum, 1)

            def mixer(t, u):
                pe.wait_ge(s_xt_ready, xt_at(LN_TOK, t))
                if not is_tile(t, 0):
                    pe.wait_ge(s_silu_ready, t)
                else:
                    pe.wait_ge(s_m_norm, 1)
                    pe.wait_ge(s_ld_up, 16)
                for w, done in ((0, s_up1), (1, s_up3)):
                    if w == 1 and not is_tile(t, 0):
                        pe.wait_ge(s_g_ready, t)
                    for m in range(KP):
                        mm = both_halves(bank[2 * w + m // 4][:, 128 * (m % 4):128 * (m % 4) + 128],
                                         lambda g: w13[:, g, HID * w + 128 * m:HID * w + 128 * m + 128],
                                         lambda g: XT[:, u, g, :], bias=False)
                    mm.then_inc(done, 1)
                if not is_tile(t, T - 1):
                    turn(LN_TOK, t + 1, 1 - u)
                if not is_tile(t, T - 2, T - 1):
                    tok(t + 2, u)
                if is_tile(t, T - 1):
                    turn(LN_ATT, CLS, 0)
                pe.wait_ge(s_g_ready, t + 1)
                if not is_tile(t, 0):
                    pe.wait_ge(s_res_ready, t)
                else:
                    pe.wait_ge(s_ld_down, 16)
                for k in range(KP):
                    mm = pe.matmul(bank[6][:, 0:C], gT[:, u, k, :], w2t[:, k, :], start=(k == 0), stop=(k == KP - 1))
                mm.then_inc(s_down_ready, 1)

            tok(1, 1)
            turn(LN_TOK, 0, 0)
            in_pairs(pe, mixer)

            def route(t, u):
                if t < T:
                    turn(LN_TWO, t + 1, 1 - u)
                r = rows_of(t)
                k, i = [(k, t - t0) for k, (t0, t1) in enumerate(LG_TILES) if t0 <= t < t1][0]
                pe.wait_ge(s_xt_ready, xt_at(LN_TWO, t))
                both_halves(bank[k][0:r, E * i:E * i + E], lambda g: XT[:, u, g, 0:r], lambda g: w_gate[:, g, :], bias=False)\
                    .then_inc(s_lg_psum, 1)

            def out_turn(t, u, L):
                pe.wait_ge(s_on_ready, L * T + t + 1)
                pe.wait_ge(s_res_ready, res_at(L, t) - 1)
                own_wait(pe)
                for g in range(2):
                    for j in range(2):
                        mm = pe.transpose(bank[7][0:HC, 128 * g + NP * j:128 * g + NP * j + NP],
                                          ON[:, u, j, HC * g:HC * g + HC], ident[0:NP, 0:NP])
                mm.then_inc(s_ot_psum, 1)

            def project(t, u, L):
                pe.wait_ge(s_ot_copied, L * T + t + 1)
                both_halves(bank[7][:, 256:256 + C], lambda g: OT[:, u, g, :], lambda g: wproj[L][:, g, :]).then_inc(s_proj_psum, 1)

            for L, n in ((0, LN_ATT), (1, LN_ONE)):
                base = L * (T + 1)

                def qkv(t, u):
                    cls = is_tile(t, CLS)
                    i = nth(t)
                    if not is_tile(t, T - 1, CLS):
                        turn(n, t + 1, 1 - u)
                    r = rows_of(t)
                    qb, kb, vb = bank[u], bank[2 + u], bank[4 + 2 * u]
                    pe.wait_ge(s_xt_ready, xt_at(n, t))
                    if not is_tile(base + i, 0, 1):
                        pe.wait_ge(s_q_copied, base + i - 1)
                        pe.wait_ge(s_k_copied, base + i - 1)
                    for m in range(4):
                        mm = both_halves((qb, kb)[m // 2][0:HC, 128 * (m % 2):128 * (m % 2) + r], lambda g: wqkv[L][:, g, HC * m:HC * m + HC],
                                         lambda g: XT[:, u, g, 0:r])
                    mm.then_inc(s_qk_psum, 1)
                    if not is_tile(base + i, 0, 1):
                        pe.wait_ge(s_v_copied, base + i - 1)
                    elif is_tile(base + i, 1):
                        pe.wait_ge(s_res_ready, T)
                    if cls:
                        if L == 0:
                            for m in range(2):
                                both_halves(vb[0:HC, 256 + B * m:256 + B * m + B],
                                            lambda g: wqkv[L][:, g, 2 * C + HC * m:2 * C + HC * m + HC],
                                            lambda g: XT[:, u, g, 0:B])
                        mm = both_halves(vb[0:B, 0:C], lambda g: XT[:, u, g, 0:B], lambda g: wqkv[L][:, g, 2 * C:3 * C])
                    else:
                        both_halves(vb[:, 0:C], lambda g: XT[:, u, g, :], lambda g: wqkv[L][:, g, 2 * C:3 * C])

                        def by_head(ap, a):
                            return ap.rearrange("p (m a d) -> p m a d", m=PAIRS, a=2)[:, :, a, :]
                        both_halves(by_head(vb[NP:128, C:2 * C], 1), lambda g: XT[:, u, g, 0:NP],
                                    lambda g: by_head(wqkv[L][:, g, 2 * C:3 * C], 1))
                        if L == 0:
                            mm = both_halves(by_head(vb[0:NP, C:2 * C], 0), lambda g: XT[:, u, g, NP:128],
                                             lambda g: by_head(wqkv[L][:, g, 2 * C:3 * C], 0))
                        else:
                            mm = both_halves(vb[0:NP, C:2 * C], lambda g: XT[:, u, g, NP:128],
                                             lambda g: wqkv[L][:, g, 2 * C:3 * C])
                    mm.then_inc(s_v_psum, 1)

                if L == 0:
                    pe.wait_ge(s_ld_attn, 16 * 6)
                    pe.wait_ge(s_silu_ready, T)
                    pe.wait_ge(s_g_ready, T)
                    pe.wait_ge(s_z_ready, T)
                    qkv(CLS, 0)
                    turn(n, 0, 1)
                else:
                    out_turn(T - 1, 1, 0)
                    qkv(CLS, 0)
                    project(T - 1, 1, 0)
                    pe.wait_ge(s_res_ready, T + L * (T + 1))
                    turn(n, 0, 1)
                in_pairs(pe, lambda t, u: qkv(t, 1 - u))

                def scores(t, u):
                    pe.wait_ge(s_q_slot, L * T + t + 1)
                    pe.wait_ge(kb_loaded[u], 16 * HH * (L * T // 2 + 1) + 8 * HH * (t - u))
                    if is_tile(t, 0):
                        pe.wait_ge(s_q_copied, base + T + 1)
                        pe.wait_ge(s_k_copied, base + T + 1)
                    elif not is_tile(t, 1):
                        pe.wait_ge(s_sub_ready, L * T + t - 1)
                    for g in range(2):
                        sc = bank[2 * u + g]
                        for j in range(2):
                            if L == 0:
                                pe.matmul(sc[NP * j:NP * j + NP, 0:HH * S], identb[:, NP * j:NP * j + NP],
                                          maskb[:, :, :], start=True, stop=False)
                            mm = pe.matmul(sc[NP * j:NP * j + NP, 0:HH * S], qs[:, u, g, NP * j:NP * j + NP],
                                           KB[:, u, g, :, S * j:S * j + S], start=(L == 1), stop=True)
                    mm.then_inc(s_s_psum, 1)

                def attend(t, u):
                    first = is_tile(t, 0)
                    pe.wait_ge(s_exp_ready, L * T + t + 1)
                    if first:
                        pe.wait_ge(s_v_copied, base + T + 1)
                        if L == 1:
                            pe.wait_ge(s_c_sub, 3)
                    else:
                        pe.wait_ge(s_pt_copied, L * T + t)
                    for p in range(PAIRS):
                        pe.transpose(bank[4 + p // 4][:, 128 * (p % 4):128 * (p % 4) + 128],
                                     P[:, u, 2 * NP * p:2 * NP * (p + 1)], ident[:, :])
                    pe.transpose(bank[5][0:HEADS, 256:384], P[:, u, HEADS * NP:], ident[:, :]).then_inc(s_pt_psum, 1)
                    if not is_tile(t, T - 2, T - 1):
                        scores(t + 2, u)
                    elif L == 1:
                        (cls_transpose if t == T - 2 else cls_output)()
                    if not first:
                        out_turn(t - 1, 1 - u, L)
                    pe.wait_ge(s_pt_copied, L * T + t + 1)
                    pe.wait_ge(s_vc_slot, L * T + t + 1)
                    if not is_tile(t, 0):
                        pe.wait_ge(s_on_ready, L * T + t)
                    for j in range(2):
                        o = bank[6][0:NP, HEADS * VW * j:HEADS * VW * (j + 1)]
                        pe.matmul(o, PT[0:HEADS, u, PAIRS, NP * j:NP * j + NP],
                                  vcs[:, u, j, :], start=True, stop=False)
                        for p in range(PAIRS):
                            mm = pe.matmul(o[:, 2 * VW * p:2 * VW * p + 2 * VW], PT[:, u, p, NP * j:NP * j + NP],
                                           VB[:, 2 * t + j, p].rearrange("p a b -> p (a b)"), start=False, stop=(p == PAIRS - 1))
                    mm.then_inc(s_o_psum, 1)
                    if not first:
                        project(t - 1, 1 - u, L)

                def project_cls():
                    pe.wait_ge(s_cls_otc, L + 1)
                    both_halves((bank[7], bank[6])[L][0:B, 256:256 + C], lambda g: OTc[:, g, :], lambda g: wproj[L][:, g, :]).then_inc(s_proj_psum, 1)

                def cls_scores():
                    pe.wait_ge(s_c_qcb, 2)
                    pe.wait_ge(s_k_copied, base + T + 1)
                    pe.wait_ge(s_v_copied, base + T + 1)
                    for b in range(B):
                        mm = both_halves(bank[4 + b // 7][0:HEADS, S * (b % 7):S * (b % 7) + S],
                                         lambda g: QCB[:, g, b, :], lambda g: kT[:, g, b, :], bias=False)
                    mm.then_inc(s_c_s, 1)

                def cls_transpose():
                    pe.wait_ge(s_c_p, 1)
                    pe.wait_ge(s_sub_ready, L * T + T - 1)
                    for b in range(B):
                        mm = pe.transpose(bank[0][0:S, HEADS * b:HEADS * b + HEADS], Pc[:, b, :], ident[0:HEADS, 0:HEADS])
                    mm.then_inc(s_c_pt, 1)

                def cls_output():
                    pe.wait_ge(s_c_ptc, 1)
                    pe.wait_ge(s_sub_ready, L * T + T)
                    pe.wait_ge(s_vn_loaded, 16)
                    pe.wait_ge(s_vn_copied, T)
                    parts = [(g, b) for g in range(2) for b in range(B)]
                    n = len(parts) // (ROUTED + 1)
                    for k in range(ROUTED + 1):
                        for g, b in parts[k * n:(k + 1) * n]:
                            c0 = (g * B + b) * HEADS
                            mm = pe.matmul(bank[2][0:HC, c0:c0 + HEADS], VN[:, b, HC * g:HC * g + HC], PcT[:, b, :],
                                           start=True, stop=True)
                        if k == 0:
                            pe.wait_ge(s_pt_copied, 2 * T)
                            pe.wait_ge(s_ld_ffn, 32)
                            turn(LN_TWO, 0, 0)
                        elif k < ROUTED:
                            route(k - 1, (k - 1) % 2)
                    mm.then_inc(s_c_o, 1)
                    route(ROUTED - 1, (ROUTED - 1) % 2)

                pe.wait_ge(s_xt_ready, xt_at(n, T - 1))
                if L == 1:
                    cls_scores()
                scores(0, 0)
                scores(1, 1)
                if L == 0:
                    project_cls()
                in_pairs(pe, attend)
                if L == 0:
                    turn(LN_ONE, CLS, 0)

            route(ROUTED, ROUTED % 2)
            out_turn(T - 1, 1, 1)
            route(ROUTED + 1, (ROUTED + 1) % 2)
            project(T - 1, 1, 1)
            project_cls()
            for t in range(ROUTED + 2, T + 1):
                if t == T - 1:
                    pe.wait_ge(s_cls_otc, 2)
                route(t, t % 2)

            pe.wait_ge(s_picked_ready, 1)
            pe.wait_ge(s_lg_copied, 4)
            pe.matmul(bank[0][:, 0:(T + 1) * E], tri[:, :], picked[:, :, :],
                      start=True, stop=False)
            for t in range(T):
                pe.matmul(bank[0][:, (t + 1) * E:(T + 1) * E], ones128[:, :], bcast(picked[:, t, :], 1, T - t),
                          start=False, stop=(t == T - 1))
            pe.matmul(bank[1][:, 0:(T + 1) * E], ones128[:, :], picked[:, :, :], start=True, stop=True).then_inc(s_rank_psum, 1)

            def gates_turned(t, u):
                r = rows_of(t)
                if t > 1:
                    pe.wait_ge(s_gt_copied, t - 1)
                pe.transpose(bank[6 - 4 * u][0:E, 0:r], gate[0:r, t, :], ident[0:r, 0:r]).then_inc(s_gt_psum, 1)

            def bias_out(t, u):
                r = rows_of(t)
                if t < T:
                    gates_turned(t + 1, 1 - u)
                pe.wait_ge(s_gt_copied, t + 1)
                if t > 1:
                    pe.wait_ge(s_b2_added, t - 1)
                pe.matmul(bank[7 - 4 * u][0:r, 0:C], gateT[:, u, 0:r], b2[:, :], start=True, stop=True).then_inc(s_b2_psum, 1)

            pe.wait_ge(s_gate_ready, len(SPANS))
            gates_turned(0, 0)
            for t in range(T + 1):
                bias_out(t, t % 2)

            def turn_slots(t, u):
                pe.wait_ge(xg_loaded[u], 8 * (t - u) + 16)
                pe.wait_ge(s_xt_ready, xt_at(LN_TWO, T) + t)
                for g in range(2):
                    mm = pe.transpose(bank[5][0:HC, 128 * g:128 * g + 128], XG[:, u, HC * g:HC * g + HC], ident[:, :])
                mm.then_inc(s_xt_psum, 1)

            def expert_of(t):
                return pe.value_load(owner[0:1, bass.ds(t, 1)], min_val=0, max_val=E - 1)

            def up(t, u):
                e = expert_of(t)
                pe.wait_ge(s_xt_ready, xt_at(LN_TWO, T) + t + 1)
                if is_tile(t, 0):
                    pe.wait_ge(s_rank_copied, 1)
                    pe.wait_ge(s_total_copied, 1)
                else:
                    pe.wait_ge(s_hid_ready, t)
                for n in range(2):
                    mm = both_halves(bank[n][:, 0:HID // 2], lambda g: XT[:, u, g, :],
                                     lambda g: w1r[:, bass.ds(e, 1), g, n * HID // 2:(n + 1) * HID // 2])
                mm.then_inc(s_up_psum, 1)

            def turn_hidden(t, u):
                pe.wait_ge(s_hid_ready, t + 1)
                if not is_tile(t, 0):
                    pe.wait_ge(s_hT_ready, t)
                for m in range(KP):
                    mm = pe.transpose(bank[2 + m // 4][:, 128 * (m % 4):128 * (m % 4) + 128], hid[:, u, 128 * m:128 * m + 128], ident[:, :])
                mm.then_inc(s_th_psum, 1)

            def down(t, u):
                e = expert_of(t)
                pe.wait_ge(s_hT_ready, t + 1)
                if not is_tile(t, 0):
                    pe.wait_ge(s_ys_ready, t)
                for m in range(KP):
                    mm = pe.matmul(bank[4][:, 0:C], hT[:, u, m, :], w2r[:, bass.ds(e, 1), m, :], start=(m == 0), stop=(m == KP - 1))
                mm.then_inc(s_y_psum, 1)

            def expert(t, u):
                first = is_tile(t, 0)
                if not first:
                    turn_hidden(t - 1, 1 - u)
                up(t, u)
                if not is_tile(t, MT - 1):
                    turn_slots(t + 1, 1 - u)
                if not first:
                    down(t - 1, 1 - u)

            pe.wait_ge(s_owner_ready, 1)
            pe.wait_ge(s_ld_w1, 16 * E)
            pe.wait_ge(s_ld_w2, 16 * E)
            turn_slots(0, 0)
            in_pairs(pe, expert, MT)
            turn_hidden(MT - 1, (MT - 1) % 2)
            down(MT - 1, (MT - 1) % 2)

        @block.vector
        def _(dve):
            def stats(n, t, s, src):
                r = rows_of(t)
                at = ln_at(n, t)
                own_wait(dve)
                dve.bn_stats(stat[0:r, 0, :], src).then_inc(s_stat_ready, 1)
                if not is_tile(slot_before(n, t), 0):
                    dve.wait_ge(s_veps_ready, slot_before(n, t))
                dve.wait_ge(s_stat_ready, at)
                own_wait(dve)
                dve.bn_aggr(mvs[0:r, s, :], stat[0:r, 0, :]).then_inc(s_mv_ready, 1)

            def normed(n, t, out, src):
                r = rows_of(t)
                dve.wait_ge(s_rstd_ready, ln_at(n, t))
                return dve.tensor_scalar(out, src, mean[0:r, n, t], rstd[0:r, n, t], ALU.subtract, ALU.mult)

            def router_norm(t):
                r = rows_of(t)
                normed(LN_TWO, t, XA[0:r, t, 0:C], U[0:r, t, :]).then_inc(s_xn_ready, 1)

            def to_slot(n, t, u, src):
                at = xt_at(n, t)
                if not (n == LN_TOK and is_tile(t, 0, 1)):
                    dve.wait_ge(s_xt_psum, at - 2)
                normed(n, t, XN[0:rows_of(t), u, :], src).then_inc(s_xn_ready, 1)

            dve.wait_ge(s_m_q, 1)
            dve.tensor_copy(qm[:, 0:HH, :], bank[0][0:HD, 0:HH * NP]).then_inc(s_m_qc, 1)
            dve.tensor_copy(qm[:, HH:HEADS, :], bank[1][0:HD, 0:HH * NP]).then_inc(s_m_qc, 1)
            dve.wait_ge(s_m_k, 1)
            dve.tensor_copy(km[:, :], bank[2][0:HD, 0:NP]).then_inc(s_m_qc, 1)
            dve.tensor_copy(VM[0:NP, 0, 0:HD], bank[2][0:NP, NP:NP + HD])
            dve.tensor_copy(VM[NP:128, 1, 0:HD], bank[2][NP:128, NP:NP + HD]).then_inc(s_m_qc, 1)
            dve.wait_ge(s_m_s, 1)
            for g in range(2):
                dve.reduce_max(mx[0:NP, 0, HH * g:HH * g + HH], bank[3 + g][0:NP, 0:HH * NP].rearrange("p (h j) -> p h j", h=HH),
                               AX_X).then_inc(s_m_max, 1)
            dve.wait_ge(s_m_max, 2)
            for g in range(2):
                dve.tensor_tensor(weights(0, 0, NP)[:, HH * g:HH * g + HH, :], bank[3 + g][0:NP, 0:HH * NP].rearrange("p (h j) -> p h j", h=HH),
                                  bcast(mx[0:NP, 0, HH * g:HH * g + HH], 2, NP), ALU.subtract).then_inc(s_m_sub, 1)
            dve.wait_ge(s_m_t, 1)
            dve.tensor_copy(PT[:, 0, 0:PAIRS, 0:NP], bank[5][:, 0:PAIRS * NP].rearrange("p (a b) -> p a b", a=PAIRS)).then_inc(s_m_tc, 1)
            dve.wait_ge(s_m_o, 1)
            o = bank[6][0:NP, 0:HEADS * VW].rearrange("p (h v) -> p h v", h=HEADS)
            dve.reciprocal(rec[:, 0, 0:HEADS], o[:, :, HD]).then_inc(s_m_rec, 1)
            dve.wait_ge(s_m_rec, 1)
            dve.tensor_tensor(ON[:, 0, 0].rearrange("p (h v) -> p h v", h=HEADS), o[:, :, 0:HD],
                              bcast(rec[:, 0, 0:HEADS], 2, HD), ALU.mult).then_inc(s_m_norm, 1)
            dve.wait_ge(s_m_ot, 1)
            dve.tensor_copy(OT[0:HC, 0].rearrange("p g (a b) -> p g a b", a=2),
                            bcast(bank[5][0:HC, 0:2 * NP].rearrange("p (g b) -> p g b", g=2), 2, 2)).then_inc(s_m_otc, 1)
            dve.wait_ge(s_m_md, 1)
            dve.tensor_copy(MD[:, :], bank[6][:, 0:C]).then_inc(s_m_mdc, 1)
            dve.wait_ge(s_m_mdc, 1)

            def z_of(t, u):
                dve.wait_ge(s_tok_ready, t + 1)
                dve.tensor_tensor(H[:, t, :], bank[7][:, 0:C], MD[:, :], ALU.add).then_inc(s_z_ready, 1)
                dve.wait_ge(s_z_ready, t + 1)
                stats(LN_TOK, t, u, H[:, t, :])
                to_slot(LN_TOK, t, u, H[:, t, :])

            def mixer(t, u):
                dve.wait_ge(s_silu_ready, t + 1)
                dve.wait_ge(s_up3, t + 1)
                if not is_tile(t, 0, 1):
                    dve.wait_ge(s_down_ready, t - 1)
                dve.tensor_tensor(gT[:, u, 0:4, :], bank[2][:, :], silu[:, u, 0:4, :], ALU.mult)
                dve.tensor_tensor(gT[:, u, 4:6, :], bank[3][:, 0:256], silu[:, u, 4:6, :], ALU.mult).then_inc(s_g_ready, 1)
                if not is_tile(t, T - 2, T - 1):
                    z_of(t + 2, u)
                if is_tile(t, T - 1):
                    to_slot(LN_ATT, CLS, 0, H[0:B, CLS, :])
                    to_slot(LN_ATT, 0, 1, H[:, 0, :])
                dve.wait_ge(s_down_ready, t + 1)
                dve.tensor_tensor(H[:, t, :], bank[6][:, 0:C], H[:, t, :], ALU.add).then_inc(s_res_ready, 1)
                dve.wait_ge(s_res_ready, t + 1)
                stats(LN_ATT, t, 3 - u, H[:, t, :])

            dve.wait_ge(s_ld_cls, 16)
            stats(LN_ATT, CLS, 2, H[0:B, CLS, :])
            z_of(0, 0)
            z_of(1, 1)
            in_pairs(dve, mixer)
            dve.wait_ge(s_ld_tables, 16 * N_TABLES)
            dve.tensor_copy(XA[:, :, C], out_row[:, :]).then_inc(s_rows_written, 1)

            def best(t):
                r = rows_of(t)
                dve.max(mx8[0:r, t, :], lg[0:r, t, :]).then_inc(s_mx8_ready, 1)
                dve.wait_ge(s_mx8_ready, t + 1)
                dve.max_index(ix8[0:r, t, :], mx8[0:r, t, :], lg[0:r, t, :]).then_inc(s_ix8_ready, 1)

            def logits_out(k):
                t0, t1 = LG_TILES[k]
                dve.wait_ge(s_lg_psum, t1)
                n = (min(t1, T) - t0) * E
                dve.tensor_copy(lg[:, t0:min(t1, T), :], bank[k][:, 0:n]).then_inc(s_lg_copied, 1)
                if t1 > T:
                    dve.tensor_copy(lg[0:B, T, :], bank[k][0:B, n:n + E]).then_inc(s_lg_copied, 1)
                dve.wait_ge(s_lg_copied, k + 2 if t1 > T else k + 1)
                for t in range(t0, t1):
                    best(t)

            def outer(t, u):
                r = rows_of(t)
                normed(LN_OUTER, t, U[0:r, t, :], H[0:r, t, :]).then_inc(s_z_ready, 1)
                dve.wait_ge(s_z_ready, T + nth(t) + 1)
                stats(LN_ONE, t, 2 + u, U[0:r, t, :])

            for L, n in ((0, LN_ATT), (1, LN_ONE)):
                base = L * (T + 1)
                X = H if L == 0 else U

                def qkv(t, u):
                    cls = is_tile(t, CLS)
                    at = base + nth(t) + 1
                    r = rows_of(t)
                    qb, vb = bank[u], bank[4 + 2 * u]
                    dve.wait_ge(s_qk_psum, at)
                    if cls and L == 1:
                        dve.wait_ge(s_q_slot, T)
                    dve.tensor_copy(qT[:, :, tile_cols(t)], qb[0:HC, 0:256].rearrange("p (a b) -> p a b", a=2)[:, :, 0:r])\
                        .then_inc(s_q_copied, 1)
                    if not is_tile(t, T - 2, T - 1):
                        nxt = 1 if cls else t + 2
                        to_slot(n, nxt, u, X[:, nxt, :])
                    dve.wait_ge(s_v_psum, at)
                    if cls:
                        if L == 0:
                            dve.wait_ge(s_ld_attn, 16 * 6)
                            dve.tensor_copy(OTc[0:HC, :, :], vb[0:HC, 256:256 + 2 * B].rearrange("p (a b) -> p a b", a=2))\
                                .then_inc(s_cls_otc, 1)
                        else:
                            dve.wait_ge(s_o_psum, T)
                            dve.wait_ge(s_vcb_loaded, 16 * HEADS)
                            dve.wait_ge(s_x_zeroed, 16 * FILLS)
                        dve.tensor_copy(VC[:, :], vb[0:B, 0:C]).then_inc(s_v_copied, 1)
                    else:
                        v = vb[:, 0:2 * C].rearrange("p (j m a d) -> p j m a d", j=2, m=PAIRS, a=2)
                        dve.tensor_copy(VB[0:NP, bass.ts(t, 2), :, 0, 0:HD], v[0:NP, :, :, 0, :])
                        for j in range(2):
                            mm = dve.tensor_copy(VB[NP:128, 2 * t + j, :, 1, 0:HD], v[NP:128, 1 - j, :, 1, :])
                        if L == 1:
                            dve.tensor_copy(VN[0:NP, bass.ts(t, 2), :], vb[0:NP, 0:2 * C]).then_inc(s_vn_copied, 1)
                            dve.wait_ge(s_vn_copied, t + 1)
                            dve.sem_inc(s_v_copied, 1)
                        else:
                            mm.then_inc(s_v_copied, 1)

                qkv(CLS, 0)
                if L == 1:
                    outer(T - 1, 0)
                in_pairs(dve, lambda t, u: qkv(t, 1 - u), tail=4)

                def shifted(t, u):
                    dve.wait_ge(s_s_psum, L * T + t + 1)
                    for g in range(2):
                        mm = dve.reduce_max(mx[:, u, HH * g:HH * g + HH], bank[2 * u + g][:, 0:HH * S].rearrange("p (h j) -> p h j", h=HH), AX_X)
                    mm.then_inc(s_max_ready, 1)
                    dve.wait_ge(s_max_ready, L * T + t + 1)
                    if not is_tile(L * T + t, 0, 1):
                        dve.wait_ge(s_pt_psum, L * T + t - 1)
                    for g in range(2):
                        sc = bank[2 * u + g][:, 0:HH * S].rearrange("p (h j) -> p h j", h=HH)
                        m = mx[:, u, HH * g:HH * g + HH]
                        dve.tensor_tensor(weights(u, 0, 128)[:, HH * g:HH * g + HH, :], sc[:, :, 0:NP], bcast(m, 2, NP), ALU.subtract)
                        c0 = HEADS * NP + HH * g
                        mm = dve.tensor_tensor(P[:, u, c0:c0 + HH], sc[:, :, NP], m, ALU.subtract)
                    mm.then_inc(s_sub_ready, 1)

                def residual(t, u):
                    r = rows_of(t)
                    dve.wait_ge(s_proj_psum, res_at(L, t) - T)
                    pb = bank[6] if L == 1 and is_tile(t, CLS) else bank[7]
                    dve.tensor_tensor(X[0:r, t, :], pb[0:r, 256:256 + C], X[0:r, t, :], ALU.add).then_inc(s_res_ready, 1)
                    dve.wait_ge(s_res_ready, res_at(L, t))
                    stats(LN_OUTER if L == 0 else LN_TWO, t, u, X[0:r, t, :])

                def attend(t, u):
                    first = is_tile(t, 0)
                    if not is_tile(t, T - 1):
                        shifted(t + 1, 1 - u)
                    if L == 0 and first:
                        outer(CLS, 0)
                    elif L == 0 and not is_tile(t, 1):
                        outer(t - 2, 1 - u)
                    if L == 0 and is_tile(t, T - 1):
                        to_slot(LN_ONE, CLS, 0, U[0:B, CLS, :])
                        to_slot(LN_ONE, 0, 1, U[:, 0, :])
                    if L == 1:
                        if is_tile(t, 1):
                            cls_weights()
                        elif not first:
                            router_norm(t - 2)
                        if is_tile(t, T - 2):
                            cls_turned()
                        if is_tile(t, T - 1):
                            cls_out()
                    dve.wait_ge(s_o_psum, L * T + t + 1)
                    o = bank[6][0:NP, 0:2 * HEADS * VW].rearrange("p (h v) -> p h v", v=VW)
                    dve.reciprocal(rec[:, u, :], o[:, :, HD]).then_inc(s_rec_ready, 1)
                    dve.wait_ge(s_rec_ready, L * T + t + 1)
                    dve.tensor_tensor(ON[:, u].rearrange("p j (h v) -> p (j h) v", v=HD), o[:, :, 0:HD],
                                      bcast(rec[:, u, :], 2, HD), ALU.mult).then_inc(s_on_ready, 1)
                    if not first:
                        residual(t - 1, u if L == 0 else 1 - u)

                spans = ((0, 7), (7, 14), (14, 16))
                sc = [bank[4 + i][0:HEADS, 0:S * (b1 - b0)].rearrange("p (b j) -> p b j", j=S) for i, (b0, b1) in enumerate(spans)]

                def cls_shifted():
                    dve.wait_ge(s_c_s, 1)
                    for i, (b0, b1) in enumerate(spans):
                        dve.reduce_max(mxc[:, b0:b1], sc[i], AX_X).then_inc(s_c_max, 1)
                    dve.wait_ge(s_c_max, 3)
                    for i, (b0, b1) in enumerate(spans):
                        dve.tensor_tensor(Pc[:, b0:b1, :], sc[i], bcast(mxc[:, b0:b1], 2, S), ALU.subtract).then_inc(s_c_sub, 1)

                def cls_weights():
                    dve.wait_ge(s_c_exp, 1)
                    dve.reduce_sum(smc[:, :], Pc[:, :, :], AX_X).then_inc(s_c_sum, 1)
                    dve.wait_ge(s_c_sum, 1)
                    dve.reciprocal(mxc[:, :], smc[:, :]).then_inc(s_c_rec, 1)
                    dve.wait_ge(s_c_rec, 1)
                    dve.tensor_tensor(Pc[:, :, :], Pc[:, :, :], bcast(mxc[:, :], 2, S), ALU.mult).then_inc(s_c_p, 1)

                def cls_turned():
                    dve.wait_ge(s_c_pt, 1)
                    dve.tensor_copy(PcT[:, :, :], bank[0][0:S, 0:B * HEADS]).then_inc(s_c_ptc, 1)

                def cls_out():
                    dve.wait_ge(s_c_o, 1)
                    for g in range(2):
                        dve.tensor_tensor(OCm[:, g], bank[2][0:HC, g * B * HEADS:(g + 1) * B * HEADS].rearrange("p (b h) -> p b h", b=B),
                                          bcast(head_mask[:, g, :], 1, B), ALU.mult).then_inc(s_c_om, 1)
                    dve.wait_ge(s_c_om, 2)
                    dve.reduce_sum(OTc[0:HC, :, :], OCm[:, :, :, :], AX_X).then_inc(s_cls_otc, 1)

                if L == 1:
                    cls_shifted()
                shifted(0, 0)
                if L == 0:
                    residual(CLS, 0)
                in_pairs(dve, attend)
                if L == 0:
                    outer(T - 2, 1)
                if L == 1:
                    router_norm(T - 2)
                    logits_out(0)
                residual(T - 1, 0 if L == 0 else 1)
                if L == 1:
                    residual(CLS, 0)
                    router_norm(T - 1)
                    router_norm(CLS)

            def chosen(k):
                r, ts = SPANS[k]
                nt = ts.stop - ts.start
                dve.tensor_copy(ixf[0:r, ts, :], ix8[0:r, ts, 0:TOP]).then_inc(s_r1, 1)
                dve.tensor_tensor(e2[0:r, ts, :], mx8[0:r, ts, 1:2], mx8[0:r, ts, 0:1], ALU.subtract).then_inc(s_r2, 1)
                dve.wait_ge(s_r1, k + 1)
                for j in range(TOP):
                    dve.tensor_tensor(hot[0:r, j, ts, :], bcast(iota8[0:r, :], 1, nt), ixf[0:r, ts, j:j + 1].to_broadcast([r, nt, E]),
                                      ALU.is_equal).then_inc(s_hot_ready, 1)

            def gates_of(k):
                r, ts = SPANS[k]
                nt = ts.stop - ts.start
                dve.wait_ge(s_r3, k + 1)
                dve.tensor_scalar(g12[0:r, ts, 0:1], e2[0:r, ts, :], 1.0, None, ALU.add).then_inc(s_r4, 1)
                dve.wait_ge(s_r4, k + 1)
                dve.reciprocal(g12[0:r, ts, 0:1], g12[0:r, ts, 0:1]).then_inc(s_r5, 1)
                dve.wait_ge(s_r5, k + 1)
                dve.tensor_tensor(g12[0:r, ts, 1:2], e2[0:r, ts, :], g12[0:r, ts, 0:1], ALU.mult).then_inc(s_r6, 1)
                dve.wait_ge(s_r6, k + 1)
                for j, out in enumerate((gate1, gate2)):
                    dve.tensor_tensor(out[0:r, ts, :], hot[0:r, j, ts, :], g12[0:r, ts, j:j + 1].to_broadcast([r, nt, E]),
                                      ALU.mult).then_inc(s_gates2, 1)
                dve.wait_ge(s_gates2, 2 * k + 2)
                dve.tensor_tensor(gate[0:r, ts, :], gate1[0:r, ts, :], gate2[0:r, ts, :], ALU.add).then_inc(s_gate_ready, 1)

            dve.wait_ge(s_hot_cleared, 3)
            for k in range(1, len(LG_TILES)):
                if k == 2:
                    dve.wait_ge(s_ix8_ready, T - 1)
                    chosen(0)
                    dve.wait_ge(s_hot_ready, TOP)
                    gates_of(0)
                logits_out(k)
            dve.wait_ge(s_ix8_ready, T + 1)
            chosen(1)
            chosen(2)
            dve.wait_ge(s_hot_ready, 3 * TOP)
            dve.tensor_tensor(picked[:, :, :], hot[:, 0], hot[:, 1], ALU.add).then_inc(s_picked_ready, 1)
            gates_of(1)
            gates_of(2)
            dve.wait_ge(s_rank_psum, 1)
            dve.tensor_copy(rank[:, :, :], bank[0][:, 0:(T + 1) * E]).then_inc(s_rank_copied, 1)
            dve.reduce_sum(total[:, :], bank[1][:, 0:(T + 1) * E].rearrange("p (t e) -> p e t", e=E), AX_X).then_inc(s_total_copied, 1)
            dve.wait_ge(s_total_copied, 1)
            dve.tensor_tensor(full[:, :, :], bcast(total[:, :], 2, T + 2), bcast(steps[:, :], 1, E), ALU.is_gt).then_inc(s_full_ready, 1)
            dve.wait_ge(s_full_ready, 1)
            dve.reduce_sum(tiles[:, :], full[:, :, :], AX_X).then_inc(s_tiles_ready, 1)
            dve.wait_ge(s_tiles_ready, 1)
            dve.tensor_tensor(ahead[:, :, :], before[:, :, :], bcast(tiles[:, :], 1, E), ALU.mult).then_inc(s_ahead_ready, 1)
            dve.wait_ge(s_ahead_ready, 1)
            dve.reduce_sum(first[:, :], ahead[:, :, :], AX_X).then_inc(s_first_ready, 1)
            dve.wait_ge(s_first_ready, 1)
            dve.scalar_tensor_tensor(out=rank[:, :, :], in0=bcast(first[:, :], 1, T + 1), scalar=128.0, in1=rank[:, :, :],
                                     op0=ALU.mult, op1=ALU.add).then_inc(s_rank_copied, 1)
            dve.wait_ge(s_rank_copied, 2)
            for j in range(TOP):
                dve.tensor_tensor(place[:, j], hot[:, j], rank[:, :, :], ALU.mult).then_inc(s_place_ready, 1)
            dve.wait_ge(s_place_ready, TOP)
            dve.reduce_sum(slotf[:, :, :], place[:, :, :, :], AX_X).then_inc(s_slot_f, 1)
            dve.wait_ge(s_slot_f, 1)
            dve.tensor_copy(slot[:, :, :], slotf[:, :, :]).then_inc(s_slot_ready, 1)
            dve.tensor_tensor(last[:, :], first[:, :], tiles[:, :], ALU.add).then_inc(s_last_ready, 1)
            dve.wait_ge(s_last_ready, 1)
            dve.tensor_tensor(past[:, :, :], bcast(last[:, :], 1, MT), bcast(tile_no[:, :], 2, E), ALU.is_le).then_inc(s_past_ready, 1)
            dve.wait_ge(s_past_ready, 1)
            dve.reduce_sum(ownerf[:, :], past[0:1, :, :], AX_X).then_inc(s_owner_f, 1)
            dve.tensor_tensor(own[:, :, :], bcast(first[:, :], 1, MT), bcast(tile_no[:, :], 2, E), ALU.is_le).then_inc(s_own_first, 1)
            dve.wait_ge(s_owner_f, 1)
            dve.tensor_scalar(ownerf[:, :], ownerf[:, :], float(E - 1), None, ALU.min).then_inc(s_owner_m, 1)
            dve.wait_ge(s_owner_m, 1)
            dve.tensor_copy(owner[:, :], ownerf[:, :]).then_inc(s_owner_ready, 1)
            dve.wait_ge(s_own_first, 1)
            dve.tensor_tensor(own[:, :, :], own[:, :, :], past[:, :, :], ALU.subtract).then_inc(s_own_ready, 1)
            def gates_out(t, u):
                r = rows_of(t)
                if t > 1:
                    dve.wait_ge(s_b2_psum, t - 1)
                dve.wait_ge(s_gt_psum, t + 1)
                dve.tensor_copy(gateT[:, u, 0:r], bank[6 - 4 * u][0:E, 0:r]).then_inc(s_gt_copied, 1)
            gates_out(0, 0)
            for t in range(T + 1):
                r = rows_of(t)
                if t < T:
                    gates_out(t + 1, (t + 1) % 2)
                dve.tensor_tensor(H[0:r, t, :], H[0:r, t, :], U[0:r, t, :], ALU.add).then_inc(s_own_first, 1)
                dve.wait_ge(s_own_first, 2 + t)
                dve.wait_ge(s_b2_psum, t + 1)
                dve.tensor_tensor(H[0:r, t, :], bank[7 - 4 * (t % 2)][0:r, 0:C], H[0:r, t, :], ALU.add).then_inc(s_b2_added, 1)
            def hidden_out(t, u):
                dve.wait_ge(s_th_psum, t + 1)
                if not is_tile(t, 0, 1):
                    dve.wait_ge(s_y_psum, t - 1)
                dve.tensor_copy(hT[:, u, 0:4, :], bank[2][:, :])
                dve.tensor_copy(hT[:, u, 4:6, :], bank[3][:, 0:256]).then_inc(s_hT_ready, 1)

            def numbers(t, u):
                dve.wait_ge(s_xt_psum, xt_at(LN_TWO, T) + t + 1)
                if not is_tile(t, 0, 1):
                    dve.wait_ge(s_ys_ready, t - 1)
                own_wait(dve)
                dve.tensor_copy(meta[:, u, :], XG[:, u, C:C + 1])
                dve.tensor_tensor(picks[:, u, :], XG[:, u, C + 1:], own[:, t, :], ALU.mult).then_inc(s_picks_ready, 1)
                dve.wait_ge(s_picks_ready, t + 1)
                dve.reduce_sum(weight[:, u, :], picks[:, u, :].unsqueeze(1), AX_X).then_inc(s_meta_ready, 1)

            def y_out(t, u):
                dve.wait_ge(s_meta_ready, t + 1)
                dve.wait_ge(s_y_psum, t + 1)
                if not is_tile(t, 0, 1):
                    dve.wait_ge(s_added, 16 * (t - 1))
                own_wait(dve)
                dve.tensor_copy(to_row[:, u, :], meta[:, u, :])
                dve.tensor_scalar(YS[:, u, :], bank[4][:, 0:C], weight[:, u, :], None, ALU.mult).then_inc(s_ys_ready, 1)

            def expert(t, u):
                hidden_out(t, u)
                y_out(t, u)
                if not is_tile(t, MT - 2, MT - 1):
                    numbers(t + 2, u)
            dve.wait_ge(s_own_ready, 1)
            numbers(0, 0)
            numbers(1, 1)
            in_pairs(dve, expert, MT)

        @block.scalar
        def _(act):
            act.wait_ge(s_m_sub, 2)
            act.activation(P[0:NP, 0, 0:HEADS * NP], P[0:NP, 0, 0:HEADS * NP], ACT.Exp, scale=SCALE).then_inc(s_m_exp, 1)

            def turned(n, t, u, cols):
                r = rows_of(t)
                act.wait_ge(s_xt_psum, xt_at(n, t))
                for g in range(2):
                    src = turn_bank(n, u)[0:HC, 128 * g:128 * g + r]
                    dst = XT[0:HC, u, g, 0:r]
                    if cols is None:
                        a = act.activation(dst, src, ACT.Copy)
                    else:
                        a = act.activation(dst, src, ACT.Identity, bias=ln_cols[:, cols, 1, g:g + 1], scale=ln_cols[:, cols, 0, g:g + 1])
                a.then_inc(s_xt_ready, 1)

            act.wait_ge(s_ld_const, 16 * N_CONST)
            turned(LN_TOK, 0, 0, 0)

            def mixer(t, u):
                act.wait_ge(s_up1, t + 1)
                if not is_tile(t, 0, 1):
                    act.wait_ge(s_g_ready, t - 1)
                act.activation(silu[:, u, 0:4, :], bank[0][:, :], ACT.Silu)
                act.activation(silu[:, u, 4:6, :], bank[1][:, 0:256], ACT.Silu).then_inc(s_silu_ready, 1)
                if not is_tile(t, T - 1):
                    turned(LN_TOK, t + 1, 1 - u, 0)
                else:
                    turned(LN_ATT, CLS, 0, None)
            in_pairs(act, mixer)

            def route(t, u):
                if t > 1:
                    act.wait_ge(s_lg_psum, t - 1)
                turned(LN_TWO, t, u, 2)

            def turned_out(t, u, L):
                act.wait_ge(s_ot_psum, L * T + t + 1)
                if not is_tile(t, 0, 1):
                    act.wait_ge(s_proj_psum, res_at(L, t) - T - 2)
                act.activation(OT[0:HC, u], bank[7][0:HC, 0:256].rearrange("p (a c) -> p a c", a=2), ACT.Copy).then_inc(s_ot_copied, 1)

            for L, n in ((0, LN_ATT), (1, LN_ONE)):
                base = L * (T + 1)
                cols = None if L == 0 else 1

                def qkv(t, u):
                    cls = is_tile(t, CLS)
                    at = base + nth(t) + 1
                    if not is_tile(t, T - 1):
                        if not (base == 0 and cls):
                            act.wait_ge(s_v_psum, at - 1)
                        turned(n, 0 if cls else t + 1, 1 - u, cols)
                    act.wait_ge(s_qk_psum, at)
                    if L == 1 and cls:
                        for u2 in range(2):
                            act.wait_ge(kb_loaded[u2], 16 * HH * (T // 2))
                    src = bank[2 + u][0:HC, 0:256].rearrange("p (a c) -> p a c", a=2)
                    if cls:
                        act.activation(kT[:, :, :, NP], src[:, :, 0:B], ACT.Copy).then_inc(s_k_copied, 1)
                    else:
                        for g in range(2):
                            a = act.activation(kT[:, g, bass.ts(t, 2), 0:NP], src[:, g, :].rearrange("p (j c) -> p j c", j=2), ACT.Copy)
                        a.then_inc(s_k_copied, 1)
                if L == 0:
                    act.wait_ge(s_up3, T)
                else:
                    turned_out(T - 1, 1, 0)
                qkv(CLS, 0)
                in_pairs(act, lambda t, u: qkv(t, 1 - u))

                def exponentials(t, u):
                    act.wait_ge(s_sub_ready, L * T + t + 1)
                    act.activation(P[:, u], P[:, u], ACT.Exp, scale=SCALE).then_inc(s_exp_ready, 1)

                def attend(t, u):
                    act.wait_ge(s_pt_psum, L * T + t + 1)
                    if not is_tile(L * T + t, 0, 1):
                        act.wait_ge(s_o_psum, L * T + t - 1)
                    act.activation(PT[:, u, 0:4, :], bank[4][:, :], ACT.Copy)
                    act.activation(PT[:, u, 4:6, :], bank[5][:, 0:256], ACT.Copy)
                    act.activation(PT[0:HEADS, u, 6, :], bank[5][0:HEADS, 256:384], ACT.Copy).then_inc(s_pt_copied, 1)
                    if L == 1 and is_tile(t, T - 1):
                        for k in range(ROUTED + 1):
                            route(k, k % 2)
                    if not is_tile(t, 0):
                        turned_out(t - 1, 1 - u, L)
                    if not is_tile(t, T - 1):
                        exponentials(t + 1, 1 - u)

                exponentials(0, 0)
                if L == 1:
                    act.wait_ge(s_c_sub, 3)
                    act.activation(Pc[:, :, :], Pc[:, :, :], ACT.Exp, scale=SCALE).then_inc(s_c_exp, 1)
                in_pairs(act, attend)
                if L == 0:
                    turned(LN_ONE, CLS, 0, 1)
                else:
                    route(ROUTED + 1, (ROUTED + 1) % 2)
                    turned_out(T - 1, 1, L)
            for t in range(ROUTED + 2, T + 1):
                route(t, t % 2)
            for k, (r, ts) in enumerate(SPANS):
                act.wait_ge(s_r2, k + 1)
                act.activation(e2[0:r, ts, :], e2[0:r, ts, :], ACT.Exp).then_inc(s_r3, 1)

            for t in range(T):
                act.wait_ge(s_b2_added, t + 1)
                for j in range(2):
                    act.dma_start(d["out"][2 * t + j, 1:S, :], H[NP * j:NP * j + NP, t, :]).then_inc(s_out_done, 16)
            act.activation(veps[0:1, 3], mhalf[0:1, :], ACT.Gelu)
            act.wait_ge(s_b2_added, T + 1)
            act.dma_start(d["out"][:, 0, :], H[0:B, CLS, :]).then_inc(s_out_done, 16)

            def slots_turned(t, u):
                act.wait_ge(s_xt_psum, xt_at(LN_TWO, T) + t + 1)
                if is_tile(t, 0, 1):
                    act.wait_ge(s_lg_psum, T + 1)
                else:
                    act.wait_ge(s_up_psum, t - 1)
                for g in range(2):
                    a = act.activation(XT[0:HC, u, g, :], bank[5][0:HC, 128 * g:128 * g + 128], ACT.Identity,
                                       bias=ln_cols[:, 2, 1, g:g + 1], scale=ln_cols[:, 2, 0, g:g + 1])
                a.then_inc(s_xt_ready, 1)

            def expert(t, u):
                act.wait_ge(s_up_psum, t + 1)
                if not is_tile(t, 0, 1):
                    act.wait_ge(s_th_psum, t - 1)
                for n in range(2):
                    a = act.activation(hid[:, u, n * HID // 2:(n + 1) * HID // 2], bank[n][:, 0:HID // 2], ACT.Gelu)
                a.then_inc(s_hid_ready, 1)
                if not is_tile(t, MT - 1):
                    slots_turned(t + 1, 1 - u)
            slots_turned(0, 0)
            in_pairs(act, expert, MT)

        @block.gpsimd
        def _(pool):
            for n, (buf, value) in enumerate(((mhalf[:, :], -0.5), (OT[HC:HC + 1], 1.0), (OTc[HC:HC + 1], 1.0), (XT[HC:HC + 1], 1.0))):
                pool.memset(buf, value).then_inc(s_presets, 1)
                pool.wait_ge(s_presets, n + 1)
            pool.memset(KB[:], 0.0).then_inc(s_kb_zero, 1)
            pool.memset(empty[:, :, :], 0.0).then_inc(s_kb_zero, 1)
            pool.wait_ge(s_kb_zero, 2)
            pool.wait_ge(s_ld_tables, 16 * N_TABLES)
            pool.tensor_copy(empty[:, :, C], spare_row[:, :]).then_inc(s_kb_zero, 1)
            pool.wait_ge(s_kb_zero, 3)
            for k, buf in enumerate((hot, g12, slotf)):
                pool.memset(buf[:], 0.0).then_inc(s_hot_cleared, 1)
                pool.wait_ge(s_hot_cleared, k + 1)

            def inv_std(n, t, s):
                r = rows_of(t)
                at = ln_at(n, t)
                pool.wait_ge(s_mv_ready, at)
                pool.tensor_copy(mean[0:r, n, t], mvs[0:r, s, 0:1]).then_inc(s_mean_ready, 1)
                pool.wait_ge(s_mean_ready, at)
                own_wait(pool)
                pool.tensor_scalar(veps[0:r, s], mvs[0:r, s, 1:2], LN_EPS, None, ALU.add).then_inc(s_veps_ready, 1)
                pool.wait_ge(s_veps_ready, at)
                pool.tensor_tensor(rstd[0:r, n, t], veps[0:r, s], mhalf[0:r, :], ALU.pow).then_inc(s_rstd_ready, 1)
                pool.wait_ge(s_rstd_ready, at)

            def mixer(t, u):
                if not is_tile(t, T - 2, T - 1):
                    inv_std(LN_TOK, t + 2, u)
                inv_std(LN_ATT, t, 3 - u)
            inv_std(LN_ATT, CLS, 2)
            inv_std(LN_TOK, 0, 0)
            inv_std(LN_TOK, 1, 1)
            in_pairs(pool, mixer)
            for L in range(2):
                if L == 1:
                    pool.wait_ge(s_q_copied, T + 2)
                    for g in range(2):
                        pool.tensor_tensor(QCB[:, g], qT[:, g, T * 128:T * 128 + B].unsqueeze(2).to_broadcast([HC, B, HEADS]),
                                           bcast(head_mask[:, g, :], 1, B), ALU.mult).then_inc(s_c_qcb, 1)
                    pool.wait_ge(s_c_qcb, 2)

                def queries(t, u):
                    if is_tile(t, 2):
                        pool.wait_ge(s_q_copied, (L + 1) * (T + 1))
                    elif is_tile(t, 0, 1):
                        pool.wait_ge(s_q_copied, L * (T + 1) + t + 2)
                    if not is_tile(L * T + t, 0, 1):
                        pool.wait_ge(s_s_psum, L * T + t - 1)
                    pool.tensor_copy(qs[:, u], qT[:, :, bass.ts(t, 128)]).then_inc(s_q_slot, 1)
                    pool.wait_ge(s_q_slot, L * T + t + 1)

                def cls_values(t, u):
                    if is_tile(t, 0):
                        pool.wait_ge(s_vcb_loaded, 16 * HEADS * (L + 1))
                    if not is_tile(L * T + t, 0, 1):
                        pool.wait_ge(s_o_psum, L * T + t - 1)
                    pool.tensor_copy(vcs[:, u], VCB[:, bass.ts(t, 2), :]).then_inc(s_vc_slot, 1)
                    pool.wait_ge(s_vc_slot, L * T + t + 1)

                def attend(t, u):
                    if not is_tile(t, T - 3, T - 2, T - 1):
                        queries(t + 3, 1 - u)
                    if not is_tile(t, T - 1):
                        cls_values(t + 1, 1 - u)
                    if L == 0:
                        if is_tile(t, 0):
                            inv_std(LN_OUTER, CLS, 0)
                            inv_std(LN_ONE, CLS, 2)
                        elif not is_tile(t, 1):
                            inv_std(LN_ONE, t - 2, 3 - u)
                        if not is_tile(t, 0):
                            inv_std(LN_OUTER, t - 1, u)
                    elif not is_tile(t, 0):
                        inv_std(LN_TWO, t - 1, 1 - u)

                queries(0, 0)
                queries(1, 1)
                cls_values(0, 0)
                queries(2, 0)
                in_pairs(pool, attend, tail=4)
                if L == 0:
                    inv_std(LN_ONE, T - 2, 3)
                    inv_std(LN_OUTER, T - 1, 0)
                    inv_std(LN_ONE, T - 1, 2)
                else:
                    inv_std(LN_TWO, T - 1, 1)
                    inv_std(LN_TWO, CLS, 0)

            pool.wait_ge(s_slot_ready, 1)
            pool.wait_ge(s_x_zeroed, 16 * FILLS)
            pool.wait_ge(s_xn_ready, xt_at(LN_TWO, T))
            pool.wait_ge(s_rows_written, 1)
            pool.wait_ge(s_gate_ready, len(SPANS))
            for t in range(T + 1):
                r = rows_of(t)
                for j in range(TOP):
                    pool.indirect_dma_start(x_slots, bass.IndirectOffsetOnAxis(slot[0:r, j, t:t + 1], 0), XA[0:r, t, :],
                                            None).then_inc(s_scattered, 16)

            def add_rows(t, u):
                if not is_tile(t, 0):
                    pool.wait_ge(s_added, 16 * t)
                pool.wait_ge(s_ys_ready, t + 1)
                own_wait(pool)
                pool.indirect_dma_start(result, bass.IndirectOffsetOnAxis(to_row[:, u, :], 0), YS[:, u, :], None,
                                        compute_op=ALU.add, bounds_check=B * S - 1, oob_is_err=False).then_inc(s_added, 16)
            pool.wait_ge(s_out_done, 16 * (2 * T + 1))
            result = d["out"].rearrange("b s c -> (b s) c")
            in_pairs(pool, add_rows, MT)


def kernel(x, cls_tok, **w):
    import concourse.bacc as bacc
    from concourse.bass_utils import run_bass_kernel_spmd

    arrays = {f"in_{n}": a for n, a in layout(x, cls_tok, w).items()}
    nc = bacc.Bacc("TRN2", target_bir_lowering=False, num_devices=1)
    d = {n[3:]: nc.dram_tensor(n, a.shape, mybir.dt.from_np(a.dtype), kind="ExternalInput").ap() for n, a in arrays.items()}
    d["out"] = nc.dram_tensor("out", (B, S, C), F32, kind="ExternalOutput").ap()
    build(nc, d)
    return run_bass_kernel_spmd(nc, [arrays], core_ids=[0]).results[0]["out"]


def layout(x, cls_tok, w):
    def halves(a, bias=None, row=False):
        a = np.asarray(a)
        out = np.zeros((HC + int(row or bias is not None), 2, a.shape[1]), np.float32)
        out[0:HC] = a.reshape(2, HC, a.shape[1]).transpose(1, 0, 2)
        if bias is not None:
            out[HC, 1] = np.asarray(bias)
        return out

    def chunks(a):
        a = np.asarray(a)
        return np.ascontiguousarray(a.reshape(KP, 128, a.shape[1]).transpose(1, 0, 2))

    side, patch = 8, 16
    p = np.asarray(x).reshape(B, 3, side, patch, side, patch).transpose(0, 2, 4, 3, 5, 1)
    p = p.reshape(T, 128, KP, 128).transpose(0, 3, 2, 1)

    scales = np.linspace(1.0, 5.0, C // 4)
    seq = np.linspace(-1.0, 1.0, side)[:, None] * scales[None, :] * np.pi
    xs = np.broadcast_to(seq[:, None, :], (side, side, C // 4))
    ys = np.broadcast_to(seq[None, :, :], (side, side, C // 4))
    sin = np.repeat(np.concatenate([np.sin(xs), np.sin(ys)], -1).reshape(NP, C // 2), 2, axis=-1)
    sinT = halves(np.tile(sin.T.astype(np.float32), (1, 2)), row=True)
    sinT[HC] = 1.0

    n = np.arange(128)
    out_row = np.stack([(2 * t + n // NP) * S + 1 + n % NP for t in range(T)] + [np.minimum(n, B - 1) * S], 1)
    i, j = np.arange(128)[:, None] % NP, np.arange(S)[None, :]
    mask = np.where((j <= i) | (j == NP), 0.0, -1e30)
    mask = np.broadcast_to(mask[:, None, :], (128, HH, S)).astype(np.dtype("bfloat16"))
    head_mask = np.zeros((HC, 2, HEADS), np.float32)
    for h in range(HEADS):
        head_mask[HD * (h % HH):HD * (h % HH) + HD, h // HH, h] = 1.0
    vb0 = np.zeros((128, B, PAIRS, 2, VW), np.float32)
    vb0[0:NP, :, :, 0, HD] = 1.0
    vb0[NP:128, :, :, 1, HD] = 1.0
    vcb0 = np.zeros((HEADS, B, HEADS * VW), np.float32)
    for h in range(HEADS):
        vcb0[h, :, VW * h + HD] = 1.0
    cols = np.stack([np.stack([np.asarray(w[n]).reshape(2, HC).T for n in pair], 1) for pair in (
        ("L0_tok_ln_g", "L0_tok_ln_b"), ("L0_ffn_ln1_g", "L0_ffn_ln1_b"), ("L0_ffn_ln2_g", "L0_ffn_ln2_b"))], 1)
    return {
        "patches": np.ascontiguousarray(p),
        "cls": np.ascontiguousarray(np.broadcast_to(np.asarray(cls_tok).reshape(1, C), (B, C))),
        "sinT": sinT.reshape(HC + 1, 2, 2, NP),
        "ident": np.eye(128, dtype=np.float32),
        "identb": np.eye(128).astype(np.dtype("bfloat16")),
        "maskb": np.ascontiguousarray(mask),
        "ones": np.ones((1, 128), np.float32),
        "head_mask": head_mask,
        "iota8": np.broadcast_to(np.arange(E, dtype=np.float32), (128, E)).copy(),
        "tri": np.triu(np.ones((128, 128)), 1).astype(np.dtype("bfloat16")),
        "ones128": np.ones((128, 128)).astype(np.dtype("bfloat16")),
        "steps": np.broadcast_to(128.0 * np.arange(T + 2, dtype=np.float32), (128, T + 2)).copy(),
        "before": np.broadcast_to(np.tril(np.ones((E, E), np.float32), -1), (128, E, E)).copy(),
        "tile_no": np.broadcast_to(np.arange(MT, dtype=np.float32), (128, MT)).copy(),
        "out_row": np.ascontiguousarray(out_row, np.float32),
        "spare_row": (B * S + np.arange(SLOTS // FILLS, dtype=np.float32).reshape(128, -1) % 128),
        "vm0": vb0[:, 0, 0].copy(),
        "vb0": vb0,
        "vcb0": vcb0,
        "ln_cols": np.ascontiguousarray(cols),
        "patch_b": np.asarray(w["L0_tok_patch_b"]).reshape(1, C),
        "w_patch": chunks(w["L0_tok_patch_w"]),
        "wqkv_m": halves(w["L0_tok_wqkv"], w["L0_tok_bqkv"]),
        "wo_m": halves(w["L0_tok_wo"], w["L0_tok_bo"]),
        "w13": halves(np.concatenate([np.asarray(w["L0_tok_w1"]), np.asarray(w["L0_tok_w3"])], 1)),
        "w2t": chunks(w["L0_tok_w2"]),
        "wqkv0": halves(w["L0_attn_w_attn"], w["L0_attn_b_attn"]),
        "wproj0": halves(w["L0_attn_w_proj"], w["L0_attn_b_proj"]),
        "wqkv1": halves(w["L0_ffn_qkv_w"], w["L0_ffn_qkv_b"]),
        "wproj1": halves(w["L0_ffn_proj_w"], w["L0_ffn_proj_b"]),
        "w_gate": halves(w["L0_ffn_gate_w"]),
        "w1": np.stack([halves(np.asarray(w["L0_ffn_w1"])[e], np.asarray(w["L0_ffn_b1"])[e]) for e in range(E)]),
        "w2": np.stack([chunks(np.asarray(w["L0_ffn_w2"])[e]) for e in range(E)]),
        "b2": np.asarray(w["L0_ffn_b2"]),
    }
```
